# Optimizing a Trainium2 kernel written in Bass

```python
import numpy as np
import jax
import jax.numpy as jnp

def _softmax(x, axis=-1):
    return jax.nn.softmax(x, axis=axis)

def _gelu(x):
    return jax.nn.gelu(x, approximate=True)

def _silu(x):
    return jax.nn.silu(x)

def _sigmoid(x):
    return jax.nn.sigmoid(x)

def _layernorm(x, axis=-1, eps=1e-05):
    m = jnp.mean(x, axis=axis, keepdims=True)
    v = jnp.var(x, axis=axis, keepdims=True)
    return (x - m) / jnp.sqrt(v + eps)

def _scatter_add(tgt, idx, src, axis=0):
    return tgt.at[idx].add(src)

def _segment_sum(src, seg, n):
    return jax.ops.segment_sum(src, seg, n)
kernel_name = 'mk_perceiver_d4_seqx_r4_54b6b7'

def setup_inputs(seed: int=0):
    np.random.seed(seed)
    _w = jnp.asarray

    def _rec_inputs():
        import jax
        import jax.numpy as jnp
        _rk = jax.random.key(seed)
        x = -9.806e-05 + 1 * jax.random.normal(jax.random.fold_in(_rk, 1), (1, 128, 256), jnp.float32)
        _lenS = 128 - jax.random.randint(jax.random.fold_in(_rk, 7), (1,), 0, max(1, 128 // 4) + 1, jnp.int32)
        _lenS2 = 12544 - jax.random.randint(jax.random.fold_in(_rk, 8), (1,), 0, max(1, 12544 // 4) + 1, jnp.int32)
        _ctx_1024P = jax.random.normal(jax.random.fold_in(_rk, 11), (1, 16, 256), jnp.float32)
        _ctx_1024c = jax.random.dirichlet(jax.random.fold_in(_rk, 511), 0.3 * jnp.ones((16,), jnp.float32), (1, 12544))
        _ctx_1024t = jnp.einsum('bsk,bkd->bsd', _ctx_1024c, _ctx_1024P)
        _ctx_1024t = _ctx_1024t * jax.lax.rsqrt(jnp.mean(jnp.square(_ctx_1024t)) + 1e-12) * 0.953939
        ctx_1024 = -1.52775e-05 + 0.999936 * (_ctx_1024t + 0.3 * jax.random.normal(jax.random.fold_in(_rk, 611), (1, 12544, 256), jnp.float32))
        _validS = jnp.arange(128)[None, :] < _lenS[:, None]
        _validS2 = jnp.arange(12544)[None, :] < _lenS2[:, None]
        _causal = jnp.tril(jnp.ones((128, 128), dtype=bool))
        mask_1x1xSxS2_if1 = jnp.where(jnp.ones((1, 1, 128, 12544), dtype=bool), 1, 0).astype(jnp.int32)
        return (x, ctx_1024, _lenS2, mask_1x1xSxS2_if1)
    x, ctx_1024, _lenS2, mask_1x1xSxS2_if1 = _rec_inputs()

    def _L0_xattn_setup():
        import jax, jax.numpy as jnp
        import numpy as np
        EPS = 1e-06
        NUM_ITERS = 3

        def rmsnorm(x, w, eps=EPS):
            return x * jax.lax.rsqrt(jnp.mean(x * x, axis=-1, keepdims=True) + eps) * w

        def gru_cell(x, h, wi, wh, bi, bh):
            d = h.shape[-1]
            gi = jnp.einsum('...d,ed->...e', x, wi) + bi
            gh = jnp.einsum('...d,ed->...e', h, wh) + bh
            ir, iz, inn = (gi[..., :d], gi[..., d:2 * d], gi[..., 2 * d:])
            hr, hz, hn = (gh[..., :d], gh[..., d:2 * d], gh[..., 2 * d:])
            r = jax.nn.sigmoid(ir + hr)
            z = jax.nn.sigmoid(iz + hz)
            n = jnp.tanh(inn + r * hn)
            return (1.0 - z) * n + z * h
        key = jax.random.key(seed)
        ks = jax.random.split(key, 12)
        B, K, M, d = (8, 64, 1024, 256)
        s = 0.02
        return {'slots': jax.random.normal(ks[0], (B, K, d), jnp.float32), 'P': jax.random.normal(ks[1], (B, M, d), jnp.float32), 'Wq': jax.random.normal(ks[2], (d, d), jnp.float32) * s, 'Wk': jax.random.normal(ks[3], (d, d), jnp.float32) * s, 'Wv': jax.random.normal(ks[4], (d, d), jnp.float32) * s, 'gru_wi': jax.random.normal(ks[5], (3 * d, d), jnp.float32) * s, 'gru_wh': jax.random.normal(ks[6], (3 * d, d), jnp.float32) * s, 'gru_bi': jax.random.normal(ks[7], (3 * d,), jnp.float32) * s, 'gru_bh': jax.random.normal(ks[8], (3 * d,), jnp.float32) * s, 'slot_norm_w': jnp.ones((d,), jnp.float32), 'input_norm_w': jnp.ones((d,), jnp.float32)}
    _L0_xattn_all = _L0_xattn_setup()
    _L0_xattn_in = {k: v for k, v in _L0_xattn_all.items() if k in ('Wq', 'Wk', 'Wv', 'gru_wi', 'gru_wh', 'gru_bi', 'gru_bh', 'slot_norm_w', 'input_norm_w')}
    del _L0_xattn_all

    def _L0_attn_setup():
        import jax, jax.numpy as jnp
        import numpy as np
        EMB = 256
        HEADS = 16
        EPS = 1e-05

        def layer_norm(x):
            mu = jnp.mean(x, axis=-1, keepdims=True)
            var = jnp.var(x, axis=-1, keepdims=True)
            return (x - mu) / jnp.sqrt(var + EPS)

        def pattention(x, K, V):
            scale = EMB ** (-0.5)
            a = jax.nn.softmax(scale * jnp.einsum('btc,nc->btn', x, K), axis=-1)
            return jnp.einsum('btn,nc->btc', a, V)

        def causal_sdpa(q, k, v):
            T = q.shape[2]
            d = q.shape[-1]
            scores = jnp.einsum('bhqd,bhkd->bhqk', q, k) / jnp.sqrt(jnp.asarray(d, q.dtype))
            mask = jnp.tril(jnp.ones((T, T), dtype=bool))
            scores = jnp.where(mask, scores, jnp.asarray(-jnp.inf, q.dtype))
            attn = jax.nn.softmax(scores, axis=-1)
            return jnp.einsum('bhqk,bhkd->bhqd', attn, v)
        key = jax.random.key(seed)
        ks = jax.random.split(key, 11)
        B, T, C = (2, 512, EMB)
        N = 512 // 2
        inp = {'x': jax.random.normal(ks[0], (B, T, C), dtype=jnp.float32)}
        names = ['qK', 'qV', 'kK', 'kV', 'vK', 'vV', 'pK', 'pV']
        for i, nm in enumerate(names):
            inp[nm] = jax.random.normal(ks[1 + i], (N, C), dtype=jnp.float32)
        inp['fK'] = jax.random.normal(ks[9], (4 * N, C), dtype=jnp.float32)
        inp['fV'] = jax.random.normal(ks[10], (4 * N, C), dtype=jnp.float32)
        return inp
    _L0_attn_all = _L0_attn_setup()
    _L0_attn_in = {k: v for k, v in _L0_attn_all.items() if k in ('qK', 'qV', 'kK', 'kV', 'vK', 'vV', 'pK', 'pV', 'fK', 'fV')}
    del _L0_attn_all

    def _L0_ffn_setup():
        import jax, jax.numpy as jnp
        import numpy as np
        BLOCK = 32
        W_BITS = 4
        ACT_BITS = 16

        def act_qdq(x):
            qmax = 2.0 ** (ACT_BITS - 1) - 1.0
            scale = jnp.maximum(jnp.max(jnp.abs(x)) / qmax, 1e-12)
            return jnp.clip(jnp.round(x / scale), -qmax - 1.0, qmax) * scale

        def fixed_qdq_u16(x):
            scale = 1.0 / 65536.0
            return jnp.clip(jnp.round(x / scale), 0.0, 65535.0) * scale

        def lpbq_dequant(w):
            O, I = w.shape
            qmax = 2.0 ** (W_BITS - 1) - 1.0
            wb = w.reshape(O, I // BLOCK, BLOCK)
            s = jnp.maximum(jnp.max(jnp.abs(wb), axis=-1, keepdims=True) / qmax, 1e-12)
            wq = jnp.clip(jnp.round(wb / s), -qmax - 1.0, qmax) * s
            return wq.reshape(O, I)
        key = jax.random.key(seed)
        k1, k2, k3, k4 = jax.random.split(key, 4)
        B, S, H, I = (2, 1024, 256, 768)
        x = jax.random.normal(k1, (B, S, H), jnp.float32)
        w_gate = jax.random.normal(k2, (I, H), jnp.float32) * 0.02
        w_up = jax.random.normal(k3, (I, H), jnp.float32) * 0.02
        w_down = jax.random.normal(k4, (H, I), jnp.float32) * 0.02
        return {'x': x, 'w_gate': w_gate, 'w_up': w_up, 'w_down': w_down}
    _L0_ffn_all = _L0_ffn_setup()
    _L0_ffn_in = {k: v for k, v in _L0_ffn_all.items() if k in ('w_gate', 'w_up', 'w_down')}
    del _L0_ffn_all

    def _L1_xattn_setup():
        import jax, jax.numpy as jnp
        import numpy as np
        NEG = -10000000000000.0
        key = jax.random.key(seed)
        ks = jax.random.split(key, 7)
        B, L, D, E = (8, 512, 256, 256)
        Q = jax.random.normal(ks[0], (B, L, D), dtype=jnp.float32)
        K = jax.random.normal(ks[1], (B, L, D), dtype=jnp.float32)
        V = jax.random.normal(ks[2], (B, L, D), dtype=jnp.float32)
        query_pad_idxs = jax.random.randint(ks[3], (B,), 0, L)
        key_pad_idxs = jax.random.randint(ks[4], (B,), 0, L)
        W = jax.random.normal(ks[5], (E, D), dtype=jnp.float32) / np.sqrt(D)
        b = jax.random.normal(ks[6], (E,), dtype=jnp.float32) * 0.01
        return {'Q': Q, 'K': K, 'V': V, 'query_pad_idxs': query_pad_idxs, 'key_pad_idxs': key_pad_idxs, 'W': W, 'b': b}
    _L1_xattn_all = _L1_xattn_setup()
    _L1_xattn_in = {k: v for k, v in _L1_xattn_all.items() if k in ('W', 'b')}
    del _L1_xattn_all

    def _L1_attn_setup():
        import math
        import jax, jax.numpy as jnp
        import numpy as np
        HEADS = 16
        key = jax.random.key(seed)
        k1, k2, k3, k4, k5 = jax.random.split(key, 5)
        B, S, D = (2, 512, 256)
        return {'x': jax.random.normal(k1, (B, S, D), dtype=jnp.float32), 'Wqkv': jax.random.normal(k2, (3 * D, D), dtype=jnp.float32) * (1.0 / math.sqrt(D)), 'bqkv': jax.random.normal(k3, (3 * D,), dtype=jnp.float32) * 0.02, 'Wo': jax.random.normal(k4, (D, D), dtype=jnp.float32) * (1.0 / math.sqrt(D)), 'bo': jax.random.normal(k5, (D,), dtype=jnp.float32) * 0.02}
    _L1_attn_all = _L1_attn_setup()
    _L1_attn_in = {k: v for k, v in _L1_attn_all.items() if k in ('Wqkv', 'bqkv', 'Wo', 'bo')}
    del _L1_attn_all

    def _L1_ffn_setup():
        import jax, jax.numpy as jnp
        import numpy as np
        key = jax.random.key(seed)
        k1, k2, k3, k4 = jax.random.split(key, 4)
        B, T, M = (4, 512, 256)
        E, F = (16, 1024)
        x = jax.random.normal(k1, (B, T, M), dtype=jnp.float32) * 0.02
        Wg = jax.random.normal(k2, (M, E), dtype=jnp.float32) * 0.02
        w1 = jax.random.normal(k3, (E, M, F), dtype=jnp.float32) * 0.02
        w2 = jax.random.normal(k4, (E, F, M), dtype=jnp.float32) * 0.02
        return {'x': x, 'Wg': Wg, 'w1': w1, 'w2': w2}
    _L1_ffn_all = _L1_ffn_setup()
    _L1_ffn_in = {k: v for k, v in _L1_ffn_all.items() if k in ('Wg', 'w1', 'w2')}
    del _L1_ffn_all

    def _L2_xattn_setup():
        import jax, jax.numpy as jnp
        import numpy as np
        D_MODEL = 256
        HEAD = 16
        D_K = D_MODEL // HEAD
        NEG = -1000000000.0
        key = jax.random.key(seed)
        ks = jax.random.split(key, 8)
        B, S = (2, 512)
        q = jax.random.normal(ks[0], (B, S, D_MODEL), dtype=jnp.float32)
        k = jax.random.normal(ks[1], (B, S, D_MODEL), dtype=jnp.float32)
        v = jax.random.normal(ks[2], (B, S, D_MODEL), dtype=jnp.float32)
        mask = jnp.ones((1, 1, S, S), dtype=jnp.int32)
        scale = 1.0 / np.sqrt(D_MODEL)
        w_q = jax.random.normal(ks[3], (D_MODEL, D_MODEL), dtype=jnp.float32) * scale
        w_k = jax.random.normal(ks[4], (D_MODEL, D_MODEL), dtype=jnp.float32) * scale
        w_v = jax.random.normal(ks[5], (D_MODEL, D_MODEL), dtype=jnp.float32) * scale
        w_o = jax.random.normal(ks[6], (D_MODEL, D_MODEL), dtype=jnp.float32) * scale
        return {'q': q, 'k': k, 'v': v, 'mask': mask, 'w_q': w_q, 'w_k': w_k, 'w_v': w_v, 'w_o': w_o}
    _L2_xattn_all = _L2_xattn_setup()
    _L2_xattn_in = {k: v for k, v in _L2_xattn_all.items() if k in ('w_q', 'w_k', 'w_v', 'w_o')}
    del _L2_xattn_all

    def _L2_attn_setup():
        import jax, jax.numpy as jnp
        import numpy as np
        B, L, D, H = (2, 1024, 256, 4)
        DK = D // H
        DV = D // H
        CONV_K = 4
        FIR_S, FIR_L = (5, 64)
        GATE_HID = D * 2 // 2
        CHUNK = 32
        FLOOR_EPS = 0.08
        GATE_BIAS = np.array([-0.5, -0.5, 1.0, 3.0], np.float32)
        GATE_LOGIT_INIT = float(np.log(np.expm1(0.7)))
        CONV_RES_INIT = float(np.log(0.1 / 0.9))

        def _l2norm(x):
            return x / jnp.sqrt(jnp.sum(x * x, -1, keepdims=True) + 1e-12)

        def _causal_dwconv(x, w):
            k = w.shape[-1]
            xp = jnp.pad(x, ((0, 0), (k - 1, 0), (0, 0))).transpose(0, 2, 1)
            y = jax.lax.conv_general_dilated(xp, w[:, None, :], (1,), 'VALID', feature_group_count=w.shape[0], dimension_numbers=('NCH', 'OIH', 'NCH'))
            return y.transpose(0, 2, 1)

        def _delta_chunkwise(q, k, v, beta):
            b, h, Lq, dk = q.shape
            dv = v.shape[-1]
            c = CHUNK
            n = Lq // c
            q = _l2norm(q)
            k = _l2norm(k)
            v = v * beta[..., None]
            kb = k * beta[..., None]
            rs = lambda t: t.reshape(b, h, n, c, t.shape[-1])
            q, k, v, kb = map(rs, (q, k, v, kb))
            tri_lo_strict = jnp.tril(jnp.ones((c, c), bool), -1)
            tri_lo = jnp.tril(jnp.ones((c, c), bool), 0)
            A = jnp.where(tri_lo_strict, kb @ jnp.swapaxes(k, -1, -2), 0.0)
            eye = jnp.eye(c, dtype=q.dtype)
            inv = jax.scipy.linalg.solve_triangular(eye + A, jnp.broadcast_to(eye, A.shape), lower=True, unit_diagonal=True)
            u = inv @ v
            w = inv @ kb

            def step(S, xs):
                qi, ki, ui, wi = xs
                attn = jnp.where(tri_lo, qi @ jnp.swapaxes(ki, -1, -2), 0.0)
                u_i = ui - wi @ S
                o = qi @ S + attn @ u_i
                return (S + jnp.swapaxes(ki, -1, -2) @ u_i, o)
            mv = lambda t: jnp.moveaxis(t, 2, 0)
            S0 = jnp.zeros((b, h, dk, dv), q.dtype)
            _, out = jax.lax.scan(step, S0, (mv(q), mv(k), mv(u), mv(w)))
            return jnp.moveaxis(out, 0, 2).reshape(b, h, Lq, dv)

        def _stats(x):
            mean = jnp.mean(x, -1, keepdims=True)
            var = jnp.var(x, -1, keepdims=True)
            am = jnp.mean(jnp.abs(x), -1, keepdims=True)
            l2 = jnp.linalg.norm(x, axis=-1, keepdims=True)
            return jnp.concatenate([mean, var, am, l2], -1)
        key = jax.random.key(seed)
        ks = jax.random.split(key, 20)
        rn = lambda i, shape, sc: jax.random.normal(ks[i], shape, jnp.float32) * sc
        fir_s = jnp.zeros((H, DV, FIR_S), jnp.float32).at[..., 0].set(1.0) + rn(8, (H, DV, FIR_S), 0.02)
        fir_l = jnp.zeros((H, DV, FIR_L), jnp.float32).at[..., 0].set(1.0) + rn(9, (H, DV, FIR_L), 0.02)
        return {'hidden_states': rn(0, (B, L, D), 1.0), 'Wq': rn(1, (D, D), 0.02), 'Wk': rn(2, (D, D), 0.02), 'Wv': rn(3, (D, D), 0.02), 'Wb': rn(4, (D, H), 0.02), 'conv_w_q': rn(5, (D, CONV_K), 0.3), 'conv_w_k': rn(6, (D, CONV_K), 0.3), 'conv_w_v': rn(7, (D, CONV_K), 0.3), 'fir_short_w': fir_s, 'fir_long_w': fir_l, 'mlp_w1': rn(10, (D + 16, GATE_HID), 0.02), 'mlp_b1': jnp.zeros((GATE_HID,), jnp.float32), 'mlp_w2': rn(11, (GATE_HID, 4), 0.02), 'mlp_b2': jnp.asarray(GATE_BIAS), 'logit_temp': jnp.full((1,), GATE_LOGIT_INIT, jnp.float32), 'conv_res_logit': jnp.full((H,), CONV_RES_INIT, jnp.float32), 'rms_w': jnp.ones((DV,), jnp.float32), 'Wo': rn(12, (D, D), 0.02)}
    _L2_attn_all = _L2_attn_setup()
    _L2_attn_in = {k: v for k, v in _L2_attn_all.items() if k in ('Wq', 'Wk', 'Wv', 'Wb', 'conv_w_q', 'conv_w_k', 'conv_w_v', 'fir_short_w', 'fir_long_w', 'mlp_w1', 'mlp_b1', 'mlp_w2', 'mlp_b2', 'logit_temp', 'conv_res_logit', 'rms_w', 'Wo')}
    del _L2_attn_all

    def _L2_ffn_setup():
        import jax, jax.numpy as jnp
        import numpy as np
        DIM = 256
        DEPTH = 2
        HEADS = 8
        DIM_HEAD = 64
        WINDOW = 128
        INNER = HEADS * DIM_HEAD
        HID = int(DIM * 4 * 2 / 3)
        B, N = (2, 2048)
        QK_SCALE = 8.0

        def shift_token(t):
            t1, t2 = jnp.split(t, 2, axis=-1)
            t2 = jnp.pad(t2, ((0, 0), (1, 0), (0, 0)))[:, :-1]
            return jnp.concatenate([t1, t2], axis=-1)

        def l2norm(t):
            return t / jnp.clip(jnp.linalg.norm(t, axis=-1, keepdims=True), 1e-12)

        def rotate_half(x):
            x1, x2 = jnp.split(x, 2, axis=-1)
            return jnp.concatenate([-x2, x1], axis=-1)

        def rotary_xpos(q, k):
            n = q.shape[-2]
            half_idx = jnp.arange(0, DIM_HEAD, 2, dtype=jnp.float32)
            inv_freq = 1.0 / 10000.0 ** (half_idx / DIM_HEAD)
            t = jnp.arange(n, dtype=jnp.float32)
            freqs = t[:, None] * inv_freq[None, :]
            freqs = jnp.concatenate([freqs, freqs], axis=-1)
            base = (half_idx + 0.4 * DIM_HEAD) / (1.4 * DIM_HEAD)
            power = (t - n // 2) / float(WINDOW // 2)
            scale = base[None, :] ** power[:, None]
            scale = jnp.concatenate([scale, scale], axis=-1)
            cos, sin = (jnp.cos(freqs), jnp.sin(freqs))
            q = q * cos * scale + rotate_half(q) * sin * scale
            k = k * cos / scale + rotate_half(k) * sin / scale
            return (q, k)

        def local_attention(q, k, v):
            b, h, n, d = q.shape
            w = n // WINDOW
            bq = q.reshape(b, h, w, WINDOW, d) * QK_SCALE
            bk = k.reshape(b, h, w, WINDOW, d)
            bv = v.reshape(b, h, w, WINDOW, d)

            def look_around(t):
                p = jnp.pad(t, ((0, 0), (0, 0), (1, 0), (0, 0), (0, 0)))
                return jnp.concatenate([p[:, :, :w], p[:, :, 1:]], axis=3)
            bk, bv = (look_around(bk), look_around(bv))
            bt = jnp.arange(n).reshape(w, WINDOW)
            btp = jnp.pad(bt, ((1, 0), (0, 0)), constant_values=-1)
            btk = jnp.concatenate([btp[:w], btp[1:]], axis=1)
            sim = jnp.einsum('bhwid,bhwjd->bhwij', bq, bk)
            i = bt[:, :, None]
            j = btk[:, None, :]
            mask = (i < j) | (i > j + WINDOW) | (j == -1)
            sim = jnp.where(mask, -jnp.finfo(sim.dtype).max, sim)
            attn = jax.nn.softmax(sim, axis=-1)
            out = jnp.einsum('bhwij,bhwjd->bhwid', attn, bv)
            return out.reshape(b, h, n, d)

        def _layer(x, wqkv, qs, ksc, wo, lg, lb, w1, b1, w2, b2):
            b, n, _ = x.shape
            h = shift_token(x)
            qkv = h @ wqkv
            q, k, v = jnp.split(qkv, 3, axis=-1)
            to_heads = lambda t: t.reshape(b, n, HEADS, DIM_HEAD).transpose(0, 2, 1, 3)
            q, k, v = (to_heads(q), to_heads(k), to_heads(v))
            q = l2norm(q) * qs
            k = l2norm(k) * ksc
            q, k = rotary_xpos(q, k)
            o = local_attention(q, k, v)
            o = o.transpose(0, 2, 1, 3).reshape(b, n, INNER)
            x = x + o @ wo
            h = shift_token(x)
            mu = h.mean(-1, keepdims=True)
            var = h.var(-1, keepdims=True)
            h = (h - mu) / jnp.sqrt(var + 1e-05) * lg + lb
            h = h @ w1 + b1
            a, g = jnp.split(h, 2, axis=-1)
            h = a * jax.nn.gelu(g, approximate=False)
            x = x + h @ w2 + b2
            return x
        key = jax.random.key(seed)
        ks = jax.random.split(key, 6)
        return {'x': jax.random.normal(ks[0], (B, N, DIM), jnp.float32), 'wqkv': jax.random.normal(ks[1], (DEPTH, DIM, 3 * INNER), jnp.float32) * 0.02, 'q_scale': jnp.ones((DEPTH, DIM_HEAD), jnp.float32), 'k_scale': jnp.ones((DEPTH, DIM_HEAD), jnp.float32), 'wo': jax.random.normal(ks[2], (DEPTH, INNER, DIM), jnp.float32) * 0.02, 'ln_g': jnp.ones((DEPTH, DIM), jnp.float32), 'ln_b': jnp.zeros((DEPTH, DIM), jnp.float32), 'w1': jax.random.normal(ks[3], (DEPTH, DIM, 2 * HID), jnp.float32) * 0.02, 'b1': jnp.zeros((DEPTH, 2 * HID), jnp.float32), 'w2': jax.random.normal(ks[4], (DEPTH, HID, DIM), jnp.float32) * 0.02, 'b2': jnp.zeros((DEPTH, DIM), jnp.float32)}
    _L2_ffn_all = _L2_ffn_setup()
    _L2_ffn_in = {k: v for k, v in _L2_ffn_all.items() if k in ('wqkv', 'q_scale', 'k_scale', 'wo', 'ln_g', 'ln_b', 'w1', 'b1', 'w2', 'b2')}
    del _L2_ffn_all

    def _L3_xattn_setup():
        import jax, jax.numpy as jnp
        import numpy as np
        key = jax.random.key(seed)
        k1, k2 = jax.random.split(key)
        B, Tq, Tk, D = (8, 512, 512, 256)
        query = jax.random.normal(k1, (B, Tq, D), dtype=jnp.float32)
        key_t = jax.random.normal(k2, (B, Tk, D), dtype=jnp.float32)
        return {'query': query, 'key': key_t}
    _L3_xattn_all = _L3_xattn_setup()
    _L3_xattn_in = {k: v for k, v in _L3_xattn_all.items() if k in ()}
    del _L3_xattn_all

    def _L3_attn_setup():
        import jax, jax.numpy as jnp
        import numpy as np
        import math
        NUM_HEADS = 8
        EMB = 256
        HEAD_DIM = 128
        B, T = (1, 1024)

        def sinusoidal_pe(T, d, dtype=jnp.float32):
            pos = jnp.arange(T, dtype=dtype)[:, None]
            inv_freq = jnp.exp(-math.log(10000.0) * jnp.arange(0, d, 2, dtype=dtype) / d)
            ang = pos * inv_freq[None, :]
            pe = jnp.zeros((T, d), dtype=dtype)
            pe = pe.at[:, 0::2].set(jnp.sin(ang))
            pe = pe.at[:, 1::2].set(jnp.cos(ang))
            return pe
        key = jax.random.key(seed)
        ks = jax.random.split(key, 6)
        s = lambda fan_in: 1.0 / math.sqrt(fan_in)
        x = jax.random.normal(ks[0], (B, T, EMB), dtype=jnp.float32)
        Wq = jax.random.normal(ks[1], (EMB, NUM_HEADS * HEAD_DIM), dtype=jnp.float32) * s(EMB)
        bq = jax.random.normal(ks[2], (NUM_HEADS * HEAD_DIM,), dtype=jnp.float32) * s(EMB)
        Wkv = jax.random.normal(ks[3], (EMB, 2 * HEAD_DIM), dtype=jnp.float32) * s(EMB)
        bkv = jax.random.normal(ks[4], (2 * HEAD_DIM,), dtype=jnp.float32) * s(EMB)
        Wo = jax.random.normal(ks[5], (NUM_HEADS * HEAD_DIM, EMB), dtype=jnp.float32) * s(NUM_HEADS * HEAD_DIM)
        return {'x': x, 'Wq': Wq, 'bq': bq, 'Wkv': Wkv, 'bkv': bkv, 'Wo': Wo}
    _L3_attn_all = _L3_attn_setup()
    _L3_attn_in = {k: v for k, v in _L3_attn_all.items() if k in ('Wq', 'bq', 'Wkv', 'bkv', 'Wo')}
    del _L3_attn_all

    def _L3_ffn_setup():
        import jax, jax.numpy as jnp
        import numpy as np
        E = 8
        TOPK = 2
        PRIME = 11
        HASH_OFF = 7919
        N_SHARED = 1
        key = jax.random.key(seed)
        ks = jax.random.split(key, 8)
        B, T, C, Hs, Hr = (4, 2048, 256, 512, 256)
        sc = lambda k, shape, fan: jax.random.normal(k, shape, jnp.float32) * fan ** (-0.5)
        return {'x': jax.random.normal(ks[0], (B, T, C), jnp.float32), 't_emb': jax.random.normal(ks[1], (B, C), jnp.float32), 'sw1': sc(ks[2], (C, Hs), C), 'sb1': jnp.zeros((Hs,), jnp.float32), 'sw3': sc(ks[3], (C, Hs), C), 'sb3': jnp.zeros((Hs,), jnp.float32), 'sw2': sc(ks[4], (Hs, C), Hs), 'sb2': jnp.zeros((C,), jnp.float32), 'w1': sc(ks[5], (E, C, Hr), C), 'b1': jnp.zeros((E, Hr), jnp.float32), 'w2': sc(ks[6], (E, Hr, C), Hr), 'b2': jnp.zeros((E, C), jnp.float32)}
    _L3_ffn_all = _L3_ffn_setup()
    _L3_ffn_in = {k: v for k, v in _L3_ffn_all.items() if k in ('t_emb', 'sw1', 'sb1', 'sw3', 'sb3', 'sw2', 'sb2', 'w1', 'b1', 'w2', 'b2')}
    del _L3_ffn_all
    return {'x': x, 'ctx_1024': ctx_1024, '_lenS2': _lenS2, 'mask_1x1xSxS2_if1': mask_1x1xSxS2_if1, 'L0_xattn_Wq': _L0_xattn_in['Wq'], 'L0_xattn_Wk': _L0_xattn_in['Wk'], 'L0_xattn_Wv': _L0_xattn_in['Wv'], 'L0_xattn_gru_wi': _L0_xattn_in['gru_wi'], 'L0_xattn_gru_wh': _L0_xattn_in['gru_wh'], 'L0_xattn_gru_bi': _L0_xattn_in['gru_bi'], 'L0_xattn_gru_bh': _L0_xattn_in['gru_bh'], 'L0_xattn_slot_norm_w': _L0_xattn_in['slot_norm_w'], 'L0_xattn_input_norm_w': _L0_xattn_in['input_norm_w'], 'L0_attn_qK': _L0_attn_in['qK'], 'L0_attn_qV': _L0_attn_in['qV'], 'L0_attn_kK': _L0_attn_in['kK'], 'L0_attn_kV': _L0_attn_in['kV'], 'L0_attn_vK': _L0_attn_in['vK'], 'L0_attn_vV': _L0_attn_in['vV'], 'L0_attn_pK': _L0_attn_in['pK'], 'L0_attn_pV': _L0_attn_in['pV'], 'L0_attn_fK': _L0_attn_in['fK'], 'L0_attn_fV': _L0_attn_in['fV'], 'L0_ffn_w_gate': _L0_ffn_in['w_gate'], 'L0_ffn_w_up': _L0_ffn_in['w_up'], 'L0_ffn_w_down': _L0_ffn_in['w_down'], 'L1_xattn_W': _L1_xattn_in['W'], 'L1_xattn_b': _L1_xattn_in['b'], 'L1_attn_Wqkv': _L1_attn_in['Wqkv'], 'L1_attn_bqkv': _L1_attn_in['bqkv'], 'L1_attn_Wo': _L1_attn_in['Wo'], 'L1_attn_bo': _L1_attn_in['bo'], 'L1_ffn_Wg': _L1_ffn_in['Wg'], 'L1_ffn_w1': _L1_ffn_in['w1'], 'L1_ffn_w2': _L1_ffn_in['w2'], 'L2_xattn_w_q': _L2_xattn_in['w_q'], 'L2_xattn_w_k': _L2_xattn_in['w_k'], 'L2_xattn_w_v': _L2_xattn_in['w_v'], 'L2_xattn_w_o': _L2_xattn_in['w_o'], 'L2_attn_Wq': _L2_attn_in['Wq'], 'L2_attn_Wk': _L2_attn_in['Wk'], 'L2_attn_Wv': _L2_attn_in['Wv'], 'L2_attn_Wb': _L2_attn_in['Wb'], 'L2_attn_conv_w_q': _L2_attn_in['conv_w_q'], 'L2_attn_conv_w_k': _L2_attn_in['conv_w_k'], 'L2_attn_conv_w_v': _L2_attn_in['conv_w_v'], 'L2_attn_fir_short_w': _L2_attn_in['fir_short_w'], 'L2_attn_fir_long_w': _L2_attn_in['fir_long_w'], 'L2_attn_mlp_w1': _L2_attn_in['mlp_w1'], 'L2_attn_mlp_b1': _L2_attn_in['mlp_b1'], 'L2_attn_mlp_w2': _L2_attn_in['mlp_w2'], 'L2_attn_mlp_b2': _L2_attn_in['mlp_b2'], 'L2_attn_logit_temp': _L2_attn_in['logit_temp'], 'L2_attn_conv_res_logit': _L2_attn_in['conv_res_logit'], 'L2_attn_rms_w': _L2_attn_in['rms_w'], 'L2_attn_Wo': _L2_attn_in['Wo'], 'L2_ffn_wqkv': _L2_ffn_in['wqkv'], 'L2_ffn_q_scale': _L2_ffn_in['q_scale'], 'L2_ffn_k_scale': _L2_ffn_in['k_scale'], 'L2_ffn_wo': _L2_ffn_in['wo'], 'L2_ffn_ln_g': _L2_ffn_in['ln_g'], 'L2_ffn_ln_b': _L2_ffn_in['ln_b'], 'L2_ffn_w1': _L2_ffn_in['w1'], 'L2_ffn_b1': _L2_ffn_in['b1'], 'L2_ffn_w2': _L2_ffn_in['w2'], 'L2_ffn_b2': _L2_ffn_in['b2'], 'L3_attn_Wq': _L3_attn_in['Wq'], 'L3_attn_bq': _L3_attn_in['bq'], 'L3_attn_Wkv': _L3_attn_in['Wkv'], 'L3_attn_bkv': _L3_attn_in['bkv'], 'L3_attn_Wo': _L3_attn_in['Wo'], 'L3_ffn_t_emb': _L3_ffn_in['t_emb'], 'L3_ffn_sw1': _L3_ffn_in['sw1'], 'L3_ffn_sb1': _L3_ffn_in['sb1'], 'L3_ffn_sw3': _L3_ffn_in['sw3'], 'L3_ffn_sb3': _L3_ffn_in['sb3'], 'L3_ffn_sw2': _L3_ffn_in['sw2'], 'L3_ffn_sb2': _L3_ffn_in['sb2'], 'L3_ffn_w1': _L3_ffn_in['w1'], 'L3_ffn_b1': _L3_ffn_in['b1'], 'L3_ffn_w2': _L3_ffn_in['w2'], 'L3_ffn_b2': _L3_ffn_in['b2']}

def reference(x, ctx_1024, _lenS2, mask_1x1xSxS2_if1, L0_xattn_Wq, L0_xattn_Wk, L0_xattn_Wv, L0_xattn_gru_wi, L0_xattn_gru_wh, L0_xattn_gru_bi, L0_xattn_gru_bh, L0_xattn_slot_norm_w, L0_xattn_input_norm_w, L0_attn_qK, L0_attn_qV, L0_attn_kK, L0_attn_kV, L0_attn_vK, L0_attn_vV, L0_attn_pK, L0_attn_pV, L0_attn_fK, L0_attn_fV, L0_ffn_w_gate, L0_ffn_w_up, L0_ffn_w_down, L1_xattn_W, L1_xattn_b, L1_attn_Wqkv, L1_attn_bqkv, L1_attn_Wo, L1_attn_bo, L1_ffn_Wg, L1_ffn_w1, L1_ffn_w2, L2_xattn_w_q, L2_xattn_w_k, L2_xattn_w_v, L2_xattn_w_o, L2_attn_Wq, L2_attn_Wk, L2_attn_Wv, L2_attn_Wb, L2_attn_conv_w_q, L2_attn_conv_w_k, L2_attn_conv_w_v, L2_attn_fir_short_w, L2_attn_fir_long_w, L2_attn_mlp_w1, L2_attn_mlp_b1, L2_attn_mlp_w2, L2_attn_mlp_b2, L2_attn_logit_temp, L2_attn_conv_res_logit, L2_attn_rms_w, L2_attn_Wo, L2_ffn_wqkv, L2_ffn_q_scale, L2_ffn_k_scale, L2_ffn_wo, L2_ffn_ln_g, L2_ffn_ln_b, L2_ffn_w1, L2_ffn_b1, L2_ffn_w2, L2_ffn_b2, L3_attn_Wq, L3_attn_bq, L3_attn_Wkv, L3_attn_bkv, L3_attn_Wo, L3_ffn_t_emb, L3_ffn_sw1, L3_ffn_sb1, L3_ffn_sw3, L3_ffn_sb3, L3_ffn_sw2, L3_ffn_sb2, L3_ffn_w1, L3_ffn_b1, L3_ffn_w2, L3_ffn_b2):
    import jax
    import jax.numpy as jnp

    def _L0_xattn_ref(slots, P, Wq, Wk, Wv, gru_wi, gru_wh, gru_bi, gru_bh, slot_norm_w, input_norm_w):
        import jax, jax.numpy as jnp
        import numpy as np
        EPS = 1e-06
        NUM_ITERS = 3

        def rmsnorm(x, w, eps=EPS):
            return x * jax.lax.rsqrt(jnp.mean(x * x, axis=-1, keepdims=True) + eps) * w

        def gru_cell(x, h, wi, wh, bi, bh):
            d = h.shape[-1]
            gi = jnp.einsum('...d,ed->...e', x, wi) + bi
            gh = jnp.einsum('...d,ed->...e', h, wh) + bh
            ir, iz, inn = (gi[..., :d], gi[..., d:2 * d], gi[..., 2 * d:])
            hr, hz, hn = (gh[..., :d], gh[..., d:2 * d], gh[..., 2 * d:])
            r = jax.nn.sigmoid(ir + hr)
            z = jax.nn.sigmoid(iz + hz)
            n = jnp.tanh(inn + r * hn)
            return (1.0 - z) * n + z * h
        d = slots.shape[-1]
        scale = d ** (-0.5)
        Pn = rmsnorm(P, input_norm_w)
        k_proj = jnp.einsum('bmd,ed->bme', Pn, Wk)
        v_proj = jnp.einsum('bmd,ed->bme', Pn, Wv)
        for _ in range(NUM_ITERS):
            sn = rmsnorm(slots, slot_norm_w)
            q = jnp.einsum('bkd,ed->bke', sn, Wq)
            scores = jnp.einsum('bkd,bmd->bkm', q, k_proj) * scale
            attn = jax.nn.softmax(scores, axis=-2)
            attn = attn / (jnp.sum(attn, axis=-1, keepdims=True) + EPS)
            updates = jnp.einsum('bkm,bmd->bkd', attn, v_proj)
            slots = gru_cell(updates, slots, gru_wi, gru_wh, gru_bi, gru_bh)
        return slots

    def _L0_attn_ref(x, qK, qV, kK, kV, vK, vV, pK, pV, fK, fV):
        import jax, jax.numpy as jnp
        import numpy as np
        EMB = 256
        HEADS = 16
        EPS = 1e-05

        def layer_norm(x):
            mu = jnp.mean(x, axis=-1, keepdims=True)
            var = jnp.var(x, axis=-1, keepdims=True)
            return (x - mu) / jnp.sqrt(var + EPS)

        def pattention(x, K, V):
            scale = EMB ** (-0.5)
            a = jax.nn.softmax(scale * jnp.einsum('btc,nc->btn', x, K), axis=-1)
            return jnp.einsum('btn,nc->btc', a, V)

        def causal_sdpa(q, k, v):
            T = q.shape[2]
            d = q.shape[-1]
            scores = jnp.einsum('bhqd,bhkd->bhqk', q, k) / jnp.sqrt(jnp.asarray(d, q.dtype))
            mask = jnp.tril(jnp.ones((T, T), dtype=bool))
            scores = jnp.where(mask, scores, jnp.asarray(-jnp.inf, q.dtype))
            attn = jax.nn.softmax(scores, axis=-1)
            return jnp.einsum('bhqk,bhkd->bhqd', attn, v)
        B, T, C = x.shape
        H = HEADS
        D = C // H
        x_in = x
        h = layer_norm(x)
        k = pattention(h, kK, kV)
        q = pattention(h, qK, qV)
        v = pattention(h, vK, vV)
        to_heads = lambda t: t.reshape(B, T, H, D).transpose(0, 2, 1, 3)
        o = causal_sdpa(to_heads(q), to_heads(k), to_heads(v))
        o = o.transpose(0, 2, 1, 3).reshape(B, T, C)
        o = pattention(o, pK, pV)
        x = o + x_in
        x_inter = x
        x = pattention(layer_norm(x), fK, fV)
        return x + x_inter

    def _L0_ffn_ref(x, w_gate, w_up, w_down):
        import jax, jax.numpy as jnp
        import numpy as np
        BLOCK = 32
        W_BITS = 4
        ACT_BITS = 16

        def act_qdq(x):
            qmax = 2.0 ** (ACT_BITS - 1) - 1.0
            scale = jnp.maximum(jnp.max(jnp.abs(x)) / qmax, 1e-12)
            return jnp.clip(jnp.round(x / scale), -qmax - 1.0, qmax) * scale

        def fixed_qdq_u16(x):
            scale = 1.0 / 65536.0
            return jnp.clip(jnp.round(x / scale), 0.0, 65535.0) * scale

        def lpbq_dequant(w):
            O, I = w.shape
            qmax = 2.0 ** (W_BITS - 1) - 1.0
            wb = w.reshape(O, I // BLOCK, BLOCK)
            s = jnp.maximum(jnp.max(jnp.abs(wb), axis=-1, keepdims=True) / qmax, 1e-12)
            wq = jnp.clip(jnp.round(wb / s), -qmax - 1.0, qmax) * s
            return wq.reshape(O, I)
        x = act_qdq(x)
        up = act_qdq(x @ lpbq_dequant(w_up).T)
        gate = act_qdq(x @ lpbq_dequant(w_gate).T)
        sig = fixed_qdq_u16(jax.nn.sigmoid(gate))
        gate = act_qdq(gate * sig)
        o = act_qdq(gate * up)
        return o @ lpbq_dequant(w_down).T

    def _L1_xattn_ref(Q, K, V, query_pad_idxs, key_pad_idxs, W, b):
        import jax, jax.numpy as jnp
        import numpy as np
        NEG = -10000000000000.0
        B, Lq, D = Q.shape
        Lk = K.shape[1]
        scale = 1.0 / jnp.sqrt(jnp.asarray(D, dtype=Q.dtype))
        scores = jnp.einsum('bqd,bkd->bqk', Q, K) * scale
        qpos = jnp.arange(Lq)[None, :, None]
        kpos = jnp.arange(Lk)[None, None, :]
        mask = (qpos >= query_pad_idxs[:, None, None]) & (kpos >= key_pad_idxs[:, None, None])
        scores = jnp.where(mask, jnp.asarray(NEG, scores.dtype), scores)
        attn = jax.nn.softmax(scores, axis=2)
        out = jnp.einsum('bqk,bkd->bqd', attn, V)
        return out @ W.T + b

    def _L1_attn_ref(x, Wqkv, bqkv, Wo, bo):
        import math
        import jax, jax.numpy as jnp
        import numpy as np
        HEADS = 16
        B, S, D = x.shape
        H = HEADS
        hd = D // H
        qkv = x @ Wqkv.T + bqkv
        qkv = qkv.reshape(B, H, S, 3 * hd)
        q, k, v = jnp.split(qkv, 3, axis=-1)
        scores = jnp.einsum('bhsd,bhtd->bhst', q, k) * (1.0 / math.sqrt(hd))
        attn = jax.nn.softmax(scores, axis=-1)
        vals = jnp.einsum('bhst,bhtd->bhsd', attn, v)
        vals = vals.reshape(B, S, D)
        return vals @ Wo.T + bo

    def _L1_ffn_ref(x, Wg, w1, w2):
        import jax, jax.numpy as jnp
        import numpy as np
        d = x.shape[-1]
        xr = x.reshape(-1, d)
        S = xr.shape[0]
        E = Wg.shape[1]
        C = (S + E - 1) // E
        gate = jax.nn.softmax(xr @ Wg, axis=-1)
        idx = jnp.argmax(gate, axis=1)
        gates_s = jnp.take_along_axis(gate, idx[:, None], axis=1)[:, 0]
        onehot = jax.nn.one_hot(idx, E, dtype=jnp.int32)
        loc = jnp.sum((jnp.cumsum(onehot, axis=0) - 1) * onehot, axis=1)
        valid = loc < C
        loc_pad = jnp.minimum(loc, C)
        dispatched = jnp.zeros((E, C + 1, d), dtype=x.dtype).at[idx, loc_pad].set(xr)
        dispatched = dispatched[:, :C]
        h = jax.nn.relu(jnp.einsum('ecm,emf->ecf', dispatched, w1))
        expert_out = jnp.einsum('ecf,efm->ecm', h, w2)
        gathered = expert_out[idx, jnp.minimum(loc, C - 1)]
        combined = gathered * (gates_s * valid.astype(x.dtype))[:, None]
        return combined.reshape(x.shape)

    def _L2_xattn_ref(q, k, v, mask, w_q, w_k, w_v, w_o):
        import jax, jax.numpy as jnp
        import numpy as np
        D_MODEL = 256
        HEAD = 16
        D_K = D_MODEL // HEAD
        NEG = -1000000000.0
        B, S, _ = q.shape

        def proj(x, w):
            return (x @ w.T).reshape(B, -1, HEAD, D_K).transpose(0, 2, 1, 3)
        Q = proj(q, w_q)
        K = proj(k, w_k)
        V = proj(v, w_v)
        scores = jnp.einsum('bhqd,bhkd->bhqk', Q, K) / jnp.sqrt(jnp.float32(D_K))
        scores = jnp.where(mask == 0, NEG, scores)
        attn = jax.nn.softmax(scores, axis=-1)
        x = jnp.einsum('bhqk,bhkd->bhqd', attn, V)
        x = x.transpose(0, 2, 1, 3).reshape(B, S, HEAD * D_K)
        return x @ w_o.T

    def _L2_attn_ref(hidden_states, Wq, Wk, Wv, Wb, conv_w_q, conv_w_k, conv_w_v, fir_short_w, fir_long_w, mlp_w1, mlp_b1, mlp_w2, mlp_b2, logit_temp, conv_res_logit, rms_w, Wo):
        import jax, jax.numpy as jnp
        import numpy as np
        B, L, D, H = (2, 1024, 256, 4)
        DK = D // H
        DV = D // H
        CONV_K = 4
        FIR_S, FIR_L = (5, 64)
        GATE_HID = D * 2 // 2
        CHUNK = 32
        FLOOR_EPS = 0.08
        GATE_BIAS = np.array([-0.5, -0.5, 1.0, 3.0], np.float32)
        GATE_LOGIT_INIT = float(np.log(np.expm1(0.7)))
        CONV_RES_INIT = float(np.log(0.1 / 0.9))

        def _l2norm(x):
            return x / jnp.sqrt(jnp.sum(x * x, -1, keepdims=True) + 1e-12)

        def _causal_dwconv(x, w):
            k = w.shape[-1]
            xp = jnp.pad(x, ((0, 0), (k - 1, 0), (0, 0))).transpose(0, 2, 1)
            y = jax.lax.conv_general_dilated(xp, w[:, None, :], (1,), 'VALID', feature_group_count=w.shape[0], dimension_numbers=('NCH', 'OIH', 'NCH'))
            return y.transpose(0, 2, 1)

        def _delta_chunkwise(q, k, v, beta):
            b, h, Lq, dk = q.shape
            dv = v.shape[-1]
            c = CHUNK
            n = Lq // c
            q = _l2norm(q)
            k = _l2norm(k)
            v = v * beta[..., None]
            kb = k * beta[..., None]
            rs = lambda t: t.reshape(b, h, n, c, t.shape[-1])
            q, k, v, kb = map(rs, (q, k, v, kb))
            tri_lo_strict = jnp.tril(jnp.ones((c, c), bool), -1)
            tri_lo = jnp.tril(jnp.ones((c, c), bool), 0)
            A = jnp.where(tri_lo_strict, kb @ jnp.swapaxes(k, -1, -2), 0.0)
            eye = jnp.eye(c, dtype=q.dtype)
            inv = jax.scipy.linalg.solve_triangular(eye + A, jnp.broadcast_to(eye, A.shape), lower=True, unit_diagonal=True)
            u = inv @ v
            w = inv @ kb

            def step(S, xs):
                qi, ki, ui, wi = xs
                attn = jnp.where(tri_lo, qi @ jnp.swapaxes(ki, -1, -2), 0.0)
                u_i = ui - wi @ S
                o = qi @ S + attn @ u_i
                return (S + jnp.swapaxes(ki, -1, -2) @ u_i, o)
            mv = lambda t: jnp.moveaxis(t, 2, 0)
            S0 = jnp.zeros((b, h, dk, dv), q.dtype)
            _, out = jax.lax.scan(step, S0, (mv(q), mv(k), mv(u), mv(w)))
            return jnp.moveaxis(out, 0, 2).reshape(b, h, Lq, dv)

        def _stats(x):
            mean = jnp.mean(x, -1, keepdims=True)
            var = jnp.var(x, -1, keepdims=True)
            am = jnp.mean(jnp.abs(x), -1, keepdims=True)
            l2 = jnp.linalg.norm(x, axis=-1, keepdims=True)
            return jnp.concatenate([mean, var, am, l2], -1)
        hs = hidden_states
        b, l, _ = hs.shape
        silu = jax.nn.silu
        q = silu(_causal_dwconv(hs @ Wq, conv_w_q))
        k = silu(_causal_dwconv(hs @ Wk, conv_w_k))
        v = silu(_causal_dwconv(hs @ Wv, conv_w_v))
        qh = q.reshape(b, l, H, DK)
        kh = k.reshape(b, l, H, DK)
        vh = v.reshape(b, l, H, DV)
        beta = jax.nn.sigmoid(hs @ Wb)
        tr = lambda t: jnp.transpose(t, (0, 2, 1, 3))
        delta_out = tr(_delta_chunkwise(tr(qh), tr(kh), tr(vh), jnp.transpose(beta, (0, 2, 1))))
        fir = lambda x, w: _causal_dwconv(x.reshape(b, l, H * DV), w.reshape(H * DV, -1)).reshape(b, l, H, DV)
        local_short = fir(vh, fir_short_w)
        local_long = fir(vh, fir_long_w)
        stats = jnp.concatenate([_stats(local_short), _stats(local_long), _stats(delta_out), _stats(vh)], -1)
        hs_exp = jnp.broadcast_to(hs[:, :, None, :], (b, l, H, hs.shape[-1]))
        gate_in = jnp.concatenate([hs_exp, stats], -1)
        hgate = jax.nn.gelu(gate_in @ mlp_w1 + mlp_b1, approximate=False)
        logits = hgate @ mlp_w2 + mlp_b2
        temp = jax.nn.softplus(logit_temp) + 1e-06
        probs = jax.nn.softmax(logits / temp, -1)
        floor = jnp.array([FLOOR_EPS, FLOOR_EPS, 0.0, 0.0], probs.dtype)
        probs = probs * (1.0 - 2.0 * FLOOR_EPS) + floor
        o = probs[..., 0:1] * local_short + probs[..., 1:2] * local_long + probs[..., 2:3] * delta_out + probs[..., 3:4] * vh
        o = o + jax.nn.sigmoid(conv_res_logit)[None, None, :, None] * local_short
        o = o * jax.lax.rsqrt(jnp.mean(o * o, -1, keepdims=True) + 1e-05) * rms_w
        return o.reshape(b, l, H * DV) @ Wo

    def _L2_ffn_ref(x, wqkv, q_scale, k_scale, wo, ln_g, ln_b, w1, b1, w2, b2):
        import jax, jax.numpy as jnp
        import numpy as np
        DIM = 256
        DEPTH = 2
        HEADS = 8
        DIM_HEAD = 64
        WINDOW = 128
        INNER = HEADS * DIM_HEAD
        HID = int(DIM * 4 * 2 / 3)
        B, N = (2, 2048)
        QK_SCALE = 8.0

        def shift_token(t):
            t1, t2 = jnp.split(t, 2, axis=-1)
            t2 = jnp.pad(t2, ((0, 0), (1, 0), (0, 0)))[:, :-1]
            return jnp.concatenate([t1, t2], axis=-1)

        def l2norm(t):
            return t / jnp.clip(jnp.linalg.norm(t, axis=-1, keepdims=True), 1e-12)

        def rotate_half(x):
            x1, x2 = jnp.split(x, 2, axis=-1)
            return jnp.concatenate([-x2, x1], axis=-1)

        def rotary_xpos(q, k):
            n = q.shape[-2]
            half_idx = jnp.arange(0, DIM_HEAD, 2, dtype=jnp.float32)
            inv_freq = 1.0 / 10000.0 ** (half_idx / DIM_HEAD)
            t = jnp.arange(n, dtype=jnp.float32)
            freqs = t[:, None] * inv_freq[None, :]
            freqs = jnp.concatenate([freqs, freqs], axis=-1)
            base = (half_idx + 0.4 * DIM_HEAD) / (1.4 * DIM_HEAD)
            power = (t - n // 2) / float(WINDOW // 2)
            scale = base[None, :] ** power[:, None]
            scale = jnp.concatenate([scale, scale], axis=-1)
            cos, sin = (jnp.cos(freqs), jnp.sin(freqs))
            q = q * cos * scale + rotate_half(q) * sin * scale
            k = k * cos / scale + rotate_half(k) * sin / scale
            return (q, k)

        def local_attention(q, k, v):
            b, h, n, d = q.shape
            w = n // WINDOW
            bq = q.reshape(b, h, w, WINDOW, d) * QK_SCALE
            bk = k.reshape(b, h, w, WINDOW, d)
            bv = v.reshape(b, h, w, WINDOW, d)

            def look_around(t):
                p = jnp.pad(t, ((0, 0), (0, 0), (1, 0), (0, 0), (0, 0)))
                return jnp.concatenate([p[:, :, :w], p[:, :, 1:]], axis=3)
            bk, bv = (look_around(bk), look_around(bv))
            bt = jnp.arange(n).reshape(w, WINDOW)
            btp = jnp.pad(bt, ((1, 0), (0, 0)), constant_values=-1)
            btk = jnp.concatenate([btp[:w], btp[1:]], axis=1)
            sim = jnp.einsum('bhwid,bhwjd->bhwij', bq, bk)
            i = bt[:, :, None]
            j = btk[:, None, :]
            mask = (i < j) | (i > j + WINDOW) | (j == -1)
            sim = jnp.where(mask, -jnp.finfo(sim.dtype).max, sim)
            attn = jax.nn.softmax(sim, axis=-1)
            out = jnp.einsum('bhwij,bhwjd->bhwid', attn, bv)
            return out.reshape(b, h, n, d)

        def _layer(x, wqkv, qs, ksc, wo, lg, lb, w1, b1, w2, b2):
            b, n, _ = x.shape
            h = shift_token(x)
            qkv = h @ wqkv
            q, k, v = jnp.split(qkv, 3, axis=-1)
            to_heads = lambda t: t.reshape(b, n, HEADS, DIM_HEAD).transpose(0, 2, 1, 3)
            q, k, v = (to_heads(q), to_heads(k), to_heads(v))
            q = l2norm(q) * qs
            k = l2norm(k) * ksc
            q, k = rotary_xpos(q, k)
            o = local_attention(q, k, v)
            o = o.transpose(0, 2, 1, 3).reshape(b, n, INNER)
            x = x + o @ wo
            h = shift_token(x)
            mu = h.mean(-1, keepdims=True)
            var = h.var(-1, keepdims=True)
            h = (h - mu) / jnp.sqrt(var + 1e-05) * lg + lb
            h = h @ w1 + b1
            a, g = jnp.split(h, 2, axis=-1)
            h = a * jax.nn.gelu(g, approximate=False)
            x = x + h @ w2 + b2
            return x
        for l in range(DEPTH):
            x = _layer(x, wqkv[l], q_scale[l], k_scale[l], wo[l], ln_g[l], ln_b[l], w1[l], b1[l], w2[l], b2[l])
        return x

    def _L3_xattn_ref(query, key):
        import jax, jax.numpy as jnp
        import numpy as np
        energy = jnp.einsum('bqd,bkd->bqk', query, key)
        attention = jax.nn.softmax(energy, axis=-1)
        return jnp.einsum('bqk,bkd->bqd', attention, key)

    def _L3_attn_ref(x, Wq, bq, Wkv, bkv, Wo):
        import jax, jax.numpy as jnp
        import numpy as np
        import math
        NUM_HEADS = 8
        EMB = 256
        HEAD_DIM = 128
        B, T = (1, 1024)

        def sinusoidal_pe(T, d, dtype=jnp.float32):
            pos = jnp.arange(T, dtype=dtype)[:, None]
            inv_freq = jnp.exp(-math.log(10000.0) * jnp.arange(0, d, 2, dtype=dtype) / d)
            ang = pos * inv_freq[None, :]
            pe = jnp.zeros((T, d), dtype=dtype)
            pe = pe.at[:, 0::2].set(jnp.sin(ang))
            pe = pe.at[:, 1::2].set(jnp.cos(ang))
            return pe
        Bsz, Tlen, E = x.shape
        q = (x @ Wq + bq).reshape(Bsz, Tlen, NUM_HEADS, HEAD_DIM)
        kv = x @ Wkv + bkv
        k, v = (kv[..., :HEAD_DIM], kv[..., HEAD_DIM:])
        q = jnp.transpose(q, (0, 2, 1, 3))
        pe = sinusoidal_pe(Tlen, HEAD_DIM, x.dtype)
        q = q + pe[None, None, :, :]
        k = k + pe[None, :, :]
        scale = 1.0 / math.sqrt(HEAD_DIM)
        scores = jnp.einsum('bhqd,bkd->bhqk', q, k) * scale
        causal = jnp.tril(jnp.ones((Tlen, Tlen), dtype=bool))
        scores = jnp.where(causal[None, None, :, :], scores, jnp.finfo(scores.dtype).min)
        probs = jax.nn.softmax(scores, axis=-1)
        attn = jnp.einsum('bhqk,bkd->bhqd', probs, v)
        out = jnp.transpose(attn, (0, 2, 1, 3)).reshape(Bsz, Tlen, NUM_HEADS * HEAD_DIM)
        return out @ Wo

    def _L3_ffn_ref(x, t_emb, sw1, sb1, sw3, sb3, sw2, sb2, w1, b1, w2, b2):
        import jax, jax.numpy as jnp
        import numpy as np
        E = 8
        TOPK = 2
        PRIME = 11
        HASH_OFF = 7919
        N_SHARED = 1
        B, T, C = x.shape
        N = B * T
        xf = x.reshape(N, C)
        shared = jax.nn.silu(xf @ sw1 + sb1) * (xf @ sw3 + sb3) @ sw2 + sb2
        tok = jnp.arange(N)
        out = jnp.zeros((N, C), x.dtype)
        for k in range(TOPK):
            exp_ids = (tok * PRIME + k * HASH_OFF) % E
            sort_idx = jnp.argsort(exp_ids)
            xs = xf[sort_idx].reshape(E, N // E, C)
            h = jax.nn.gelu(jnp.einsum('enc,ech->enh', xs, w1) + b1[:, None, :], approximate=False)
            y = jnp.einsum('enh,ehc->enc', h, w2) + b2[:, None, :]
            out = out.at[sort_idx].add(y.reshape(N, C))
        out = out / TOPK
        return ((shared + out) / (N_SHARED + 1)).reshape(B, T, C)
    x = x + _L0_xattn_ref(_layernorm(x, axis=-1), ctx_1024, L0_xattn_Wq, L0_xattn_Wk, L0_xattn_Wv, L0_xattn_gru_wi, L0_xattn_gru_wh, L0_xattn_gru_bi, L0_xattn_gru_bh, L0_xattn_slot_norm_w, L0_xattn_input_norm_w)
    x = x + _L0_attn_ref(_layernorm(x, axis=-1), L0_attn_qK, L0_attn_qV, L0_attn_kK, L0_attn_kV, L0_attn_vK, L0_attn_vV, L0_attn_pK, L0_attn_pV, L0_attn_fK, L0_attn_fV)
    x = x + _L0_ffn_ref(_layernorm(x, axis=-1), L0_ffn_w_gate, L0_ffn_w_up, L0_ffn_w_down)
    x = x + _L1_xattn_ref(_layernorm(x, axis=-1), ctx_1024, ctx_1024, _lenS2, _lenS2, L1_xattn_W, L1_xattn_b)
    x = x + _L1_attn_ref(_layernorm(x, axis=-1), L1_attn_Wqkv, L1_attn_bqkv, L1_attn_Wo, L1_attn_bo)
    x = x + _L1_ffn_ref(_layernorm(x, axis=-1), L1_ffn_Wg, L1_ffn_w1, L1_ffn_w2)
    x = x + _L2_xattn_ref(_layernorm(x, axis=-1), ctx_1024, ctx_1024, mask_1x1xSxS2_if1, L2_xattn_w_q, L2_xattn_w_k, L2_xattn_w_v, L2_xattn_w_o)
    x = x + _L2_attn_ref(_layernorm(x, axis=-1), L2_attn_Wq, L2_attn_Wk, L2_attn_Wv, L2_attn_Wb, L2_attn_conv_w_q, L2_attn_conv_w_k, L2_attn_conv_w_v, L2_attn_fir_short_w, L2_attn_fir_long_w, L2_attn_mlp_w1, L2_attn_mlp_b1, L2_attn_mlp_w2, L2_attn_mlp_b2, L2_attn_logit_temp, L2_attn_conv_res_logit, L2_attn_rms_w, L2_attn_Wo)
    x = x + _L2_ffn_ref(_layernorm(x, axis=-1), L2_ffn_wqkv, L2_ffn_q_scale, L2_ffn_k_scale, L2_ffn_wo, L2_ffn_ln_g, L2_ffn_ln_b, L2_ffn_w1, L2_ffn_b1, L2_ffn_w2, L2_ffn_b2)
    x = x + _L3_xattn_ref(_layernorm(x, axis=-1), ctx_1024)
    x = x + _L3_attn_ref(_layernorm(x, axis=-1), L3_attn_Wq, L3_attn_bq, L3_attn_Wkv, L3_attn_bkv, L3_attn_Wo)
    x = x + _L3_ffn_ref(_layernorm(x, axis=-1), L3_ffn_t_emb, L3_ffn_sw1, L3_ffn_sb1, L3_ffn_sw3, L3_ffn_sb3, L3_ffn_sw2, L3_ffn_sb2, L3_ffn_w1, L3_ffn_b1, L3_ffn_w2, L3_ffn_b2)
    return x

_drawn_inputs = setup_inputs


def setup_inputs(seed=0):
    import zlib

    import numpy as np

    out = dict(_drawn_inputs(seed))
    spreads = {'L0_xattn_slot_norm_w': (1.0, 0.6),
     'L0_xattn_input_norm_w': (1.0, 0.6),
     'L2_attn_mlp_b1': (0.0, 2.0),
     'L2_attn_conv_res_logit': (-2.1972246170043945, 0.6),
     'L2_attn_rms_w': (1.0, 0.6),
     'L2_ffn_q_scale': (1.0, 0.6),
     'L2_ffn_k_scale': (1.0, 0.6),
     'L2_ffn_ln_g': (1.0, 0.6),
     'L2_ffn_ln_b': (0.0, 0.8),
     'L2_ffn_b1': (0.0, 0.8),
     'L2_ffn_b2': (0.0, 0.1),
     'L3_ffn_sb1': (0.0, 0.8),
     'L3_ffn_sb3': (0.0, 0.8),
     'L3_ffn_sb2': (0.0, 0.618),
     'L3_ffn_b1': (0.0, 0.8),
     'L3_ffn_b2': (0.0, 0.8)}
    factors = {'L0_xattn_Wq': 8.0,
     'L0_xattn_Wk': 8.0,
     'L0_xattn_gru_bi': 3.131,
     'L0_xattn_gru_bh': 4.879,
     'L0_attn_qK': 8.0,
     'L0_attn_qV': 8.0,
     'L0_attn_kK': 8.0,
     'L0_attn_kV': 8.0,
     'L0_attn_vK': 8.0,
     'L0_attn_vV': 8.0,
     'L0_attn_pK': 8.0,
     'L1_xattn_b': 6.129,
     'L1_attn_bqkv': 6.395,
     'L1_attn_bo': 4.106,
     'L1_ffn_Wg': 7.202,
     'L1_ffn_w1': 7.496,
     'L1_ffn_w2': 6.072,
     'L2_attn_Wq': 8.0,
     'L2_attn_Wk': 8.0,
     'L2_attn_Wb': 8.0,
     'L2_attn_conv_w_q': 8.0,
     'L2_attn_conv_w_k': 8.0,
     'L2_attn_fir_long_w': 3.843,
     'L2_attn_mlp_w1': 8.0,
     'L2_attn_mlp_w2': 8.0,
     'L3_attn_bq': 8.0,
     'L3_attn_bkv': 3.733}
    for name, (base, spread) in spreads.items():
        noise = np.random.default_rng([zlib.crc32(name.encode()), seed]).standard_normal(out[name].shape)
        drawn = base * np.exp(spread * noise) if base else spread * noise
        out[name] = jnp.asarray(drawn.astype(out[name].dtype))
    for name, factor in factors.items():
        out[name] = (out[name] * factor).astype(out[name].dtype)
    return out
```

```python
from contextlib import ExitStack

import numpy as np
import concourse.bass as bass
from concourse import mybir

ALU = mybir.AluOpType
ACT = mybir.ActivationFunctionType
F32 = mybir.dt.float32
BF16 = mybir.dt.bfloat16
I32 = mybir.dt.int32
X_AXIS = mybir.AxisListType.X
PSUM_BANK = 512

P = 128
D = 256
DC = D // P
CTX = 12544
TILE = 7
GROUP = TILE * P
GROUPS = CTX // GROUP
KEYS_A = PSUM_BANK
KEYS_B = GROUP - KEYS_A
LN_EPS = 1e-5
MASKED = -1e30
ROUND = 12582912.0
STAGES = range(12)


class Stage:

    def __init__(self, nc, name):
        self.nc, self.name, self.sems = nc, name, {}

    def __enter__(self):
        self.mem = ExitStack()
        return self

    def sb(self, name, shape, dt=F32):
        return self.mem.enter_context(self.nc.sbuf_tensor(f"{self.name}_{name}", shape, dt))

    def psum(self, name, banks=1):
        return self.mem.enter_context(self.nc.psum_tensor(f"{self.name}_{name}", [P, banks * PSUM_BANK], F32))

    def pack(self, dram, spec):
        buf = self.sb("weights", [P, sum(n for _, n in spec)])
        at, parts = 0, {}
        for name, n in spec:
            parts[name] = buf[:, at:at + n]
            at += n
        return buf, parts

    def __call__(self, name):
        if name not in self.sems:
            self.sems[name] = self.nc.alloc_semaphore(name=f"{self.name}_{name}")
        return self.sems[name]

    def __exit__(self, kind, *_):
        if kind is None:
            self.nc.clear_and_free_semaphores(list(self.sems.values()))
            self.nc.all_engine_barrier()
        self.mem.close()


def linked(eng, sem):
    count = [0]

    def link(ins):
        count[0] += 1
        ins.then_inc(sem, 1)
        eng.wait_ge(sem, count[0])
    return link


def await_count(eng, sem, count):
    if not (isinstance(count, int) and count <= 0):
        eng.wait_ge(sem, count)


def chunks(ap, n):
    return ap.rearrange("p (c n) -> p c n", n=n)


def spread(ap, n):
    return ap.unsqueeze(2).to_broadcast([ap.shape[0], ap.shape[1], n])


def repeat(ap, n):
    return ap.unsqueeze(1).to_broadcast([ap.shape[0], n, ap.shape[1]])


def product(pe, out, pairs):
    for i, (lhs, rhs) in enumerate(pairs):
        last = pe.matmul(out, lhs, rhs, start=i == 0, stop=i == len(pairs) - 1)
    return last


def transposes(pe, out, src, ident, n):
    for c in range(n):
        last = pe.transpose(out[:, c, :], src[:, c * P:(c + 1) * P], ident)
    return last



def norm_buffers(st, tag):
    return st.sb(f"{tag}_stats", [P, 6]), st.sb(f"{tag}_mv", [P, 4])


def norm_vector(dve, link, st, tag, x, out, bufs, eps=LN_EPS):
    stats, mv = bufs
    link(dve.bn_stats(stats[:, :], x))
    link(dve.bn_aggr(mv[:, 0:2], stats[:, :]))
    dve.tensor_scalar(mv[:, 2:3], mv[:, 1:2], eps, None, ALU.add).then_inc(st(f"{tag}_var"), 1)
    dve.wait_ge(st(f"{tag}_std"), 1)
    link(dve.reciprocal(mv[:, 2:3], mv[:, 3:4]))
    dve.tensor_scalar(out, x, mv[:, 0:1], mv[:, 2:3], ALU.subtract, ALU.mult).then_inc(st(f"{tag}_done"), 1)
    dve.wait_ge(st(f"{tag}_done"), 1)


def norm_scalar(act, st, tag, bufs):
    act.wait_ge(st(f"{tag}_var"), 1)
    act.activation(bufs[1][:, 3:4], bufs[1][:, 2:3], ACT.Sqrt).then_inc(st(f"{tag}_std"), 1)



def softmax_vector(dve, link, st, tag, src, e, small, scale, mask=None):
    heads, n = e.shape[1], e.shape[2]
    if mask is not None:
        link(dve.scalar_tensor_tensor(out=e, in0=src, scalar=scale, in1=repeat(mask, heads),
                                      op0=ALU.mult, op1=ALU.add))
        src = e
    link(dve.tensor_reduce(small[:, 0, :], src, X_AXIS, ALU.max))
    dve.tensor_tensor(e, src, spread(small[:, 0, :], n), ALU.subtract).then_inc(st(f"{tag}_shifted"), 1)
    dve.wait_ge(st(f"{tag}_exp"), 1)
    link(dve.tensor_reduce(small[:, 1, :], e, X_AXIS, ALU.add))
    link(dve.reciprocal(small[:, 0, :], small[:, 1, :]))
    dve.tensor_tensor(e, e, spread(small[:, 0, :], n), ALU.mult).then_inc(st(f"{tag}_probs"), 1)
    dve.wait_ge(st(f"{tag}_probs"), 1)


def softmax_scalar(act, st, tag, e, scale):
    act.wait_ge(st(f"{tag}_shifted"), 1)
    act.activation(e, e, ACT.Exp, scale=scale).then_inc(st(f"{tag}_exp"), 1)


def residual_vector(dve, st, x, add, ready):
    dve.wait_ge(st(ready), 1)
    dve.tensor_tensor(x, x, add, ALU.add).then_inc(st("residual"), 1)
    dve.wait_ge(st("residual"), 1)



SLOT_SPEC = [("wq", DC * D), ("wk", DC * D), ("wv", DC * D), ("wi", DC * 3 * D), ("wh", DC * 3 * D),
             ("bi", 3 * D), ("bh", 3 * D), ("slot_w", D), ("in_w", DC)]
SLOT_ITERS = 3
SLOT_EPS = 1e-6


def stage_context(nc, K, T, name="load"):
    with Stage(nc, name) as st:
        HALF = TILE // 2
        square = st.sb("square", [P, 2 * HALF, D])
        square_d = st.sb("square_d", [P, TILE - TILE // 2, D])
        ms = st.sb("ms", [P, GROUPS * TILE])
        rows = T["ctx_rows"]
        with nc.Block() as block:
            @block.sync
            def _(sp):
                def load(i, b, first=False):
                    group, tile = (i * 2 + b, i * (2 * TILE) + b * TILE) if first else \
                        (sp.snap(i * 2 + b), sp.snap(i * (2 * TILE) + b * TILE))
                    if not first:
                        sp.wait_ge(st(f"rows_in{b}"), i * 16)
                    sp.dma_start(K.ctx[:, bass.ds(tile, TILE), 0:D],
                                 rows[bass.ds(group, 1)].rearrange("o p t d -> p (o t) d")
                                 ).then_inc(st(f"rows_in{b}"), 16)

                load(0, 0, first=True)
                load(0, 1, first=True)
                with sp.Fori(1, GROUPS // 2) as i:
                    load(i, 0)
                    load(i, 1)

            @block.scalar
            def _(act):
                def squares(i, b, first=False):
                    act.wait_ge(st(f"rows_in{b}"), i * 16 + 16)
                    if not first:
                        act.wait_ge(st("ms_s"), i * (2 * HALF))
                    for t in range(HALF):
                        tile = i * (2 * TILE) + b * TILE + t
                        act.activation(square[:, b * HALF + t:b * HALF + t + 1, :], K.ctx[:, bass.ds(tile, 1), 0:D], ACT.Square,
                                       accum_out=ms[:, bass.ds(tile, 1)]).then_inc(st("ms_s"), 1)

                squares(0, 0, first=True)
                squares(0, 1, first=True)
                with act.Fori(1, GROUPS // 2) as i:
                    squares(i, 0)
                    squares(i, 1)
                act.wait_ge(st("ms_mean"), 1)
                act.activation(K.ctx[:, :, D], ms[:, :], ACT.Sqrt).then_inc(st("rms"), 1)

            @block.vector
            def _(dve):
                def squares(i, b, first=False):
                    dve.wait_ge(st(f"rows_in{b}"), i * 16 + 16)
                    some = bass.ds(i * (2 * TILE) + b * TILE + HALF, TILE - HALF)
                    if not first:
                        dve.wait_ge(st("ms_d"), i * 2 + b)
                    dve.tensor_tensor(square_d[:, :], K.ctx[:, some, 0:D], K.ctx[:, some, 0:D], ALU.mult).then_inc(st("squared"), 1)
                    dve.wait_ge(st("squared"), i * 2 + b + 1)
                    dve.tensor_reduce(ms[:, some], square_d[:, :], X_AXIS, ALU.add).then_inc(st("ms_d"), 1)

                squares(0, 0, first=True)
                squares(0, 1)
                with dve.Fori(1, GROUPS // 2) as i:
                    squares(i, 0)
                    squares(i, 1)
                dve.wait_ge(st("ms_s"), GROUPS * HALF)
                dve.wait_ge(st("ms_d"), GROUPS)
                link = linked(dve, st("ms_mean"))
                link(dve.tensor_scalar(ms[:, :], ms[:, :], 1.0 / D, SLOT_EPS, ALU.mult, ALU.add))
                dve.wait_ge(st("rms"), 1)
                dve.reciprocal(K.rinv[:, :], K.ctx[:, :, D]).then_inc(st("rinv"), 1)
                dve.wait_ge(st("rinv"), 1)


def stage_slots(nc, K, T):
    with Stage(nc, "slots") as st:
        wbuf, W = st.pack(nc, SLOT_SPEC)
        wq, wk, wv = (chunks(W[n], D) for n in ("wq", "wk", "wv"))
        wi, wh = chunks(W["wi"], 3 * D), chunks(W["wh"], 3 * D)
        ctxT = st.sb("ctxT", [P, 2, DC, GROUP])
        probs = st.sb("probs", [P, 2, TILE, P])
        slots = st.sb("slots", [P, D])
        normed = st.sb("normed", [P, D])
        slotsT = st.sb("slotsT", [P, DC, P])
        normedT = st.sb("normedT", [P, DC, P])
        qT = st.sb("qT", [P, DC, P])
        qkT = st.sb("qkT", [P, DC, P])
        pooled = st.sb("pooled", [P, D + 1])
        pooledT = st.sb("pooledT", [P, DC, P])
        updT = st.sb("updT", [P, DC, P])
        gate = st.sb("gate", [P, 2 * D])
        cand = st.sb("cand", [P, D])
        hcand = st.sb("hcand", [P, D])
        small = st.sb("small", [P, 8])
        rg = st.sb("rg", [P, 2, 4, TILE])
        lnb = norm_buffers(st, "ln")
        scores = st.psum("scores", 4)
        attended = st.psum("attended", 2)
        mm = st.psum("mm", 2)
        sc = [scores[:, b * 1024:b * 1024 + GROUP].rearrange("p (t k) -> p t k", k=P) for b in range(2)]
        at = [attended[:, b * 512:b * 512 + D + 1] for b in range(2)]
        mmT = mm[:, 0:512].rearrange("p (a c k) -> p a c k", a=2, k=P)
        rz, hn, inn = mm[:, 0:512], mm[:, 512:768], mm[:, 768:1024]
        PAIRS = GROUPS // 2

        with nc.Block() as block:
            @block.sync
            def _(sp):
                sp.dma_start(wbuf[:, :], T["w_slots"]).then_inc(st("weights"), 16)

                def load(i, n, b, first=False):
                    if first:
                        group = i * 2 + b
                    else:
                        group, done = sp.snap(i * 2 + b), sp.snap(n)
                        sp.wait_ge(st(f"scored{b}"), done)
                    sp.dma_start(ctxT[:, b], T["ctxT"][bass.ds(group, 1)].rearrange("o p c m -> p (o c) m")
                                 ).then_inc(st(f"ctxT_in{b}"), 16)

                for it in range(SLOT_ITERS):
                    load(0, it * PAIRS, 0, first=it == 0)
                    load(0, it * PAIRS, 1, first=it == 0)
                    with sp.Fori(1, PAIRS) as i:
                        load(i, i + it * PAIRS, 0)
                        load(i, i + it * PAIRS, 1)

            @block.tensor
            def _(pe):
                pe.wait_ge(st("weights"), 16)
                for it in range(SLOT_ITERS):
                    pe.wait_ge(st("normed"), it + 1)
                    transposes(pe, mmT[:, 0], slots, K.ident, DC)
                    transposes(pe, mmT[:, 1], normed, K.ident, DC).then_inc(st("slotsT_mm"), 1)
                    pe.wait_ge(st("normedT"), it + 1)
                    for c in range(DC):
                        last = product(pe, mmT[:, 0, c], [(wq[:, k, c * P:(c + 1) * P], normedT[:, k]) for k in range(DC)])
                    last.then_inc(st("q_mm"), 1)
                    pe.wait_ge(st("qT"), it + 1)
                    for c in range(DC):
                        last = product(pe, mmT[:, 1, c], [(wk[:, k, c * P:(c + 1) * P], qT[:, k]) for k in range(DC)])
                    last.then_inc(st("qk_mm"), 1)
                    pe.wait_ge(st("qkT"), it + 1)

                    def score(n, b, first=False):
                        pe.wait_ge(st(f"ctxT_in{b}"), n * 16 + 16)
                        if not first:
                            pe.wait_ge(st(f"exp{b}"), n)
                        for t in range(TILE):
                            last = product(pe, sc[b][:, t], [(ctxT[:, b, c, t * P:(t + 1) * P], qkT[:, c]) for c in range(DC)])
                        last.then_inc(st(f"scored{b}"), 1)

                    def attend(i, n, b):
                        pe.wait_ge(st(f"probs{b}"), n + 1)
                        if not (isinstance(n, int) and n == 0):
                            pe.wait_ge(st(f"added{b}"), n)
                        for t in range(TILE):
                            last = pe.matmul(at[b].unsqueeze(1), probs[:, b, t],
                                             K.ctx[:, bass.ds(i * (2 * TILE) + b * TILE + t, 1), :],
                                             start=t == 0, stop=t == TILE - 1)
                        last.then_inc(st(f"attended{b}"), 1)

                    n0 = it * PAIRS
                    score(n0, 0, first=it == 0)
                    score(n0, 1, first=it == 0)
                    attend(0, n0, 0)
                    with pe.Fori(1, PAIRS) as i:
                        score(i + n0, 0)
                        attend(i - 1, i - 1 + n0, 1)
                        score(i + n0, 1)
                        attend(i, i + n0, 0)
                    attend(PAIRS - 1, PAIRS - 1 + n0, 1)

                    pe.wait_ge(st("pooled"), it + 1)
                    transposes(pe, mmT[:, 0], pooled, K.ident, DC).then_inc(st("pooledT_mm"), 1)
                    pe.wait_ge(st("pooledT"), it + 1)
                    for c in range(DC):
                        last = product(pe, mmT[:, 1, c], [(wv[:, k, c * P:(c + 1) * P], pooledT[:, k]) for k in range(DC)])
                    last.then_inc(st("upd_mm"), 1)
                    pe.wait_ge(st("updT"), it + 1)
                    both = [(updT[:, k], wi[:, k, :]) for k in range(DC)] + [(slotsT[:, k], wh[:, k, :]) for k in range(DC)]
                    product(pe, rz, [(a, w[:, 0:2 * D]) for a, w in both])
                    product(pe, inn, [(a, w[:, 2 * D:]) for a, w in both[:DC]])
                    product(pe, hn, [(a, w[:, 2 * D:]) for a, w in both[DC:]]).then_inc(st("gates_mm"), 1)

            @block.scalar
            def _(act):
                norm_scalar(act, st, "ln", lnb)
                for it in range(SLOT_ITERS):
                    act.wait_ge(st("ms"), it + 1)
                    act.activation(small[:, 2:3], small[:, 1:2], ACT.Sqrt).then_inc(st("rms"), 1)

                    def exponentials(n):
                        for b in range(2):
                            act.wait_ge(st(f"bias{b}"), n + 1)
                            for t in range(TILE):
                                last = act.activation(probs[:, b, t], sc[b][:, t], ACT.Exp, bias=rg[:, b, 1, t:t + 1],
                                                      scale=rg[:, b, 0, t:t + 1], accum_out=rg[:, b, 2, t:t + 1])
                            last.then_inc(st(f"exp{b}"), 1)

                    exponentials(it * PAIRS)
                    with act.Fori(1, PAIRS) as i:
                        exponentials(i + it * PAIRS)
                    act.wait_ge(st("gates_in"), it + 1)
                    act.activation(gate[:, :], gate[:, :], ACT.Sigmoid).then_inc(st("gates"), 1)
                    act.wait_ge(st("cand_in"), it + 1)
                    act.activation(cand[:, :], cand[:, :], ACT.Tanh).then_inc(st("cand"), 1)

            @block.vector
            def _(dve):
                link = linked(dve, st("vector_step"))
                norm_vector(dve, link, st, "ln", K.x, slots[:, :], lnb)
                dve.wait_ge(st("weights"), 16)
                link(dve.tensor_tensor(W["bi"][:, 0:2 * D], W["bi"][:, 0:2 * D], W["bh"][:, 0:2 * D], ALU.add))
                for it in range(SLOT_ITERS):
                    link(dve.tensor_tensor_reduce(normed[:, :], slots[:, :], slots[:, :], 1.0, 0.0, ALU.mult, ALU.add, small[:, 0:1]))
                    dve.tensor_scalar(small[:, 1:2], small[:, 0:1], 1.0 / D, SLOT_EPS, ALU.mult, ALU.add).then_inc(st("ms"), 1)
                    dve.wait_ge(st("rms"), it + 1)
                    link(dve.reciprocal(small[:, 3:4], small[:, 2:3]))
                    dve.scalar_tensor_tensor(out=normed[:, :], in0=slots[:, :], scalar=small[:, 3:4], in1=W["slot_w"],
                                             op0=ALU.mult, op1=ALU.mult).then_inc(st("normed"), 1)
                    dve.wait_ge(st("slotsT_mm"), it + 1)
                    dve.tensor_copy(slotsT[:, :], mmT[:, 0])
                    dve.tensor_copy(normedT[:, :], mmT[:, 1]).then_inc(st("normedT"), 1)
                    dve.wait_ge(st("q_mm"), it + 1)
                    dve.tensor_copy(qT[:, :], mmT[:, 0]).then_inc(st("qT"), 1)
                    dve.wait_ge(st("qk_mm"), it + 1)
                    for c in range(DC):
                        last = dve.tensor_scalar(qkT[:, c], mmT[:, 1, c], W["in_w"][:, c:c + 1], D ** -0.5, ALU.mult, ALU.mult)
                    last.then_inc(st("qkT"), 1)
                    link(dve.memset(pooled[:, :], 0.0))
                    n0 = it * PAIRS

                    def maxima(i, b):
                        dve.wait_ge(st(f"scored{b}"), i + n0 + 1)
                        dve.tensor_reduce(rg[:, b, 3], sc[b], X_AXIS, ALU.max).then_inc(st("max_step"), 1)
                        dve.tensor_copy(rg[:, b, 0], K.rinv[:, bass.ds(i * (2 * TILE) + b * TILE, TILE)]).then_inc(st("max_step"), 1)
                        dve.wait_ge(st("max_step"), (i + n0) * 4 + 2 * b + 2)
                        dve.scalar_tensor_tensor(out=rg[:, b, 1], in0=rg[:, b, 3], scalar=-1.0, in1=rg[:, b, 0],
                                                 op0=ALU.mult, op1=ALU.mult).then_inc(st(f"bias{b}"), 1)

                    def normalise(i, b):
                        dve.wait_ge(st(f"exp{b}"), i + n0 + 1)
                        dve.reciprocal(rg[:, b, 3], rg[:, b, 2]).then_inc(st("norm_step"), 1)
                        dve.wait_ge(st("norm_step"), (i + n0) * 4 + 2 * b + 1)
                        dve.tensor_tensor(rg[:, b, 2], rg[:, b, 3], rg[:, b, 0], ALU.mult).then_inc(st("norm_step"), 1)
                        dve.wait_ge(st("norm_step"), (i + n0) * 4 + 2 * b + 2)
                        dve.tensor_tensor(probs[:, b], probs[:, b], spread(rg[:, b, 2], P), ALU.mult).then_inc(st(f"probs{b}"), 1)

                    def add(i, b):
                        dve.wait_ge(st(f"attended{b}"), i + n0 + 1)
                        dve.tensor_tensor(pooled[:, :], pooled[:, :], at[b], ALU.add).then_inc(st(f"added{b}"), 1)

                    maxima(0, 0)
                    maxima(0, 1)
                    normalise(0, 0)
                    normalise(0, 1)
                    add(0, 0)
                    with dve.Fori(1, PAIRS) as i:
                        maxima(i, 0)
                        dve.wait_ge(st("added0"), i + n0)
                        add(i - 1, 1)
                        normalise(i, 0)
                        maxima(i, 1)
                        dve.wait_ge(st("added1"), i + n0)
                        add(i, 0)
                        normalise(i, 1)
                    dve.wait_ge(st("added0"), PAIRS + n0)
                    add(PAIRS - 1, 1)
                    dve.wait_ge(st("added1"), PAIRS + n0)

                    link(dve.tensor_scalar(small[:, 4:5], pooled[:, D:D + 1], SLOT_EPS, None, ALU.add))
                    link(dve.reciprocal(small[:, 5:6], small[:, 4:5]))
                    dve.tensor_scalar(pooled[:, 0:D], pooled[:, 0:D], small[:, 5:6], None, ALU.mult).then_inc(st("pooled"), 1)
                    dve.wait_ge(st("pooledT_mm"), it + 1)
                    for c in range(DC):
                        last = dve.tensor_scalar(pooledT[:, c], mmT[:, 0, c], W["in_w"][:, c:c + 1], None, ALU.mult)
                    last.then_inc(st("pooledT"), 1)
                    dve.wait_ge(st("upd_mm"), it + 1)
                    dve.tensor_copy(updT[:, :], mmT[:, 1]).then_inc(st("updT"), 1)
                    dve.wait_ge(st("gates_mm"), it + 1)
                    dve.tensor_tensor(gate[:, :], rz, W["bi"][:, 0:2 * D], ALU.add).then_inc(st("gates_in"), 1)
                    link(dve.tensor_tensor(hcand[:, :], hn, W["bh"][:, 2 * D:], ALU.add))
                    link(dve.tensor_tensor(cand[:, :], inn, W["bi"][:, 2 * D:], ALU.add))
                    dve.wait_ge(st("gates"), it + 1)
                    link(dve.tensor_tensor(hcand[:, :], hcand[:, :], gate[:, 0:D], ALU.mult))
                    dve.tensor_tensor(cand[:, :], cand[:, :], hcand[:, :], ALU.add).then_inc(st("cand_in"), 1)
                    dve.wait_ge(st("cand"), it + 1)
                    link(dve.tensor_tensor(hcand[:, :], slots[:, :], cand[:, :], ALU.subtract))
                    link(dve.tensor_tensor(hcand[:, :], hcand[:, :], gate[:, D:2 * D], ALU.mult))
                    link(dve.tensor_tensor(slots[:, :], hcand[:, :], cand[:, :], ALU.add))
                link(dve.tensor_tensor(K.x, K.x, slots[:, :], ALU.add))



def probs_transposed(pe, st, tag, out, e, ident):
    pe.wait_ge(st(f"{tag}_probs"), 1)
    for h in range(e.shape[1]):
        last = pe.transpose(out[:, h, :], e[:, h, :], ident)
    last.then_inc(st(f"{tag}_probsT_mm"), 1)



PATT = [("kk", DC * D), ("kv", DC * D), ("qk", DC * D), ("qv", DC * D), ("vk", DC * D), ("vv", DC * D),
        ("pk", DC * D), ("pv", DC * D), ("fk", DC * 4 * D), ("fv", 4 * DC * D), ("head_mask", 8)]
HEADS16 = 16
HEAD16 = D // HEADS16


def stage_pattention(nc, K, T):
    with Stage(nc, "patt") as st:
        wbuf, W0 = st.pack(nc, PATT)
        W = {n: chunks(ap, 4 * D if n == "fk" else D) for n, ap in W0.items() if n != "head_mask"}
        xin = st.sb("xin", [P, D])
        h = st.sb("h", [P, D])
        hT = st.sb("hT", [P, DC, P])
        e = {n: st.sb(f"e_{n}", [P, 1, D]) for n in "kqvp"}
        eT = {n: st.sb(f"eT_{n}", [P, DC, P]) for n in "kqvp"}
        ef = st.sb("ef", [P, 1, 4 * D])
        efT = st.sb("efT", [P, 4 * DC, P])
        qT = st.sb("qT", [P, DC, P])
        kblk = st.sb("kblk", [P, DC, 8, P])
        v = st.sb("v", [P, D])
        pr = st.sb("pr", [P, HEADS16, P])
        prT = kblk[:, :].rearrange("p c h k -> p (c h) k")
        o = st.sb("o", [P, D])
        oT = st.sb("oT", [P, DC, P])
        x2 = st.sb("x2", [P, D])
        small = st.sb("small", [P, 2, 16])
        lnb = [norm_buffers(st, f"ln{i}") for i in range(3)]
        sc = st.psum("scores", 4)
        mm = st.psum("mm", 4)
        heads = sc[:, :].rearrange("p (h k) -> p h k", k=P)
        headsT = mm[:, :].rearrange("p (h k) -> p h k", k=P)
        s_of = {"k": sc[:, 0:D], "q": sc[:, 512:512 + D], "v": sc[:, 1024:1024 + D], "p": sc[:, 1536:1536 + D]}
        t_of = {n: mm[:, 512 * i:512 * i + D].rearrange("p (c k) -> p c k", k=P) for i, n in enumerate("kqvp")}
        hT_mm = mm[:, 1536:1536 + D].rearrange("p (c k) -> p c k", k=P)
        kT_mm = sc[:, 0:D].rearrange("p (c k) -> p c k", k=P)
        qT_mm = sc[:, 512:512 + D].rearrange("p (c k) -> p c k", k=P)
        v_mm = sc[:, 1024:1024 + D]
        o_mm, oT_mm = sc[:, 0:D], sc[:, 512:512 + D].rearrange("p (c k) -> p c k", k=P)
        p_mm = mm[:, 0:D]
        h2T_mm = mm[:, 512:512 + D].rearrange("p (c k) -> p c k", k=P)
        f_sc = sc[:, 0:4 * D]
        fT_mm = mm[:, 0:4 * D].rearrange("p (c k) -> p c k", k=P)
        f_mm = sc[:, 1536:1536 + D]

        with nc.Block() as block:
            @block.sync
            def _(sp):
                sp.dma_start(wbuf[:, :], T["w_patt"]).then_inc(st("weights"), 16)

            @block.scalar
            def _(act):
                norm_scalar(act, st, "ln0", lnb[0])
                norm_scalar(act, st, "ln1", lnb[1])
                for n in "kqv":
                    softmax_scalar(act, st, n, e[n][:, :], D ** -0.5)
                softmax_scalar(act, st, "sdpa", pr[:, :], 1.0)
                softmax_scalar(act, st, "p", e["p"][:, :], D ** -0.5)
                norm_scalar(act, st, "ln2", lnb[2])
                softmax_scalar(act, st, "f", ef[:, :], D ** -0.5)

            @block.tensor
            def _(pe):
                pe.wait_ge(st("ln1_done"), 1)
                transposes(pe, hT_mm, h, K.ident, DC).then_inc(st("hT_mm"), 1)
                pe.wait_ge(st("weights"), 16)
                pe.wait_ge(st("hT"), 1)
                for n in "kqv":
                    product(pe, s_of[n], [(hT[:, c], W[n + "k"][:, c]) for c in range(DC)]).then_inc(st(f"{n}_scores"), 1)
                for n in "kqv":
                    pe.wait_ge(st(f"{n}_probs"), 1)
                    transposes(pe, t_of[n], e[n][:, 0], K.ident, DC).then_inc(st(f"{n}_probsT_mm"), 1)
                for n, out in (("k", kT_mm), ("q", qT_mm)):
                    pe.wait_ge(st(f"{n}_probsT"), 1)
                    for c in range(DC):
                        last = product(pe, out[:, c], [(W[n + "v"][:, j, c * P:(c + 1) * P], eT[n][:, j]) for j in range(DC)])
                    last.then_inc(st(f"{n}T_mm"), 1)
                pe.wait_ge(st("v_probsT"), 1)
                product(pe, v_mm, [(eT["v"][:, j], W["vv"][:, j]) for j in range(DC)]).then_inc(st("v_mm"), 1)
                pe.wait_ge(st("qT"), 1)
                pe.wait_ge(st("v"), 1)
                pe.wait_ge(st("kblk"), 1)
                for c in range(DC):
                    for j in range(2):
                        last = pe.matmul(heads[:, 8 * c + 4 * j:8 * c + 4 * j + 4, :], qT[:, c], kblk[:, c, 4 * j:4 * j + 4, :],
                                         start=True, stop=True)
                last.then_inc(st("sdpa_scores"), 1)
                probs_transposed(pe, st, "sdpa", headsT, pr, K.ident)
                pe.wait_ge(st("sdpa_probsT"), 2)
                for hd in range(HEADS16):
                    last = pe.matmul(o_mm[:, hd * HEAD16:(hd + 1) * HEAD16], prT[:, hd, :], v[:, hd * HEAD16:(hd + 1) * HEAD16],
                                     start=True, stop=True)
                last.then_inc(st("o_mm"), 1)
                pe.wait_ge(st("o"), 1)
                transposes(pe, oT_mm, o, K.ident, DC).then_inc(st("oT_mm"), 1)
                pe.wait_ge(st("oT"), 1)
                product(pe, s_of["p"], [(oT[:, c], W["pk"][:, c]) for c in range(DC)]).then_inc(st("p_scores"), 1)
                pe.wait_ge(st("p_probs"), 1)
                transposes(pe, t_of["p"], e["p"][:, 0], K.ident, DC).then_inc(st("p_probsT_mm"), 1)
                pe.wait_ge(st("p_probsT"), 1)
                product(pe, p_mm, [(eT["p"][:, c], W["pv"][:, c]) for c in range(DC)]).then_inc(st("p_mm"), 1)
                pe.wait_ge(st("ln2_done"), 1)
                transposes(pe, h2T_mm, h, K.ident, DC).then_inc(st("h2T_mm"), 1)
                pe.wait_ge(st("h2T"), 1)
                for j in range(2):
                    last = product(pe, f_sc[:, j * 512:(j + 1) * 512], [(hT[:, c], W["fk"][:, c, j * 512:(j + 1) * 512]) for c in range(DC)])
                last.then_inc(st("f_scores"), 1)
                pe.wait_ge(st("f_probs"), 1)
                transposes(pe, fT_mm, ef[:, 0], K.ident, 4 * DC).then_inc(st("f_probsT_mm"), 1)
                pe.wait_ge(st("f_probsT"), 1)
                product(pe, f_mm, [(efT[:, c], W["fv"][:, c]) for c in range(4 * DC)]).then_inc(st("f_mm"), 1)

            @block.vector
            def _(dve):
                link = linked(dve, st("vector_step"))
                norm_vector(dve, link, st, "ln0", K.x, xin[:, :], lnb[0])
                norm_vector(dve, link, st, "ln1", xin[:, :], h[:, :], lnb[1])
                dve.wait_ge(st("hT_mm"), 1)
                dve.tensor_copy(hT[:, :], hT_mm).then_inc(st("hT"), 1)
                for n in "kqv":
                    dve.wait_ge(st(f"{n}_scores"), 1)
                    softmax_vector(dve, link, st, n, s_of[n].unsqueeze(1), e[n][:, :], small[:, :, 0:1], 1.0)
                for n in "kqv":
                    dve.wait_ge(st(f"{n}_probsT_mm"), 1)
                    dve.tensor_copy(eT[n][:, :], t_of[n]).then_inc(st(f"{n}_probsT"), 1)
                dve.wait_ge(st("weights"), 16)
                dve.wait_ge(st("kT_mm"), 1)
                for c in range(DC):
                    last = dve.tensor_tensor(kblk[:, c], repeat(kT_mm[:, c], 8), spread(W0["head_mask"], P), ALU.mult)
                last.then_inc(st("kblk"), 1)
                dve.wait_ge(st("qT_mm"), 1)
                dve.tensor_copy(qT[:, :], qT_mm).then_inc(st("qT"), 1)
                dve.wait_ge(st("v_mm"), 1)
                dve.tensor_copy(v[:, :], v_mm).then_inc(st("v"), 1)
                dve.wait_ge(st("sdpa_scores"), 1)
                softmax_vector(dve, link, st, "sdpa", heads, pr[:, :], small[:, :, :], HEAD16 ** -0.5, mask=K.causal)
                dve.wait_ge(st("sdpa_probsT_mm"), 1)
                dve.tensor_copy(prT[:, 0:8], headsT[:, 0:8]).then_inc(st("sdpa_probsT"), 1)
                dve.tensor_copy(prT[:, 8:16], headsT[:, 8:16]).then_inc(st("sdpa_probsT"), 1)
                dve.wait_ge(st("o_mm"), 1)
                dve.tensor_copy(o[:, :], o_mm).then_inc(st("o"), 1)
                dve.wait_ge(st("oT_mm"), 1)
                dve.tensor_copy(oT[:, :], oT_mm).then_inc(st("oT"), 1)
                dve.wait_ge(st("p_scores"), 1)
                softmax_vector(dve, link, st, "p", s_of["p"].unsqueeze(1), e["p"][:, :], small[:, :, 0:1], 1.0)
                dve.wait_ge(st("p_probsT_mm"), 1)
                dve.tensor_copy(eT["p"][:, :], t_of["p"]).then_inc(st("p_probsT"), 1)
                dve.wait_ge(st("p_mm"), 1)
                link(dve.tensor_tensor(x2[:, :], p_mm, xin[:, :], ALU.add))
                norm_vector(dve, link, st, "ln2", x2[:, :], h[:, :], lnb[2])
                dve.wait_ge(st("h2T_mm"), 1)
                dve.tensor_copy(hT[:, :], h2T_mm).then_inc(st("h2T"), 1)
                dve.wait_ge(st("f_scores"), 1)
                softmax_vector(dve, link, st, "f", f_sc.unsqueeze(1), ef[:, :], small[:, :, 0:1], 1.0)
                dve.wait_ge(st("f_probsT_mm"), 1)
                dve.tensor_copy(efT[:, :], fT_mm).then_inc(st("f_probsT"), 1)
                link(dve.tensor_tensor(K.x, K.x, x2[:, :], ALU.add))
                residual_vector(dve, st, K.x, f_mm, "f_mm")



QFFN = 768
QC = QFFN // P
QUANT_SPEC = [("up", QC * D), ("gate", QC * D), ("down", DC * QFFN)]
QBLOCK = 32
QCOLS = 2 * QC * D + DC * QFFN
WQMAX, AQMAX, SIGQ = 7.0, 32767.0, 65536.0


def stage_quantised(nc, K, T):
    with Stage(nc, "quant") as st:
        wbuf, W = st.pack(nc, QUANT_SPEC)
        blocks = wbuf[:, :].rearrange("p (b k) -> p b k", k=QBLOCK)
        nb = QCOLS // QBLOCK
        bmax = st.sb("bmax", [P, nb])
        brec = st.sb("brec", [P, nb])
        upT = st.sb("upT", [P, DC, QFFN])
        gateT = st.sb("gateT", [P, DC, QFFN])
        downT = st.sb("downT", [P, QC, D])
        h = st.sb("h", [P, D])
        hT = st.sb("hT", [P, DC, P])
        up = st.sb("up", [P, QFFN])
        gate = st.sb("gate", [P, QFFN])
        sig = st.sb("sig", [P, QFFN])
        oT = st.sb("oT", [P, QC, P])
        small = st.sb("small", [P, 4])
        lnb = norm_buffers(st, "ln")
        tr = st.psum("tr", 2)
        tr4 = [tr[:, b * 512:(b + 1) * 512] for b in range(2)]
        mm_up, mm_gate = st.psum("mm_up", 2), st.psum("mm_gate", 2)
        oT_mm = st.psum("oT_mm", 2)
        up_n, gate_n = (W[n].rearrange("p (o i) -> p o i", i=D) for n in ("up", "gate"))
        down_n = W["down"].rearrange("p (o i) -> p o i", i=QFFN)
        lots = []
        for src, dst in ((up_n, upT), (gate_n, gateT)):
            for c in range(DC):
                for o in range(0, QC, 3):
                    lots.append(([src[:, o + j, c * P:(c + 1) * P] for j in range(3)], dst[:, c, o * P:(o + 3) * P]))
        for i in range(QC):
            lots.append(([down_n[:, o, i * P:(i + 1) * P] for o in range(DC)], downT[:, i, :]))

        with nc.Block() as block:
            @block.sync
            def _(sp):
                sp.dma_start(wbuf[:, :], T["w_quant"]).then_inc(st("weights"), 16)

            @block.scalar
            def _(act):
                norm_scalar(act, st, "ln", lnb)
                act.wait_ge(st("gate_ready"), 1)
                act.activation(sig[:, :], gate[:, :], ACT.Sigmoid).then_inc(st("sigmoid"), 1)

            @block.gpsimd
            def _(pool):
                for i in range(5):
                    pool.wait_ge(st("row_max"), i + 1)
                    pool.partition_all_reduce(small[:, 1:2], small[:, 0:1], P,
                                              bass.bass_isa.ReduceOp.max).then_inc(st("all_max"), 1)

            @block.tensor
            def _(pe):
                pe.wait_ge(st("weights_q"), 1)
                for n, (srcs, _) in enumerate(lots):
                    if n >= 2:
                        pe.wait_ge(st("lot_copied"), n - 1)
                    for j, src in enumerate(srcs):
                        last = pe.transpose(tr4[n % 2][:, j * P:(j + 1) * P], src, K.ident)
                    last.then_inc(st("lot_mm"), 1)
                pe.wait_ge(st("h_q"), 1)
                transposes(pe, oT_mm[:, 0:D].rearrange("p (c k) -> p c k", k=P), h, K.ident, DC).then_inc(st("hT_mm"), 1)
                pe.wait_ge(st("hT"), 1)
                pe.wait_ge(st("lot_copied"), len(lots))
                for mm, wT, done in ((mm_up, upT, "up_mm"), (mm_gate, gateT, "gate_mm")):
                    for a, b in ((0, 512), (512, QFFN)):
                        last = product(pe, mm[:, a:b], [(hT[:, c], wT[:, c, a:b]) for c in range(DC)])
                    last.then_inc(st(done), 1)
                pe.wait_ge(st("o_q"), 1)
                transposes(pe, oT_mm[:, 0:QFFN].rearrange("p (c k) -> p c k", k=P), up, K.ident, QC).then_inc(st("oT_mm"), 1)
                pe.wait_ge(st("oT"), 1)
                product(pe, mm_up[:, 0:D], [(oT[:, c], downT[:, c]) for c in range(QC)]).then_inc(st("y_mm"), 1)

            @block.vector
            def _(dve):
                link = linked(dve, st("vector_step"))

                def quantise(n, x, src, signal):
                    dve.tensor_reduce(small[:, 0:1], src, X_AXIS, ALU.max, apply_absolute_value=True).then_inc(st("row_max"), 1)
                    dve.wait_ge(st("all_max"), n + 1)
                    link(dve.tensor_scalar(small[:, 2:3], small[:, 1:2], 1.0 / AQMAX, 1e-12, ALU.mult, ALU.max))
                    link(dve.reciprocal(small[:, 3:4], small[:, 2:3]))
                    link(dve.tensor_scalar(x, src, small[:, 3:4], ROUND, ALU.mult, ALU.add))
                    link(dve.tensor_scalar(x, x, ROUND, AQMAX, ALU.subtract, ALU.min))
                    dve.tensor_scalar(x, x, -AQMAX - 1.0, small[:, 2:3], ALU.max, ALU.mult).then_inc(st(signal), 1)
                    dve.wait_ge(st(signal), 1)

                norm_vector(dve, link, st, "ln", K.x, h[:, :], lnb)
                dve.wait_ge(st("weights"), 16)
                link(dve.tensor_reduce(bmax[:, :], blocks, X_AXIS, ALU.max, apply_absolute_value=True))
                link(dve.tensor_scalar(bmax[:, :], bmax[:, :], 1.0 / WQMAX, 1e-12, ALU.mult, ALU.max))
                link(dve.reciprocal(brec[:, :], bmax[:, :]))
                link(dve.tensor_tensor(blocks, blocks, spread(brec[:, :], QBLOCK), ALU.mult))
                link(dve.tensor_scalar(wbuf[:, :], wbuf[:, :], ROUND, ROUND, ALU.add, ALU.subtract))
                link(dve.tensor_scalar(wbuf[:, :], wbuf[:, :], WQMAX, -WQMAX - 1.0, ALU.min, ALU.max))
                dve.tensor_tensor(blocks, blocks, spread(bmax[:, :], QBLOCK), ALU.mult).then_inc(st("weights_q"), 1)
                for n, (srcs, dst) in enumerate(lots):
                    dve.wait_ge(st("lot_mm"), n + 1)
                    dve.tensor_copy(dst, tr4[n % 2][:, 0:len(srcs) * P]).then_inc(st("lot_copied"), 1)
                quantise(0, h[:, :], h[:, :], "h_q")
                dve.wait_ge(st("hT_mm"), 1)
                dve.tensor_copy(hT[:, :], oT_mm[:, 0:D].rearrange("p (c k) -> p c k", k=P)).then_inc(st("hT"), 1)
                dve.wait_ge(st("gate_mm"), 1)
                quantise(1, gate[:, :], mm_gate[:, 0:QFFN], "gate_ready")
                dve.wait_ge(st("up_mm"), 1)
                quantise(2, up[:, :], mm_up[:, 0:QFFN], "up_q")
                dve.wait_ge(st("sigmoid"), 1)
                link(dve.tensor_scalar(sig[:, :], sig[:, :], SIGQ, ROUND, ALU.mult, ALU.add))
                link(dve.tensor_scalar(sig[:, :], sig[:, :], ROUND, 0.0, ALU.subtract, ALU.max))
                link(dve.tensor_scalar(sig[:, :], sig[:, :], SIGQ - 1.0, 1.0 / SIGQ, ALU.min, ALU.mult))
                link(dve.tensor_tensor(gate[:, :], gate[:, :], sig[:, :], ALU.mult))
                quantise(3, gate[:, :], gate[:, :], "gated_q")
                link(dve.tensor_tensor(up[:, :], up[:, :], gate[:, :], ALU.mult))
                quantise(4, up[:, :], up[:, :], "o_q")
                dve.wait_ge(st("oT_mm"), 1)
                dve.tensor_copy(oT[:, :], oT_mm[:, 0:QFFN].rearrange("p (c k) -> p c k", k=P)).then_inc(st("oT"), 1)
                residual_vector(dve, st, K.x, mm_up[:, 0:D], "y_mm")



class CtxAttention:
    def __init__(self, st, K, T, scale, qT, pad=None, load_rows=False):
        self.load_rows = load_rows
        self.st, self.K, self.T, self.scale, self.qT, self.pad = st, K, T, scale, qT, pad
        self.ctxT = st.sb("ctxT", [P, 2, DC, GROUP])
        self.e = st.sb("e", [P, 2, GROUP])
        self.eT = st.sb("eT", [P, 2, TILE, P])
        self.acc = st.sb("acc", [P, D + 1])
        self.run = st.sb("run", [P, 2, 8])
        scores = st.psum("scores", 4)
        self.sc = [scores[:, b * 1024:b * 1024 + GROUP] for b in range(2)]
        self.turned = st.psum("turned", 2)
        self.eT_mm = self.turned[:, 0:GROUP].rearrange("p (t k) -> p t k", k=P)
        self.at = st.psum("attended", 1)[:, 0:D]

    def sync(self, sp):
        st = self.st

        def load(i, b, first=False):
            group = i * 2 + b
            if not first:
                group, done = sp.snap(i * 2 + b), sp.snap(i + 0)
                sp.wait_ge(st(f"scored{b}"), done)
            sp.dma_start(self.ctxT[:, b], self.T["ctxT"][bass.ds(group, 1)].rearrange("o p c m -> p (o c) m")
                         ).then_inc(st(f"ctxT_in{b}"), 16)
            if self.load_rows:
                tile = i * (2 * TILE) + b * TILE
                if not first:
                    tile, before = sp.snap(tile), sp.snap(i * 16)
                    sp.wait_ge(st(f"rows_in{b}"), before)
                sp.dma_start(self.K.ctx[:, bass.ds(tile, TILE), 0:D], self.T["ctx_rows"][bass.ds(group, 1)].rearrange("o p t d -> p (o t) d")
                             ).then_inc(st(f"rows_in{b}"), 16)
        load(0, 0, first=True)
        load(0, 1, first=True)
        with sp.Fori(1, GROUPS // 2) as i:
            load(i, 0)
            load(i, 1)

    def tensor(self, pe):
        st, K = self.st, self.K
        ctxT, e, eT = self.ctxT, self.e, self.eT

        def score(i, b, first=False):
            pe.wait_ge(st(f"ctxT_in{b}"), i * 16 + 16)
            if not first:
                pe.wait_ge(st(f"exp{b}"), i)
            for lo, hi in ((0, KEYS_A), (KEYS_A, GROUP)):
                last = product(pe, self.sc[b][:, lo:hi], [(self.qT[:, c], ctxT[:, b, c, lo:hi]) for c in range(DC)])
            last.then_inc(st(f"scored{b}"), 1)

        def turn(i, b, first=False):
            pe.wait_ge(st(f"exp{b}"), i + 1)
            if not first:
                pe.wait_ge(st("turned"), i * 4 + 2 * b)
            for t in range(TILE):
                last = pe.transpose(self.eT_mm[:, t], e[:, b, t * P:(t + 1) * P], K.ident)
            last.then_inc(st("turned_mm"), 1)

        def attend(i, b, first=False):
            if self.load_rows:
                pe.wait_ge(st(f"rows_in{b}"), i * 16 + 16)
            pe.wait_ge(st("turned"), i * 4 + 2 * b + 2)
            if not first:
                pe.wait_ge(st("added"), i * 2 + b)
            for t in range(TILE):
                last = pe.matmul(self.at.unsqueeze(1), eT[:, b, t], K.ctx[:, bass.ds(i * (2 * TILE) + b * TILE + t, 1), 0:D],
                                 start=t == 0, stop=t == TILE - 1)
            last.then_inc(st("attended"), 1)

        score(0, 0, first=True)
        score(0, 1, first=True)
        turn(0, 0, first=True)
        attend(0, 0, first=True)
        with pe.Fori(1, GROUPS // 2) as i:
            score(i, 0)
            turn(i - 1, 1)
            attend(i - 1, 1)
            score(i, 1)
            turn(i, 0)
            attend(i, 0)
        turn(GROUPS // 2 - 1, 1)
        attend(GROUPS // 2 - 1, 1)

    def scalar(self, act):
        st = self.st

        def exponentials(i, b, first=False):
            act.wait_ge(st("shift"), i * 2 + b + 1)
            src = self.sc[b] if self.pad is None else self.e[:, b]
            if not first:
                act.wait_ge(st("turned_mm"), i * 2 + b - 1)
            run = self.run[:, b]
            act.activation(self.e[:, b], src, ACT.Exp, bias=run[:, 1:2], scale=self.scale if self.pad is None else 1.0,
                           accum_out=run[:, 4:5]).then_inc(st(f"exp{b}"), 1)
            act.activation(run[:, 3:4], run[:, 2:3], ACT.Exp).then_inc(st("decay"), 1)

        def turned(i, b):
            act.wait_ge(st("turned_mm"), i * 2 + b + 1)
            act.copy(self.eT[:, b, 4:TILE], self.eT_mm[:, 4:TILE]).then_inc(st("turned"), 1)

        exponentials(0, 0, first=True)
        turned(0, 0)
        exponentials(0, 1, first=True)
        with act.Fori(1, GROUPS // 2) as i:
            turned(i - 1, 1)
            exponentials(i, 0)
            turned(i, 0)
            exponentials(i, 1)
        turned(GROUPS // 2 - 1, 1)

    def vector(self, dve):
        st, acc, run = self.st, self.acc, self.run
        sem, count = st("flash_step"), [0]
        limit = scale_of_max = -1.0 if self.pad is not None else -self.scale

        def maximum(i, b, first=False):
            n = (i * 2 + b) * STEPS
            new, old = run[:, b], run[:, 1 - b]
            dve.wait_ge(st(f"scored{b}"), i + 1)
            if not first:
                dve.wait_ge(st("added"), i * 2 + b - 1)
            src = self.sc[b]
            if self.pad is not None:
                keypos, start = self.pad
                if not first:
                    dve.wait_ge(st(f"exp{b}"), i)
                dve.tensor_scalar(self.e[:, b], keypos, start[:, 0:1], -1e13, ALU.is_ge, ALU.mult).then_inc(sem, 1)
                dve.wait_ge(sem, n + 1)
                dve.scalar_tensor_tensor(out=self.e[:, b], in0=src, scalar=self.scale, in1=self.e[:, b],
                                         op0=ALU.mult, op1=ALU.add).then_inc(sem, 1)
                dve.wait_ge(sem, n + 2)
                dve.tensor_scalar(start, start, float(GROUP), None, ALU.subtract).then_inc(sem, 1)
                src = self.e[:, b]
                n = n + 3
            dve.tensor_reduce(new[:, 5:6], src, X_AXIS, ALU.max).then_inc(sem, 1)
            dve.wait_ge(sem, n + 1)
            if first and b == 0:
                dve.tensor_copy(new[:, 0:1], new[:, 5:6]).then_inc(sem, 1)
                dve.wait_ge(sem, n + 2)
                dve.memset(new[:, 2:3], 0.0).then_inc(sem, 1)
            else:
                dve.tensor_tensor(new[:, 0:1], new[:, 5:6], old[:, 0:1], ALU.max).then_inc(sem, 1)
                dve.wait_ge(sem, n + 2)
                dve.tensor_scalar(new[:, 2:3], old[:, 0:1], new[:, 0:1], -scale_of_max, ALU.subtract, ALU.mult).then_inc(sem, 1)
            dve.wait_ge(sem, n + 3)
            dve.tensor_scalar(new[:, 1:2], new[:, 0:1], scale_of_max, None, ALU.mult).then_inc(st("shift"), 1)

        def turned(i, b):
            dve.wait_ge(st("turned_mm"), i * 2 + b + 1)
            dve.tensor_copy(self.eT[:, b, 0:4], self.eT_mm[:, 0:4]).then_inc(st("turned"), 1)

        def add(i, b):
            dve.wait_ge(st("decay"), i * 2 + b + 1)
            dve.wait_ge(st("attended"), i * 2 + b + 1)
            dve.scalar_tensor_tensor(out=acc[:, D:D + 1], in0=acc[:, D:D + 1], scalar=run[:, b, 3:4], in1=run[:, b, 4:5],
                                     op0=ALU.mult, op1=ALU.add).then_inc(st("added_sum"), 1)
            dve.scalar_tensor_tensor(out=acc[:, 0:D], in0=acc[:, 0:D], scalar=run[:, b, 3:4], in1=self.at,
                                     op0=ALU.mult, op1=ALU.add).then_inc(st("added"), 1)
            dve.wait_ge(st("added_sum"), i * 2 + b + 1)
            dve.wait_ge(st("added"), i * 2 + b + 1)

        STEPS = 3 if self.pad is None else 6
        dve.memset(acc[:, :], 0.0).then_inc(st("acc_zero"), 1)
        dve.wait_ge(st("acc_zero"), 1)
        maximum(0, 0, first=True)
        dve.wait_ge(st("shift"), 1)
        turned(0, 0)
        maximum(0, 1, first=True)
        dve.wait_ge(st("shift"), 2)
        add(0, 0)
        with dve.Fori(1, GROUPS // 2) as i:
            turned(i - 1, 1)
            maximum(i, 0)
            dve.wait_ge(st("shift"), i * 2 + 1)
            add(i - 1, 1)
            turned(i, 0)
            maximum(i, 1)
            dve.wait_ge(st("shift"), i * 2 + 2)
            add(i, 0)
        turned(GROUPS // 2 - 1, 1)
        add(GROUPS // 2 - 1, 1)
        dve.reciprocal(run[:, 0, 6:7], acc[:, D:D + 1]).then_inc(st("rsum"), 1)
        dve.wait_ge(st("rsum"), 1)
        dve.tensor_scalar(acc[:, 0:D], acc[:, 0:D], run[:, 0, 6:7], None, ALU.mult).then_inc(st("pooled"), 1)
        dve.wait_ge(st("pooled"), 1)



PADDED_SPEC = [("w", DC * D), ("b", D), ("keypos", GROUP), ("qpos", 1)]


def stage_padded_xattn(nc, K, T):
    with Stage(nc, "padded") as st:
        wbuf, W = st.pack(nc, PADDED_SPEC)
        w = chunks(W["w"], D)
        h = st.sb("h", [P, D])
        hT = st.sb("hT", [P, DC, P])
        pads_int = st.sb("pads_int", [P, 1], I32)
        start = st.sb("start", [P, 4])
        oT = st.sb("oT", [P, DC, P])
        lnb = norm_buffers(st, "ln")
        flash = CtxAttention(st, K, T, D ** -0.5, hT, pad=(W["keypos"], start[:, 0:1]))
        mm = st.psum("mm", 1)
        mmT = mm[:, 0:D].rearrange("p (c k) -> p c k", k=P)
        with nc.Block() as block:
            @block.sync
            def _(sp):
                sp.dma_start(pads_int[:, :], T["lens"]).then_inc(st("pads_in"), 16)
                sp.dma_start(wbuf[:, :], T["w_padded"]).then_inc(st("weights"), 16)
                flash.sync(sp)

            @block.scalar
            def _(act):
                norm_scalar(act, st, "ln", lnb)
                flash.scalar(act)

            @block.tensor
            def _(pe):
                pe.wait_ge(st("ln_done"), 1)
                transposes(pe, mmT, h, K.ident, DC).then_inc(st("hT_mm"), 1)
                pe.wait_ge(st("hT"), 1)
                flash.tensor(pe)
                pe.wait_ge(st("pooled"), 1)
                transposes(pe, mmT, flash.acc, K.ident, DC).then_inc(st("oT_mm"), 1)
                pe.wait_ge(st("weights"), 16)
                pe.wait_ge(st("oT"), 1)
                product(pe, mm[:, D:2 * D], [(oT[:, c], w[:, c]) for c in range(DC)]).then_inc(st("y_mm"), 1)

            @block.vector
            def _(dve):
                link = linked(dve, st("vector_step"))
                norm_vector(dve, link, st, "ln", K.x, h[:, :], lnb)
                dve.wait_ge(st("hT_mm"), 1)
                dve.tensor_copy(hT[:, :], mmT).then_inc(st("hT"), 1)
                dve.wait_ge(st("hT"), 1)
                dve.wait_ge(st("pads_in"), 16)
                dve.wait_ge(st("weights"), 16)
                link(dve.tensor_copy(start[:, 1:2], pads_int[:, :]))
                link(dve.tensor_tensor(start[:, 2:3], W["qpos"], start[:, 1:2], ALU.is_lt))
                link(dve.scalar_tensor_tensor(out=start[:, 0:1], in0=start[:, 2:3], scalar=float(2 * CTX), in1=start[:, 1:2],
                                              op0=ALU.mult, op1=ALU.add))
                flash.vector(dve)
                dve.wait_ge(st("oT_mm"), 1)
                dve.tensor_copy(oT[:, :], mmT).then_inc(st("oT"), 1)
                link(dve.tensor_tensor(K.x, K.x, W["b"], ALU.add))
                residual_vector(dve, st, K.x, mm[:, D:2 * D], "y_mm")



def stage_plain_xattn(nc, K, T):
    with Stage(nc, "plain") as st:
        h = st.sb("h", [P, D])
        hT = st.sb("hT", [P, DC, P])
        lnb = norm_buffers(st, "ln")
        flash = CtxAttention(st, K, T, 1.0, hT, load_rows=True)
        mm = st.psum("mm", 1)
        mmT = mm[:, 0:D].rearrange("p (c k) -> p c k", k=P)
        with nc.Block() as block:
            @block.sync
            def _(sp):
                flash.sync(sp)

            @block.scalar
            def _(act):
                norm_scalar(act, st, "ln", lnb)
                flash.scalar(act)

            @block.tensor
            def _(pe):
                pe.wait_ge(st("ln_done"), 1)
                transposes(pe, mmT, h, K.ident, DC).then_inc(st("hT_mm"), 1)
                pe.wait_ge(st("hT"), 1)
                flash.tensor(pe)

            @block.vector
            def _(dve):
                link = linked(dve, st("vector_step"))
                norm_vector(dve, link, st, "ln", K.x, h[:, :], lnb)
                dve.wait_ge(st("hT_mm"), 1)
                dve.tensor_copy(hT[:, :], mmT).then_inc(st("hT"), 1)
                dve.wait_ge(st("hT"), 1)
                flash.vector(dve)
                residual_vector(dve, st, K.x, flash.acc[:, 0:D], "pooled")



FOLD_SPEC = [("wqkv", DC * 3 * D), ("bqkv", 3 * D), ("wo", DC * D), ("bo", D), ("head_mask", 8)]


def stage_folded_attention(nc, K, T):
    with Stage(nc, "folded") as st:
        wbuf, W = st.pack(nc, FOLD_SPEC)
        wqkv, wo = chunks(W["wqkv"], 3 * D), chunks(W["wo"], D)
        h = st.sb("h", [P, D])
        hT = st.sb("hT", [P, DC, P])
        qkv = st.sb("qkv", [P, 3 * D])
        folded = st.sb("folded", [P, HEADS16, 3, HEAD16])
        q = st.sb("q", [P, 3, D])
        qT = st.sb("qT", [P, DC, P])
        kblk = st.sb("kblk", [P, DC, 8, P])
        pr = st.sb("pr", [P, HEADS16, P])
        prT = kblk[:, :].rearrange("p c h k -> p (c h) k")
        o = st.sb("o", [P, D])
        o2 = st.sb("o2", [P, D])
        oT = st.sb("oT", [P, DC, P])
        small = st.sb("small", [P, 2, 16])
        lnb = norm_buffers(st, "ln")
        sc = st.psum("scores", 4)
        mm = st.psum("mm", 4)
        heads = sc[:, :].rearrange("p (h k) -> p h k", k=P)
        headsT = mm[:, :].rearrange("p (h k) -> p h k", k=P)
        T_mm = mm[:, 1024:1536].rearrange("p (a c k) -> p a c k", a=2, k=P)
        o_mm = sc[:, 0:D]
        oT_mm = sc[:, 512:512 + D].rearrange("p (c k) -> p c k", k=P)
        y_mm = sc[:, 1024:1024 + D]
        qkv_heads = T["fold_qkv"].rearrange("t c -> (t c)").rearrange("(h s c) -> s h c", h=HEADS16, s=P)
        o_heads = T["fold_o"].rearrange("t c -> (t c)").rearrange("(h s c) -> s h c", h=HEADS16, s=P)

        with nc.Block() as block:
            @block.sync
            def _(sp):
                sp.dma_start(wbuf[:, :], T["w_fold"]).then_inc(st("weights"), 16)
                sp.wait_ge(st("qkv"), 1)
                sp.dma_start(T["fold_qkv"], qkv[:, :]).then_inc(st("qkv_out"), 16)
                sp.wait_ge(st("qkv_out"), 16)
                sp.dma_start(folded[:, :].rearrange("p h a d -> p h (a d)"), qkv_heads).then_inc(st("folded_in"), 16)
                sp.wait_ge(st("o"), 1)
                sp.dma_start(o_heads, o[:, :].rearrange("p (h d) -> p h d", d=HEAD16)).then_inc(st("o_out"), 16)
                sp.wait_ge(st("o_out"), 16)
                sp.dma_start(o2[:, :], T["fold_o"]).then_inc(st("o2_in"), 16)

            @block.scalar
            def _(act):
                norm_scalar(act, st, "ln", lnb)
                softmax_scalar(act, st, "sdpa", pr[:, :], HEAD16 ** -0.5)
                act.wait_ge(st("sdpa_probsT_mm"), 1)
                act.copy(prT[:, 8:16], headsT[:, 8:16]).then_inc(st("sdpa_probsT"), 1)

            @block.tensor
            def _(pe):
                pe.wait_ge(st("ln_done"), 1)
                transposes(pe, T_mm[:, 0], h, K.ident, DC).then_inc(st("hT_mm"), 1)
                pe.wait_ge(st("weights"), 16)
                pe.wait_ge(st("hT"), 1)
                for lo, hi in ((0, 512), (512, 3 * D)):
                    last = product(pe, mm[:, lo:hi], [(hT[:, c], wqkv[:, c, lo:hi]) for c in range(DC)])
                last.then_inc(st("qkv_mm"), 1)
                pe.wait_ge(st("q"), 1)
                for a in range(2):
                    last = transposes(pe, T_mm[:, a], q[:, a], K.ident, DC)
                last.then_inc(st("qkT_mm"), 1)
                pe.wait_ge(st("kblk"), 1)
                for c in range(DC):
                    for j in range(2):
                        last = pe.matmul(heads[:, 8 * c + 4 * j:8 * c + 4 * j + 4, :], qT[:, c], kblk[:, c, 4 * j:4 * j + 4, :],
                                         start=True, stop=True)
                last.then_inc(st("sdpa_scores"), 1)
                probs_transposed(pe, st, "sdpa", headsT, pr, K.ident)
                pe.wait_ge(st("sdpa_probsT"), 2)
                for hd in range(HEADS16):
                    last = pe.matmul(o_mm[:, hd * HEAD16:(hd + 1) * HEAD16], prT[:, hd, :], q[:, 2, hd * HEAD16:(hd + 1) * HEAD16],
                                     start=True, stop=True)
                last.then_inc(st("o_mm"), 1)
                pe.wait_ge(st("o2_in"), 16)
                transposes(pe, oT_mm, o2, K.ident, DC).then_inc(st("oT_mm"), 1)
                pe.wait_ge(st("oT"), 1)
                product(pe, y_mm, [(oT[:, c], wo[:, c]) for c in range(DC)]).then_inc(st("y_mm"), 1)

            @block.vector
            def _(dve):
                link = linked(dve, st("vector_step"))
                norm_vector(dve, link, st, "ln", K.x, h[:, :], lnb)
                dve.wait_ge(st("hT_mm"), 1)
                dve.tensor_copy(hT[:, :], T_mm[:, 0]).then_inc(st("hT"), 1)
                dve.wait_ge(st("weights"), 16)
                dve.wait_ge(st("qkv_mm"), 1)
                dve.tensor_tensor(qkv[:, :], mm[:, 0:3 * D], W["bqkv"], ALU.add).then_inc(st("qkv"), 1)
                dve.wait_ge(st("folded_in"), 16)
                dve.tensor_copy(q[:, :].rearrange("p a (h d) -> p h a d", d=HEAD16), folded[:, :]).then_inc(st("q"), 1)
                dve.wait_ge(st("qkT_mm"), 1)
                link(dve.tensor_copy(qT[:, :], T_mm[:, 0]))
                for c in range(DC):
                    last = dve.tensor_tensor(kblk[:, c], repeat(T_mm[:, 1, c], 8), spread(W["head_mask"], P), ALU.mult)
                last.then_inc(st("kblk"), 1)
                dve.wait_ge(st("sdpa_scores"), 1)
                softmax_vector(dve, link, st, "sdpa", heads, pr[:, :], small[:, :, :], 1.0)
                dve.wait_ge(st("sdpa_probsT_mm"), 1)
                dve.tensor_copy(prT[:, 0:8], headsT[:, 0:8]).then_inc(st("sdpa_probsT"), 1)
                dve.wait_ge(st("o_mm"), 1)
                dve.tensor_copy(o[:, :], o_mm).then_inc(st("o"), 1)
                dve.wait_ge(st("oT_mm"), 1)
                dve.tensor_copy(oT[:, :], oT_mm).then_inc(st("oT"), 1)
                link(dve.tensor_tensor(K.x, K.x, W["bo"], ALU.add))
                residual_vector(dve, st, K.x, y_mm, "y_mm")



EXPERTS, PLACES, WIDE = 16, P // 16, 1024
FC = WIDE // P
MOE_SPEC = [("wg", DC * EXPERTS), ("places", PLACES)]


RING = 4


def stage_experts(nc, K, T):
    with Stage(nc, "moe") as st:
        wbuf, W = st.pack(nc, MOE_SPEC)
        wg = chunks(W["wg"], EXPERTS)
        w1 = st.sb("w1", [P, RING, DC, WIDE])
        w2 = st.sb("w2", [P, RING, FC, D])
        h = st.sb("h", [P, D])
        hT = st.sb("hT", [P, DC, P])
        g = st.sb("g", [P, EXPERTS])
        best = st.sb("best", [P, EXPERTS])
        seen = st.sb("seen", [P, EXPERTS])
        zero = st.sb("zero", [P, EXPERTS])
        small = st.sb("small", [P, 8])
        send = st.sb("send", [P, EXPERTS, PLACES])
        sendT = st.sb("sendT", [PLACES, EXPERTS, P])
        here = st.sb("here", [P, PLACES])
        xT = st.sb("xT", [P, DC, P + PLACES])
        mine = st.sb("mine", [P, 2, DC, PLACES])
        hidden = st.sb("hidden", [PLACES, 2, WIDE])
        hiddenT = st.sb("hiddenT", [P, 2, FC, PLACES])
        result = st.sb("result", [PLACES, 2, D])
        back = st.sb("back", [PLACES, 2, P])
        lnb = norm_buffers(st, "ln")
        mm, mm2 = st.psum("mm", 1), st.psum("mm2", 1)
        mmT = mm[:, 0:D].rearrange("p (c k) -> p c k", k=P)
        hid_all = st.psum("hid", 4)
        hid = [hid_all[0:PLACES, n * WIDE:(n + 1) * WIDE] for n in range(2)]
        turned = mm2[:, 0:FC * PLACES].rearrange("p (f s) -> p f s", s=PLACES)
        res = [mm[0:PLACES, 0:D], st.psum("res", 1)[0:PLACES, 0:D]]
        y_mm = st.psum("y", 1)[:, 0:D]

        def all_experts(eng, body):
            for b in range(RING):
                body(b, b)
            with eng.Fori(1, EXPERTS // RING) as i:
                for b in range(RING):
                    body(i * RING + b, b)

        with nc.Block() as block:
            @block.sync
            def _(sp):
                sp.dma_start(wbuf[:, :], T["w_moe"]).then_inc(st("weights"), 16)

                def load(e, b):
                    at = e
                    if not isinstance(e, int):
                        at, done = sp.snap(e), sp.snap(e - RING + 1)
                        sp.wait_ge(st("hid_mm"), done)
                    sp.dma_start(w1[:, b], T["moe_w1"][bass.ds(at, 1)].rearrange("o (c p) f -> p (o c) f", p=P)
                                 ).then_inc(st(f"w1_in{b}"), 16)
                    if not isinstance(e, int):
                        sp.wait_ge(st("res_mm"), done)
                    sp.dma_start(w2[:, b], T["moe_w2"][bass.ds(at, 1)].rearrange("o (c p) f -> p (o c) f", p=P)
                                 ).then_inc(st(f"w2_in{b}"), 16)
                all_experts(sp, load)

            @block.scalar
            def _(act):
                norm_scalar(act, st, "ln", lnb)
                act.wait_ge(st("shifted"), 1)
                act.activation(g[:, :], g[:, :], ACT.Exp, accum_out=small[:, 1:2]).then_inc(st("exp"), 1)

            @block.tensor
            def _(pe):
                pe.wait_ge(st("ln_done"), 1)
                transposes(pe, mmT, h, K.ident, DC).then_inc(st("hT_mm"), 1)
                pe.wait_ge(st("weights"), 16)
                pe.wait_ge(st("hT"), 1)
                product(pe, mm2[:, 0:EXPERTS], [(hT[:, c], wg[:, c]) for c in range(DC)]).then_inc(st("gate_mm"), 1)
                pe.wait_ge(st("best"), 1)
                pe.matmul(y_mm[:, 0:EXPERTS], K.before, best[:, :], start=True, stop=True).then_inc(st("before_mm"), 1)
                pe.wait_ge(st("send"), 1)
                for c in range(DC):
                    pe.matmul(mmT[:, c], h[:, c * P:(c + 1) * P], send[:, :].rearrange("p e s -> p (e s)"), start=True, stop=True)
                for e in range(EXPERTS):
                    last = pe.transpose(hid_all[0:PLACES, e * P:(e + 1) * P], send[:, e], K.ident)
                last.then_inc(st("sent_mm"), 1)
                pe.wait_ge(st("xT"), 1)

                def hide(b, half, c):
                    cols = slice(half * PSUM_BANK, (half + 1) * PSUM_BANK)
                    return pe.matmul(hid[b % 2][:, cols], mine[:, b % 2, c], w1[:, b, c, cols], start=c == 0, stop=c == DC - 1)

                def await_turn(e):
                    pe.wait_ge(st("hidden"), e + 1)
                    await_count(pe, st("hiddenT"), e)

                def turn(b):
                    for f in range(FC):
                        last = pe.transpose(turned[:, f], hidden[:, b % 2, f * P:(f + 1) * P], K.ident[0:PLACES, 0:PLACES])
                    last.then_inc(st("turned_mm"), 1)

                def narrow(e, b, i):
                    pe.wait_ge(st(f"w2_in{b}"), i * 16 + 16)
                    pe.wait_ge(st("hiddenT"), e + 1)
                    await_count(pe, st("result"), e - 1)
                    product(pe, res[b % 2], [(hiddenT[:, b % 2, f], w2[:, b, f]) for f in range(FC)]).then_inc(st("res_mm"), 1)

                def scatter(e, b):
                    pe.wait_ge(st("result"), e + 1)
                    pe.wait_ge(st("back"), e + 1)
                    pe.matmul(y_mm, back[:, b % 2], result[:, b % 2], start=isinstance(e, int) and e == 0,
                              stop=isinstance(e, int) and e == EXPERTS - 1, skip_group_check=True).then_inc(st("scattered"), 1)

                def step(i, b):
                    e = i * RING + b
                    before = (i, b - 1) if b else (i - 1, RING - 1)
                    pe.wait_ge(st(f"w1_in{b}"), i * 16 + 16)
                    pe.wait_ge(st("mine"), e + 1)
                    await_count(pe, st("hidden"), e - 1)
                    hide(b, 0, 0)
                    hide(b, 0, 1)
                    some = not (isinstance(i, int) and e == 0)
                    if some:
                        await_turn(before[0] * RING + before[1])
                    hide(b, 1, 0)
                    if some:
                        turn(before[1])
                    hide(b, 1, 1).then_inc(st("hid_mm"), 1)
                    if not (isinstance(i, int) and e < 2):
                        two = (i, b - 2) if b > 1 else (i - 1, RING + b - 2)
                        scatter(two[0] * RING + two[1], two[1])
                    if some:
                        narrow(before[0] * RING + before[1], before[1], before[0])

                for b in range(RING):
                    step(0, b)
                with pe.Fori(1, EXPERTS // RING) as i:
                    for b in range(RING):
                        step(i, b)
                await_turn(EXPERTS - 1)
                turn(RING - 1)
                scatter(EXPERTS - 2, RING - 2)
                narrow(EXPERTS - 1, RING - 1, EXPERTS // RING - 1)
                scatter(EXPERTS - 1, RING - 1)

            @block.vector
            def _(dve):
                link = linked(dve, st("vector_step"))
                norm_vector(dve, link, st, "ln", K.x, h[:, :], lnb)
                dve.wait_ge(st("hT_mm"), 1)
                dve.tensor_copy(hT[:, :], mmT).then_inc(st("hT"), 1)
                link(dve.memset(zero[:, :], 0.0))
                link(dve.memset(xT[:, :, P:], 0.0))
                dve.wait_ge(st("gate_mm"), 1)
                link(dve.tensor_reduce(small[:, 0:1], mm2[:, 0:EXPERTS], X_AXIS, ALU.max))
                dve.tensor_scalar(g[:, :], mm2[:, 0:EXPERTS], small[:, 0:1], None, ALU.subtract).then_inc(st("shifted"), 1)
                dve.wait_ge(st("exp"), 1)
                link(dve.reciprocal(small[:, 2:3], small[:, 1:2]))
                link(dve.tensor_scalar(g[:, :], g[:, :], small[:, 2:3], None, ALU.mult))
                link(dve.tensor_reduce(small[:, 3:4], g[:, :], X_AXIS, ALU.max))
                link(dve.tensor_scalar(best[:, :], g[:, :], small[:, 3:4], None, ALU.is_equal))
                link(dve.tensor_tensor_scan(seen[:, :], best[:, :], zero[:, :], 0.0, ALU.add, ALU.add))
                dve.scalar_tensor_tensor(out=best[:, :], in0=seen[:, :], scalar=1.0, in1=best[:, :],
                                         op0=ALU.is_equal, op1=ALU.mult).then_inc(st("best"), 1)
                dve.wait_ge(st("before_mm"), 1)
                link(dve.tensor_tensor(seen[:, :], y_mm[:, 0:EXPERTS], best[:, :], ALU.mult))
                link(dve.tensor_reduce(small[:, 4:5], seen[:, :], X_AXIS, ALU.add))
                dve.wait_ge(st("weights"), 16)
                link(dve.tensor_scalar(here[:, :], W["places"], small[:, 4:5], None, ALU.is_equal))
                dve.tensor_tensor(send[:, :], spread(best[:, :], PLACES), repeat(here[:, :], EXPERTS), ALU.mult).then_inc(st("send"), 1)
                dve.wait_ge(st("sent_mm"), 1)
                link(dve.tensor_copy(xT[:, :, 0:P], mmT))
                dve.tensor_copy(mine[:, 0], xT[:, :, 0:PLACES]).then_inc(st("mine"), 1)
                dve.tensor_copy(sendT[:, :], hid_all[0:PLACES, :].rearrange("p (e k) -> p e k", k=P)).then_inc(st("xT"), 1)
                dve.wait_ge(st("xT"), 1)

                def step(e, b):
                    n = b % 2
                    await_count(dve, st("hid_mm"), e)
                    dve.tensor_copy(mine[:, 1 - n], xT[:, :, bass.ds((e + 1) * PLACES, PLACES)]).then_inc(st("mine"), 1)
                    await_count(dve, st("scattered"), e - 1)
                    dve.tensor_copy(back[:, n], sendT[:, bass.ds(e, 1)].rearrange("p o k -> p (o k)")).then_inc(st("back"), 1)
                    await_count(dve, st("turned_mm"), e - 1)
                    dve.wait_ge(st("hid_mm"), e + 1)
                    dve.tensor_scalar(hidden[:, n], hid[n], 0.0, None, ALU.max).then_inc(st("hidden"), 1)
                    if not (isinstance(e, int) and e == 0):
                        dve.wait_ge(st("res_mm"), e)
                        dve.tensor_copy(result[:, 1 - n], res[1 - n]).then_inc(st("result"), 1)
                    dve.wait_ge(st("turned_mm"), e + 1)
                    dve.tensor_copy(hiddenT[:, n], turned).then_inc(st("hiddenT"), 1)

                all_experts(dve, step)
                dve.wait_ge(st("res_mm"), EXPERTS)
                dve.tensor_copy(result[:, 1], res[1]).then_inc(st("result"), 1)
                dve.wait_ge(st("scattered"), EXPERTS)
                dve.scalar_tensor_tensor(out=K.x, in0=y_mm, scalar=small[:, 3:4], in1=K.x,
                                         op0=ALU.mult, op1=ALU.add).then_inc(st("residual"), 1)
                dve.wait_ge(st("residual"), 1)



CROSS_SPEC = [("wq", DC * D), ("wk", DC * D), ("wv", DC * D), ("wo", DC * D), ("head_mask", 8)]
PAIRS16 = HEADS16 // 2
HALF_KEYS = GROUP // 2


def top_half(ap):
    return ap.bitcast(BF16)[..., 1::2]


def other(par):
    return 1 - par if isinstance(par, int) else (par + 1) % 2


STORES = (2, 6)


def stage_cross_heads(nc, K, T):
    with Stage(nc, "cross") as st:
        wbuf, W = st.pack(nc, CROSS_SPEC)
        wq, wk, wv, wo = (chunks(W[n], D) for n in ("wq", "wk", "wv", "wo"))
        ctxT = st.sb("ctxT", [P, DC, GROUP])
        mask_int = st.sb("mask_int", [P, GROUP], I32)
        mask = st.sb("mask", [P, GROUP])
        keysT = st.sb("keysT", [P, 2 * DC, GROUP])
        values = st.sb("values", [P, 2 * TILE, HEADS16, 3, HEAD16 + 1])
        h = st.sb("h", [P, D])
        hT = st.sb("hT", [P, DC, P])
        qblk = st.sb("qblk", [P, DC, 8, P])
        s = st.sb("s", [P, 2, 2, GROUP])
        eT = st.sb("eT", [P, 2, 2, TILE, P])
        rest = st.sb("rest", [P, 2, 2, TILE, P])
        third = st.sb("third", [P, 2, 2, TILE, P], BF16)
        acc = st.sb("acc", [P, HEADS16, HEAD16 + 1])
        new = st.sb("new", [P, 2, HEAD16 + 1])
        top = st.sb("top", [P, HEADS16])
        run = st.sb("run", [P, PAIRS16, 5, 2])
        o = st.sb("o", [P, D])
        oT = st.sb("oT", [P, DC, P])
        rsum = st.sb("rsum", [P, HEADS16])
        marks = st.sb("marks", [P, HEADS16])
        lnb = norm_buffers(st, "ln")
        sc = st.psum("scores", 4)
        turned = st.psum("turned", 2)[:, 0:GROUP].rearrange("p (t k) -> p t k", k=P)
        mm = st.psum("mm", 1)
        attended = [bank[:, 0:6 * (HEAD16 + 1)].rearrange("p (a s d) -> p a s d", a=2, s=3)
                    for bank in (st.psum("attended", 1), mm)]
        mmT = mm[:, 0:D].rearrange("p (c k) -> p c k", k=P)
        SCALE = HEAD16 ** -0.5

        def scores(a):
            return sc[:, a * 1024:a * 1024 + GROUP]

        def key_piece(p, par):
            c, half = p // 2, (p % 2) * HALF_KEYS
            return (sc[:, p * 512:p * 512 + HALF_KEYS].unsqueeze(1),
                    keysT[:, bass.ds(par * DC + c, 1), half:half + HALF_KEYS])

        def value_piece(p, par):
            n = min(2, TILE - 2 * p)
            return (sc[:, p * 512:p * 512 + n * D].rearrange("p (t h d) -> p t h d", t=n, d=HEAD16),
                    values[:, bass.ds(par * TILE + 2 * p, n), :, 0, 0:HEAD16])

        def all_groups(eng, body):
            body(0, 0, True, False)
            with eng.Fori(1, GROUPS - 1) as g:
                body(g, eng.snap(g % 2), False, False)
            body(GROUPS - 1, (GROUPS - 1) % 2, False, True)

        with nc.Block() as block:
            @block.sync
            def _(sp):
                sp.dma_start(wbuf[:, :], T["w_cross"]).then_inc(st("weights"), 16)

                def load(g, first=False):
                    at = g
                    if not first:
                        at, keys_done = sp.snap(g + 0), sp.snap(g * 8)
                        sp.wait_ge(st("projected"), keys_done)
                    sp.dma_start(ctxT[:, :], T["ctxT"][bass.ds(at, 1)].rearrange("o p c m -> p (o c) m")
                                 ).then_inc(st("ctxT_in"), 16)
                    if not first:
                        mask_done = sp.snap(g + 0)
                        sp.wait_ge(st("mask"), mask_done)
                    sp.dma_start(mask_int[:, :], T["mask"][bass.ds(at, 1)].rearrange("o p m -> p (o m)")
                                 ).then_inc(st("mask_in"), 16)
                load(0, first=True)
                with sp.Fori(1, GROUPS) as g:
                    load(g)

            @block.gpsimd
            def _(pool):
                pool.memset(values[:, :, :, 1:3, HEAD16:HEAD16 + 1].rearrange("p t h s d -> p (t h) s d"), 0.0).then_inc(st("ones"), 1)
                pool.memset(values[:, :, :, 0, HEAD16:HEAD16 + 1], 1.0).then_inc(st("ones"), 1)

                def thirds_of_values(g, par):
                    v = values[:, bass.ds(par * TILE, TILE)].rearrange("p t h s d -> p (t h) s d")
                    pool.wait_ge(st("values_rest"), g + 1)
                    pool.tensor_tensor(v[:, :, 2, 0:HEAD16], v[:, :, 1, 0:HEAD16], top_half(v[:, :, 1, 0:HEAD16]),
                                       ALU.subtract).then_inc(st("values_third"), 1)

                def group(g, par, first, last):
                    for j in range(PAIRS16):
                        for a in range(2):
                            m = g * HEADS16 + 2 * j + a
                            src = rest[:, j % 2, a]
                            pool.wait_ge(st("rest"), m + 1)
                            pool.tensor_tensor(third[:, j % 2, a], src, top_half(src), ALU.subtract).then_inc(st("third"), 1)
                    if not last:
                        thirds_of_values(g + 1, other(par))
                thirds_of_values(0, 0)
                all_groups(pool, group)

            @block.tensor
            def _(pe):
                pe.wait_ge(st("ln_done"), 1)
                transposes(pe, mmT, h, K.ident, DC).then_inc(st("hT_mm"), 1)
                pe.wait_ge(st("weights"), 16)
                pe.wait_ge(st("hT"), 1)
                qT_mm = mm[:, D:2 * D].rearrange("p (c k) -> p c k", k=P)
                for c in range(DC):
                    last = product(pe, qT_mm[:, c], [(wq[:, k, c * P:(c + 1) * P], hT[:, k]) for k in range(DC)])
                last.then_inc(st("qT_mm"), 1)
                pe.wait_ge(st("qblk"), 1)
                pe.wait_ge(st("ones"), 2)

                def project_keys(g):
                    pe.wait_ge(st("ctxT_in"), g * 16 + 16)
                    await_count(pe, st("masked0"), g * PAIRS16)
                    await_count(pe, st("masked1"), g * PAIRS16)
                    for p in range(4):
                        out = sc[:, p * 512:p * 512 + HALF_KEYS]
                        c, half = p // 2, (p % 2) * HALF_KEYS
                        product(pe, out, [(wk[:, k, c * P:(c + 1) * P], ctxT[:, k, half:half + HALF_KEYS]) for k in range(DC)]
                                ).then_inc(st("projected"), 1)

                def project_values(g):
                    for p in range(4):
                        pe.wait_ge(st("stored_s" if p % 2 else "stored_v"), g * STORES[p % 2] + p // 2 + 1)
                        for t in range(2 * p, min(2 * p + 2, TILE)):
                            last = product(pe, sc[:, t * D:(t + 1) * D], [(ctxT[:, k, t * P:(t + 1) * P], wv[:, k]) for k in range(DC)])
                        last.then_inc(st("projected"), 1)

                def turn(g, j, a):
                    pe.wait_ge(st(f"exp{a}"), g * PAIRS16 + j + 1)
                    await_count(pe, st("copied"), g * HEADS16 + 2 * j + a)
                    for t in range(TILE):
                        last = pe.transpose(turned[:, t], s[:, j % 2, a, t * P:(t + 1) * P], K.ident)
                    last.then_inc(st("turned_mm"), 1)

                def attend(g, par, j, a):
                    m = g * HEADS16 + 2 * j + a
                    hd, out = 2 * j + a, attended[j % 2][:, a]
                    parts = ((top_half(eT[:, j % 2, a]), ("copied",)), (top_half(rest[:, j % 2, a]), ("rest",)),
                             (third[:, j % 2, a], ("third",)))
                    await_count(pe, st("added"), g * PAIRS16 + j - 1)
                    if j == 0 and a == 0:
                        pe.wait_ge(st("values_third"), g + 1)
                    for n, (part, signals) in enumerate(parts):
                        for signal in signals:
                            pe.wait_ge(st(signal), m + 1)
                        for t in range(TILE):
                            v = values[:, bass.ds(par * TILE + t, 1), hd, 0:3 - n, :].rearrange("p o s d -> p (o s) d")
                            last = pe.matmul(out[:, 0:3 - n], part[:, t], top_half(v),
                                             start=n == 0 and t == 0, stop=n == 2 and t == TILE - 1, skip_group_check=True)
                    last.then_inc(st("attended"), 1)

                def group(g, par, first, last):
                    def score(j, a):
                        await_count(pe, st(f"masked{a}"), g * PAIRS16 + j)
                        hd = 2 * j + a
                        for lo, hi in ((0, KEYS_A), (KEYS_A, GROUP)):
                            last = pe.matmul(scores(a)[:, lo:hi].unsqueeze(1), qblk[:, hd // 8, hd % 8],
                                             keysT[:, bass.ds(par * DC + hd // 8, 1), lo:hi], start=True, stop=True)
                        last.then_inc(st(f"scored{a}"), 1)

                    pe.wait_ge(st("stored_v"), g * STORES[0] + STORES[0])
                    pe.wait_ge(st("stored_s"), g * STORES[1] + STORES[1] - 2)
                    score(0, 0)
                    pe.wait_ge(st("stored_s"), g * STORES[1] + STORES[1])
                    score(0, 1)
                    for a in range(2):
                        score(1, a)
                    if not first:
                        for a in range(2):
                            attend(g - 1, other(par), PAIRS16 - 1, a)
                    for j in range(1, PAIRS16):
                        for a in range(2):
                            turn(g, j - 1, a)
                            if j + 1 < PAIRS16:
                                score(j + 1, a)
                        if j >= 2:
                            for a in range(2):
                                attend(g, par, j - 2, a)
                    if not last:
                        project_keys(g + 1)
                    for a in range(2):
                        turn(g, PAIRS16 - 1, a)
                        attend(g, par, PAIRS16 - 2, a)
                    if not last:
                        project_values(g + 1)
                project_keys(0)
                project_values(0)
                all_groups(pe, group)
                for a in range(2):
                    attend(GROUPS - 1, (GROUPS - 1) % 2, PAIRS16 - 1, a)
                pe.wait_ge(st("o"), 1)
                transposes(pe, mmT, o, K.ident, DC).then_inc(st("oT_mm"), 1)
                pe.wait_ge(st("oT"), 1)
                product(pe, mm[:, D:2 * D], [(oT[:, c], wo[:, c]) for c in range(DC)]).then_inc(st("y_mm"), 1)

            @block.scalar
            def _(act):
                norm_scalar(act, st, "ln", lnb)

                def store_keys(g, par):
                    await_count(act, st("attended"), g * HEADS16 - HEADS16)
                    for p in (1, 3):
                        src, dst = key_piece(p, par)
                        act.wait_ge(st("projected"), g * 8 + p + 1)
                        act.copy(dst, src).then_inc(st("stored_s"), 1)

                def store_values(g, par):
                    for p in range(4):
                        src, dst = value_piece(p, par)
                        act.wait_ge(st("projected"), g * 8 + p + 5)
                        act.copy(dst, src).then_inc(st("stored_s"), 1)

                def group(g, par, first, last):
                    def exponentials(j, a):
                        act.wait_ge(st("shift"), g * PAIRS16 + j + 1)
                        rows = s[:, j % 2, a]
                        act.activation(rows, rows, ACT.Exp, bias=run[:, j, 3, a:a + 1], scale=SCALE).then_inc(st(f"exp{a}"), 1)

                    def copy(j, a):
                        act.wait_ge(st("turned_mm"), g * HEADS16 + 2 * j + a + 1)
                        await_count(act, st("attended"), g * HEADS16 + 2 * (j - 2) + a + 1)
                        act.copy(eT[:, j % 2, a], turned).then_inc(st("copied"), 1)

                    for j in range(PAIRS16):
                        for a in range(2):
                            if j:
                                copy(j - 1, a)
                            exponentials(j, a)
                        act.activation(run[:, j, 4], run[:, j, 2], ACT.Exp, scale=SCALE).then_inc(st("decay"), 1)
                    if not last:
                        store_keys(g + 1, other(par))
                    for a in range(2):
                        copy(PAIRS16 - 1, a)
                    if not last:
                        store_values(g + 1, other(par))
                store_keys(0, 0)
                store_values(0, 0)
                all_groups(act, group)

            @block.vector
            def _(dve):
                link = linked(dve, st("vector_step"))
                norm_vector(dve, link, st, "ln", K.x, h[:, :], lnb)
                dve.wait_ge(st("hT_mm"), 1)
                dve.tensor_copy(hT[:, :], mmT).then_inc(st("hT"), 1)
                dve.wait_ge(st("weights"), 16)
                dve.wait_ge(st("qT_mm"), 1)
                for c in range(DC):
                    last = dve.tensor_tensor(qblk[:, c], repeat(mm[:, D + c * P:D + (c + 1) * P], 8), spread(W["head_mask"], P), ALU.mult)
                last.then_inc(st("qblk"), 1)
                link(dve.memset(acc[:, :], 0.0))
                link(dve.memset(top[:, :], -3e38))

                def store(g, par):
                    await_count(dve, st("masked1"), g * PAIRS16)
                    dve.wait_ge(st("mask_in"), g * 16 + 16)
                    dve.tensor_scalar(mask[:, :], mask_int[:, :], 0.0, MASKED, ALU.is_equal, ALU.mult).then_inc(st("mask"), 1)
                    for p in (0, 2):
                        src, dst = key_piece(p, par)
                        dve.wait_ge(st("projected"), g * 8 + p + 1)
                        dve.tensor_copy(dst, src).then_inc(st("stored_v"), 1)

                def rests_of_values(g, par):
                    v = values[:, bass.ds(par * TILE, TILE)].rearrange("p t h s d -> p (t h) s d")
                    dve.wait_ge(st("stored_s"), g * STORES[1] + STORES[1])
                    dve.tensor_tensor(v[:, :, 1, 0:HEAD16], v[:, :, 0, 0:HEAD16], top_half(v[:, :, 0, 0:HEAD16]),
                                      ALU.subtract).then_inc(st("values_rest"), 1)

                def add(g, j):
                    n = g * PAIRS16 + j
                    mine = acc[:, 2 * j:2 * j + 2]
                    dve.wait_ge(st("decay"), n + 1)
                    dve.tensor_tensor(mine, mine, spread(run[:, j, 4], HEAD16 + 1), ALU.mult).then_inc(st("add_step"), 1)
                    dve.wait_ge(st("attended"), g * HEADS16 + 2 * j + 2)
                    dve.tensor_reduce(new[:, :], attended[j % 2].rearrange("p a s d -> p a d s"), X_AXIS, ALU.add).then_inc(st("add_step"), 1)
                    dve.wait_ge(st("add_step"), n * 2 + 2)
                    dve.tensor_tensor(mine, mine, new[:, :], ALU.add).then_inc(st("added"), 1)
                    dve.wait_ge(st("added"), n + 1)

                def group(g, par, first, last):
                    def maximum(j, a):
                        dve.wait_ge(st(f"scored{a}"), g * PAIRS16 + j + 1)
                        dve.memset(marks[:, 2 * j + a:2 * j + a + 1], 0.0)
                        dve.tensor_tensor_reduce(s[:, j % 2, a], scores(a), mask[:, :], 1.0, MASKED * 2, ALU.add, ALU.max,
                                                 run[:, j, 0, a:a + 1]).then_inc(st(f"masked{a}"), 1)

                    def shift(j):
                        r, n = run[:, j], g * PAIRS16 + j
                        heads = top[:, 2 * j:2 * j + 2]
                        dve.wait_ge(st("masked0"), n + 1)
                        dve.wait_ge(st("masked1"), n + 1)
                        dve.tensor_tensor(r[:, 1], r[:, 0], heads, ALU.max).then_inc(st("small_step"), 1)
                        dve.wait_ge(st("small_step"), n * 3 + 1)
                        dve.tensor_scalar(r[:, 3], r[:, 1], -SCALE, None, ALU.mult).then_inc(st("small_step"), 1)
                        dve.tensor_tensor(r[:, 2], heads, r[:, 1], ALU.subtract).then_inc(st("shift"), 1)
                        dve.wait_ge(st("shift"), n + 1)
                        dve.tensor_copy(heads, r[:, 1]).then_inc(st("small_step"), 1)

                    def parts(j, a):
                        m = g * HEADS16 + 2 * j + a
                        dve.wait_ge(st("copied"), m + 1)
                        await_count(dve, st("attended"), m - 3)
                        src, out = eT[:, j % 2, a], rest[:, j % 2, a]
                        dve.tensor_tensor(out, src, top_half(src), ALU.subtract).then_inc(st("rest"), 1)

                    dve.wait_ge(st("mask"), g + 1)
                    for j in range(2):
                        for a in range(2):
                            maximum(j, a)
                        shift(j)
                        if j == 0:
                            rests_of_values(g, par)
                    for j in range(1, PAIRS16):
                        if j >= 3:
                            add(g, j - 3)
                        elif not first:
                            add(g - 1, PAIRS16 + j - 3)
                        for a in range(2):
                            parts(j - 1, a)
                            if j + 1 < PAIRS16:
                                maximum(j + 1, a)
                        if j + 1 < PAIRS16:
                            shift(j + 1)
                    if not last:
                        store(g + 1, other(par))
                    for a in range(2):
                        parts(PAIRS16 - 1, a)
                    add(g, PAIRS16 - 3)
                store(0, 0)
                all_groups(dve, group)
                for j in (PAIRS16 - 2, PAIRS16 - 1):
                    add(GROUPS - 1, j)
                dve.wait_ge(st("added"), GROUPS * PAIRS16)
                link(dve.reciprocal(rsum[:, :], acc[:, :, HEAD16]))
                dve.tensor_tensor(o[:, :].rearrange("p (h d) -> p h d", d=HEAD16), acc[:, :, 0:HEAD16], spread(rsum[:, :], HEAD16),
                                  ALU.mult).then_inc(st("o"), 1)
                dve.wait_ge(st("oT_mm"), 1)
                dve.tensor_copy(oT[:, :], mmT).then_inc(st("oT"), 1)
                residual_vector(dve, st, K.x, mm[:, D:2 * D], "y_mm")



HEADS4, HEAD64 = 4, 64
CONV, SHORT, LONG = 4, 5, 64
LEVELS = 7
FLOOR = 0.08
GATE_IN = 16
DELTA_SPEC = [("wq", DC * D), ("wk", DC * D), ("wv", DC * D), ("wb", DC * HEADS4), ("conv", 3 * DC * CONV),
              ("short", DC * SHORT), ("long", DC * LONG), ("w1", DC * D), ("w1s", D), ("b1", DC), ("w2", DC * 4), ("b2", 16),
              ("temp", 1), ("res", HEADS4), ("rms_w", D), ("wo", DC * D), ("upper", P), ("join", LEVELS * P),
              ("joinT", LEVELS * P)]


def stage_delta(nc, K, T):
    with Stage(nc, "delta") as st:
        wbuf, W = st.pack(nc, DELTA_SPEC)
        wqkv = [chunks(W[n], D) for n in ("wq", "wk", "wv")]
        wb, w1, w2, wo = chunks(W["wb"], HEADS4), chunks(W["w1"], D), chunks(W["w2"], 4), chunks(W["wo"], D)
        conv = W["conv"].rearrange("p (a c k) -> p a c k", a=3, c=DC)
        taps_short, taps_long = chunks(W["short"], SHORT), chunks(W["long"], LONG)
        join, joinT = chunks(W["join"], P), chunks(W["joinT"], P)
        PAD = LONG - 1
        h = st.sb("h", [P, D])
        hT = st.sb("hT", [P, DC, P])
        raw = st.sb("raw", [P, 3, DC, CONV - 1 + P])
        act_in = st.sb("act_in", [P, 3, DC, P])
        act_sig = st.sb("act_sig", [P, 3, DC, P])
        vT = st.sb("vT", [P, DC, PAD + P])
        firs = st.sb("firs", [P, 2, DC, P])
        qkvT = st.sb("qkvT", [P, 2, DC, P])
        qk = st.sb("qk", [P, 2, D])
        z = st.sb("z", [P, 4, HEADS4, HEAD64])
        zz = st.sb("zz", [P, 4, HEADS4, HEAD64])
        kb = st.sb("kb", [P, D])
        vb = st.sb("vb", [P, D])
        T3 = st.sb("T3", [P, 3, DC, P])
        beta = st.sb("beta", [P, HEADS4])
        norms = st.sb("norms", [P, 3, 8])
        A = st.sb("A", [P, 2, HEADS4, P])
        E = st.sb("E", [P, HEADS4, P])
        inv = st.sb("inv", [P, 2, HEADS4, P])
        EI = st.sb("EI", [P, HEADS4, P])
        attnT = st.sb("attnT", [P, HEADS4, P])
        u = st.sb("u", [P, D])
        stats = st.sb("stats", [P, HEADS4, 4, 4])
        mean = st.sb("mean", [P, 4, HEADS4])
        var = st.sb("var", [P, 4, HEADS4])
        msq = st.sb("msq", [P, 4, HEADS4])
        statsT = st.sb("statsT", [GATE_IN, HEADS4, P])
        gateT = st.sb("gateT", [P, DC, HEADS4 * P])
        probs = st.sb("probs", [P, HEADS4, 4])
        small = st.sb("small", [P, 2, HEADS4])
        temp = st.sb("temp", [P, 8])
        res = st.sb("res", [P, HEADS4])
        marks = st.sb("marks", [P, 4])
        o = st.sb("o", [P, D])
        oo = st.sb("oo", [P, D])
        oT = st.sb("oT", [P, DC, P])
        lnb = norm_buffers(st, "ln")
        b = [st.psum(f"bank{i}", 1) for i in range(8)]

        def two(ap):
            return ap.rearrange("p (c k) -> p c k", k=P)
        heads_of = lambda ap: ap.rearrange("p (h d) -> p h d", d=HEAD64)

        with nc.Block() as block:
            @block.sync
            def _(sp):
                sp.dma_start(wbuf[:, :], T["w_delta"]).then_inc(st("weights"), 16)

            @block.tensor
            def _(pe):
                pe.wait_ge(st("ln_done"), 1)
                transposes(pe, two(b[0][:, 0:D]), h, K.ident, DC).then_inc(st("hT_mm"), 1)
                pe.wait_ge(st("weights"), 16)
                pe.wait_ge(st("hT"), 1)
                for a in range(3):
                    for c in range(DC):
                        last = product(pe, b[1 + a][:, c * P:(c + 1) * P], [(wqkv[a][:, k, c * P:(c + 1) * P], hT[:, k]) for k in range(DC)])
                last.then_inc(st("qkv_mm"), 1)
                product(pe, b[0][:, D:D + HEADS4], [(hT[:, k], wb[:, k]) for k in range(DC)]).then_inc(st("beta_mm"), 1)
                pe.wait_ge(st("silu"), 1)
                for a in range(2):
                    for c in range(DC):
                        last = pe.transpose(b[4][:, (a * DC + c) * P:(a * DC + c + 1) * P], qkvT[:, a, c], K.ident)
                for c in range(DC):
                    last = pe.transpose(b[5][:, c * P:(c + 1) * P], vT[:, c, PAD:], K.ident)
                last.then_inc(st("rows_mm"), 1)
                pe.wait_ge(st("unit"), 1)
                for c in range(DC):
                    for a, src in ((0, qk[:, 0]), (1, qk[:, 1])):
                        pe.transpose(b[6][:, (a * DC + c) * P:(a * DC + c + 1) * P], src[:, c * P:(c + 1) * P], K.ident)
                    last = pe.transpose(b[7][:, c * P:(c + 1) * P], kb[:, c * P:(c + 1) * P], K.ident)
                last.then_inc(st("T3_mm"), 1)
                pe.wait_ge(st("T3"), 1)
                qT, kT, kbT = T3[:, 0], T3[:, 1], T3[:, 2]
                for hd in range(HEADS4):
                    rows = slice(HEAD64 * (hd % 2), HEAD64 * (hd % 2) + HEAD64)
                    at, c = slice(hd * P, (hd + 1) * P), hd // 2
                    out = (b[1], b[2], b[3]) if hd % 2 == 0 else (b[0], b[4], b[5])
                    pe.matmul(out[0][:, at], kbT[rows, c], kT[rows, c], start=True, stop=True)
                    pe.matmul(out[1][:, at], kT[rows, c], kbT[rows, c], start=True, stop=True)
                    last = pe.matmul(out[2][:, at], kT[rows, c], qT[rows, c], start=True, stop=True)
                last.then_inc(st("A_mm"), 1)
                for n in range(1, LEVELS):
                    pe.wait_ge(st("E"), n)
                    for hd in range(HEADS4):
                        last = pe.matmul(b[4][:, hd * P:(hd + 1) * P], E[:, hd], inv[:, 0, hd], start=True, stop=True)
                    last.then_inc(st("EI_mm"), 1)
                    pe.wait_ge(st("EI"), n)
                    for hd in range(HEADS4):
                        pe.matmul(b[5][:, hd * P:(hd + 1) * P], inv[:, 1, hd], EI[:, hd], start=True, stop=True)
                        last = pe.matmul(b[6][:, hd * P:(hd + 1) * P], EI[:, hd], inv[:, 1, hd], start=True, stop=True)
                    last.then_inc(st("IEI_mm"), 1)
                pe.wait_ge(st("inv"), LEVELS)
                for hd in range(HEADS4):
                    last = pe.matmul(b[7][:, hd * HEAD64:(hd + 1) * HEAD64], inv[:, 1, hd], vb[:, hd * HEAD64:(hd + 1) * HEAD64], start=True, stop=True)
                last.then_inc(st("u_mm"), 1)
                pe.wait_ge(st("u"), 1)
                for hd in range(HEADS4):
                    last = pe.matmul(b[7][:, D + hd * HEAD64:D + (hd + 1) * HEAD64], attnT[:, hd], u[:, hd * HEAD64:(hd + 1) * HEAD64], start=True, stop=True)
                last.then_inc(st("delta_mm"), 1)
                pe.wait_ge(st("firs"), 1)
                for a in range(2):
                    for c in range(DC):
                        last = pe.transpose(b[4][:, (a * DC + c) * P:(a * DC + c + 1) * P], firs[:, a, c], K.ident)
                last.then_inc(st("firs_mm"), 1)
                pe.wait_ge(st("stats"), 1)
                for hd in range(HEADS4):
                    last = pe.transpose(b[5][0:GATE_IN, hd * P:(hd + 1) * P], stats[:, hd].rearrange("p a s -> p (a s)"), K.ident)
                last.then_inc(st("statsT_mm"), 1)
                pe.wait_ge(st("statsT"), 1)
                for c in range(DC):
                    cols = slice(c * P, (c + 1) * P)
                    last = product(pe, b[c][:, :].rearrange("p (h k) -> p h k", k=P),
                                   [(w1[:, k, cols], hT[:, k].unsqueeze(1).to_broadcast([P, HEADS4, P])) for k in range(DC)]
                                   + [(W["w1s"][0:GATE_IN, cols], statsT[:, :])])
                last.then_inc(st("gate_mm"), 1)
                pe.wait_ge(st("gateT"), 1)
                for hd in range(HEADS4):
                    last = product(pe, b[2][:, hd * 4:hd * 4 + 4], [(gateT[:, c, hd * P:(hd + 1) * P], w2[:, c]) for c in range(DC)])
                last.then_inc(st("logits_mm"), 1)
                pe.wait_ge(st("o"), 1)
                transposes(pe, two(b[3][:, 0:D]), o, K.ident, DC).then_inc(st("oT_mm"), 1)
                pe.wait_ge(st("oT"), 1)
                product(pe, b[3][:, D:2 * D], [(oT[:, c], wo[:, c]) for c in range(DC)]).then_inc(st("y_mm"), 1)

            @block.scalar
            def _(act):
                link = linked(act, st("scalar_step"))
                norm_scalar(act, st, "ln", lnb)
                act.wait_ge(st("weights"), 16)
                act.wait_ge(st("conved"), 1)
                act.activation(act_sig[:, :], act_in[:, :], ACT.Sigmoid).then_inc(st("sigmoid"), 1)
                act.wait_ge(st("beta_mm"), 1)
                act.activation(beta[:, :], b[0][:, D:D + HEADS4], ACT.Sigmoid).then_inc(st("beta"), 1)
                act.activation(res[:, :], W["res"], ACT.Sigmoid).then_inc(st("res"), 1)
                link(act.activation(temp[:, 0:1], W["temp"], ACT.Abs))
                link(act.activation(temp[:, 1:2], temp[:, 0:1], ACT.Exp, scale=-1.0))
                act.activation(temp[:, 2:3], temp[:, 1:2], ACT.Ln, bias=1.0).then_inc(st("log"), 1)
                act.wait_ge(st("sumsq"), 1)
                act.activation(norms[:, 1, :], norms[:, 0, :], ACT.Sqrt).then_inc(st("lengths"), 1)
                act.wait_ge(st("msq"), 1)
                act.activation(stats[:, :, :, 3].rearrange("p h a -> p a h"), msq[:, :], ACT.Sqrt, scale=float(HEAD64)).then_inc(st("l2"), 1)
                act.wait_ge(st("gate_mm"), 1)
                for c in range(DC):
                    last = act.activation(gateT[:, c], b[c][:, :], ACT.Gelu, bias=W["b1"][:, c:c + 1])
                last.then_inc(st("gateT"), 1)
                softmax_scalar(act, st, "mix", probs[:, :], 1.0)
                act.wait_ge(st("o_msq"), 1)
                act.activation(norms[:, 1, 0:4], norms[:, 0, 0:4], ACT.Sqrt).then_inc(st("o_rms"), 1)

            @block.gpsimd
            def _(pool):
                pool.memset(raw[:, :, :, 0:CONV - 1], 0.0).then_inc(st("raw_zero"), 1)
                pool.memset(vT[:, :, 0:PAD], 0.0).then_inc(st("v_zero"), 1)

            @block.vector
            def _(dve):
                link = linked(dve, st("vector_step"))
                norm_vector(dve, link, st, "ln", K.x, h[:, :], lnb)
                dve.wait_ge(st("hT_mm"), 1)
                dve.tensor_copy(hT[:, :], two(b[0][:, 0:D])).then_inc(st("hT"), 1)
                dve.wait_ge(st("qkv_mm"), 1)
                dve.wait_ge(st("weights"), 16)
                dve.wait_ge(st("raw_zero"), 1)
                dve.wait_ge(st("v_zero"), 1)
                for a in range(3):
                    link(dve.tensor_copy(raw[:, a, :, CONV - 1:], two(b[1 + a][:, 0:D])))

                def fir(out, src, taps, width):
                    link(dve.tensor_scalar(out, src[:, 0:P], taps[:, 0:1], None, ALU.mult))
                    for k in range(1, width):
                        ins = dve.scalar_tensor_tensor(out=out, in0=src[:, k:k + P], scalar=taps[:, k:k + 1], in1=out,
                                                       op0=ALU.mult, op1=ALU.add)
                        link(ins)

                for a in range(3):
                    for c in range(DC):
                        fir(act_in[:, a, c], raw[:, a, c], conv[:, a, c], CONV)
                dve.memset(marks[:, 0:1], 0.0).then_inc(st("conved"), 1)
                dve.wait_ge(st("sigmoid"), 1)
                link(dve.tensor_tensor(vT[:, :, PAD:], act_in[:, 2], act_sig[:, 2], ALU.mult))
                dve.tensor_tensor(qkvT[:, :], act_in[:, 0:2], act_sig[:, 0:2], ALU.mult).then_inc(st("silu"), 1)
                dve.wait_ge(st("rows_mm"), 1)
                link(dve.tensor_copy(qk[:, :].rearrange("p a d -> p (a d)"), b[4][:, :]))
                link(dve.tensor_copy(z[:, 3].rearrange("p h d -> p (h d)"), b[5][:, 0:D]))
                sq = zz[:, 0:2].rearrange("p a h d -> p (a h) d")
                qk_h = qk[:, :].rearrange("p a (h d) -> p (a h) d", d=HEAD64)
                link(dve.tensor_tensor(sq, qk_h, qk_h, ALU.mult))
                link(dve.tensor_reduce(norms[:, 0, :], sq, X_AXIS, ALU.add))
                link(dve.tensor_scalar(norms[:, 0, :], norms[:, 0, :], 1e-12, None, ALU.add))
                dve.memset(marks[:, 1:2], 0.0).then_inc(st("sumsq"), 1)
                dve.wait_ge(st("lengths"), 1)
                link(dve.reciprocal(norms[:, 2, :], norms[:, 1, :]))
                link(dve.tensor_tensor(qk_h, qk_h, spread(norms[:, 2, :], HEAD64), ALU.mult))
                dve.wait_ge(st("beta"), 1)
                link(dve.tensor_tensor(heads_of(vb[:, :]), z[:, 3], spread(beta[:, :], HEAD64), ALU.mult))
                dve.tensor_tensor(heads_of(kb[:, :]), heads_of(qk[:, 1]), spread(beta[:, :], HEAD64), ALU.mult).then_inc(st("unit"), 1)
                dve.wait_ge(st("T3_mm"), 1)
                link(dve.tensor_copy(T3[:, 0:2], b[6][:, :].rearrange("p (a c k) -> p a c k", a=2, k=P)))
                dve.tensor_copy(T3[:, 2], two(b[7][:, 0:D])).then_inc(st("T3"), 1)
                dve.wait_ge(st("A_mm"), 1)
                ident4 = repeat(K.ident, HEADS4)
                for odd, src in ((0, (b[1], b[2], b[3])), (1, (b[0], b[4], b[5]))):
                    link(dve.tensor_copy(A[:, 0, odd::2], two(src[0][:, :])[:, odd::2]))
                    link(dve.tensor_copy(A[:, 1, odd::2], two(src[1][:, :])[:, odd::2]))
                    link(dve.tensor_tensor(attnT[:, odd::2], two(src[2][:, :])[:, odd::2], repeat(W["upper"], 2), ALU.mult))
                link(dve.tensor_tensor(inv[:, 0], A[:, 0], repeat(join[:, 0], HEADS4), ALU.mult))
                link(dve.tensor_tensor(inv[:, 1], A[:, 1], repeat(joinT[:, 0], HEADS4), ALU.mult))
                link(dve.tensor_tensor(inv[:, 0], ident4, inv[:, 0], ALU.subtract))
                dve.tensor_tensor(inv[:, 1], ident4, inv[:, 1], ALU.subtract).then_inc(st("inv"), 1)
                dve.wait_ge(st("inv"), 1)
                for n in range(1, LEVELS):
                    dve.tensor_tensor(E[:, :], A[:, 1], repeat(joinT[:, n], HEADS4), ALU.mult).then_inc(st("E"), 1)
                    dve.wait_ge(st("EI_mm"), n)
                    dve.tensor_copy(EI[:, :], two(b[4][:, :])).then_inc(st("EI"), 1)
                    dve.wait_ge(st("IEI_mm"), n)
                    link(dve.tensor_tensor(inv[:, 0], inv[:, 0], two(b[5][:, :]), ALU.subtract))
                    dve.tensor_tensor(inv[:, 1], inv[:, 1], two(b[6][:, :]), ALU.subtract).then_inc(st("inv"), 1)
                    dve.wait_ge(st("inv"), n + 1)
                dve.wait_ge(st("u_mm"), 1)
                dve.tensor_copy(u[:, :], b[7][:, 0:D]).then_inc(st("u"), 1)
                for c in range(DC):
                    fir(firs[:, 0, c], vT[:, c, PAD - SHORT + 1:], taps_short[:, c], SHORT)
                    fir(firs[:, 1, c], vT[:, c], taps_long[:, c], LONG)
                dve.memset(marks[:, 2:3], 0.0).then_inc(st("firs"), 1)
                dve.wait_ge(st("delta_mm"), 1)
                link(dve.tensor_copy(z[:, 2], heads_of(b[7][:, D:2 * D])))
                dve.wait_ge(st("firs_mm"), 1)
                link(dve.tensor_copy(z[:, 0:2].rearrange("p a h d -> p (a h d)"), b[4][:, :]))
                z16, zz16 = (t[:, :].rearrange("p a h d -> p (a h) d") for t in (z, zz))
                f16 = lambda t: t[:, :].rearrange("p a h -> p (a h)")
                stat = lambda k: stats[:, :, :, k].rearrange("p h a -> p a h")
                link(dve.tensor_reduce(f16(mean), z16, X_AXIS, ALU.add))
                link(dve.tensor_reduce(f16(msq), z16, X_AXIS, ALU.add, apply_absolute_value=True))
                link(dve.tensor_scalar(stat(2), msq[:, :], 1.0 / HEAD64, None, ALU.mult))
                link(dve.tensor_scalar(f16(mean), f16(mean), 1.0 / HEAD64, None, ALU.mult))
                link(dve.tensor_copy(stat(0), mean[:, :]))
                link(dve.tensor_tensor(zz16, z16, spread(f16(mean), HEAD64), ALU.subtract))
                link(dve.tensor_tensor(zz16, zz16, zz16, ALU.mult))
                link(dve.tensor_reduce(f16(var), zz16, X_AXIS, ALU.add))
                link(dve.tensor_scalar(f16(var), f16(var), 1.0 / HEAD64, None, ALU.mult))
                link(dve.tensor_copy(stat(1), var[:, :]))
                link(dve.tensor_tensor(f16(mean), f16(mean), f16(mean), ALU.mult))
                dve.tensor_tensor(f16(msq), f16(mean), f16(var), ALU.add).then_inc(st("msq"), 1)
                dve.wait_ge(st("l2"), 1)
                dve.memset(marks[:, 3:4], 0.0).then_inc(st("stats"), 1)
                dve.wait_ge(st("statsT_mm"), 1)
                dve.tensor_copy(statsT[:, :], b[5][0:GATE_IN, :].rearrange("p (h k) -> p h k", k=P)).then_inc(st("statsT"), 1)
                dve.wait_ge(st("log"), 1)
                link(dve.tensor_scalar(temp[:, 3:4], W["temp"], 0.0, None, ALU.max))
                link(dve.tensor_tensor(temp[:, 4:5], temp[:, 3:4], temp[:, 2:3], ALU.add))
                link(dve.tensor_scalar(temp[:, 4:5], temp[:, 4:5], 1e-6, None, ALU.add))
                link(dve.reciprocal(temp[:, 5:6], temp[:, 4:5]))
                dve.wait_ge(st("logits_mm"), 1)
                flat = probs[:, :].rearrange("p h k -> p (h k)")
                link(dve.tensor_tensor(flat, b[2][:, 0:16], W["b2"], ALU.add))
                link(dve.tensor_scalar(flat, flat, temp[:, 5:6], None, ALU.mult))
                softmax_vector(dve, link, st, "mix", probs[:, :], probs[:, :], small[:, :, :], 1.0)
                link(dve.tensor_scalar(flat, flat, 1.0 - 2 * FLOOR, None, ALU.mult))
                link(dve.tensor_scalar(probs[:, :, 0:2], probs[:, :, 0:2], FLOOR, None, ALU.add))
                dve.wait_ge(st("res"), 1)
                link(dve.tensor_tensor(probs[:, :, 0], probs[:, :, 0], res[:, :], ALU.add))
                for a in range(4):
                    link(dve.tensor_tensor(zz[:, a], z[:, a], spread(probs[:, :, a], HEAD64), ALU.mult))
                link(dve.tensor_tensor(zz[:, 0:2], zz[:, 0:2], zz[:, 2:4], ALU.add))
                link(dve.tensor_tensor(heads_of(o[:, :]), zz[:, 0], zz[:, 1], ALU.add))
                link(dve.tensor_tensor(oo[:, :], o[:, :], o[:, :], ALU.mult))
                link(dve.tensor_reduce(norms[:, 0, 0:4], heads_of(oo[:, :]), X_AXIS, ALU.add))
                dve.tensor_scalar(norms[:, 0, 0:4], norms[:, 0, 0:4], 1.0 / HEAD64, 1e-5, ALU.mult, ALU.add).then_inc(st("o_msq"), 1)
                dve.wait_ge(st("o_rms"), 1)
                link(dve.reciprocal(norms[:, 2, 0:4], norms[:, 1, 0:4]))
                link(dve.tensor_tensor(heads_of(o[:, :]), heads_of(o[:, :]), spread(norms[:, 2, 0:4], HEAD64), ALU.mult))
                dve.tensor_tensor(o[:, :], o[:, :], W["rms_w"], ALU.mult).then_inc(st("o"), 1)
                dve.wait_ge(st("oT_mm"), 1)
                dve.tensor_copy(oT[:, :], two(b[3][:, 0:D])).then_inc(st("oT"), 1)
                residual_vector(dve, st, K.x, b[3][:, D:2 * D], "y_mm")



LAYERS, HEADS8 = 2, 8
INNER = HEADS8 * HEAD64
IC = INNER // P
HID = int(D * 4 * 2 / 3)
HC = -(-HID // P)
HPAD = HC * P
LOCAL_SPEC = [("wqkv", DC * 3 * INNER), ("wo", IC * D), ("w1", DC * 2 * HPAD), ("w2", HC * D), ("b1", 2 * HC),
              ("ln_g", D), ("ln_b", D), ("b2", D), ("qs", HEAD64), ("ks", HEAD64)]
ROTARY_SPEC = [("cq", HEAD64), ("sq", HEAD64), ("ck", HEAD64), ("sk", HEAD64), ("shift", P)]
LOCAL_SCALE = 8.0


def stage_local(nc, K, T):
    with Stage(nc, "local") as st:
        wbuf, W = st.pack(nc, LOCAL_SPEC)
        rbuf = st.sb("rotary", [P, sum(n for _, n in ROTARY_SPEC)])
        at, R = 0, {}
        for name, n in ROTARY_SPEC:
            R[name] = rbuf[:, at:at + n]
            at += n
        wqkv, wo, w1, w2 = chunks(W["wqkv"], 3 * INNER), chunks(W["wo"], D), chunks(W["w1"], 2 * HPAD), chunks(W["w2"], D)
        x = st.sb("x", [P, D])
        hT = st.sb("hT", [P, DC, P])
        v = st.sb("v", [P, INNER])
        qk = st.sb("qk", [P, 2, HEADS8, HEAD64])
        turned = st.sb("turned", [P, 2, HEADS8, HEAD64])
        norms = st.sb("norms", [P, 3, 16])
        table = st.sb("table", [P, 4, HEAD64])
        qkT = st.sb("qkT", [P, 2, IC, P])
        pr = st.sb("pr", [P, HEADS8, P])
        prT = st.sb("prT", [P, HEADS8, P])
        small = st.sb("small", [P, 2, HEADS8])
        o = st.sb("o", [P, INNER])
        oT = st.sb("oT", [P, IC, P])
        n2 = st.sb("n2", [P, D])
        n2T = st.sb("n2T", [P, DC, P])
        gel = st.sb("gel", [P, HC, P])
        hidT = st.sb("hidT", [P, HC, P])
        lnb = norm_buffers(st, "ln")
        ln2b = norm_buffers(st, "ln2")
        big = [st.psum(f"big{i}", 2) for i in range(3)]
        mm = [st.psum(f"mm{i}", 1) for i in range(2)]
        three = lambda ap: ap.rearrange("p (c k) -> p c k", k=P)

        with nc.Block() as block:
            @block.sync
            def _(sp):
                sp.dma_start(rbuf[:, :], T["w_rotary"]).then_inc(st("rotary_in"), 16)
                for n in range(LAYERS):
                    if n:
                        sp.wait_ge(st("layer"), n)
                    sp.dma_start(wbuf[:, :], T["w_local"][n]).then_inc(st(f"weights{n}"), 16)

            @block.tensor
            def _(pe):
                pe.wait_ge(st("rotary_in"), 16)
                for n in range(LAYERS):
                    if n == 0:
                        pe.wait_ge(st("ln_done"), 1)
                    else:
                        pe.wait_ge(st("layer"), n)
                    pe.wait_ge(st(f"weights{n}"), 16)
                    transposes(pe, three(mm[0][:, 0:D]), x, K.ident, DC).then_inc(st("xT_mm"), 1)
                    pe.wait_ge(st("hT"), n + 1)
                    for a in range(3):
                        product(pe, big[a // 2][:, (a % 2) * 512:(a % 2) * 512 + 512],
                                [(hT[:, c], wqkv[:, c, a * INNER:(a + 1) * INNER]) for c in range(DC)]).then_inc(st("qkv_mm"), 1)
                    pe.wait_ge(st("rotated"), n + 1)
                    for a in range(2):
                        for c in range(IC):
                            last = pe.transpose(big[2][:, (a * IC + c) * P:(a * IC + c + 1) * P],
                                                qk[:, a].rearrange("p h d -> p (h d)")[:, c * P:(c + 1) * P], K.ident)
                    last.then_inc(st("qkT_mm"), 1)
                    pe.wait_ge(st("qkT"), n + 1)
                    for hd in range(HEADS8):
                        rows, c = slice(HEAD64 * (hd % 2), HEAD64 * (hd % 2) + HEAD64), hd // 2
                        last = pe.matmul(big[0][:, (hd % 2) * 512 + c * P:(hd % 2) * 512 + (c + 1) * P], qkT[rows, 0, c], qkT[rows, 1, c],
                                         start=True, stop=True)
                    last.then_inc(st("scores_mm"), 1)
                    pe.wait_ge(st(f"sdpa{n}_probs"), 1)
                    for hd in range(HEADS8):
                        last = pe.transpose(big[1][:, hd * P:(hd + 1) * P], pr[:, hd], K.ident)
                    last.then_inc(st("prT_mm"), 1)
                    pe.wait_ge(st("prT"), n + 1)
                    for hd in range(HEADS8):
                        last = pe.matmul(mm[1][:, hd * HEAD64:(hd + 1) * HEAD64], prT[:, (hd % 2) * IC + hd // 2],
                                         v[:, hd * HEAD64:(hd + 1) * HEAD64], start=True, stop=True)
                    last.then_inc(st("o_mm"), 1)
                    pe.wait_ge(st("o"), n + 1)
                    transposes(pe, three(mm[0][:, :]), o, K.ident, IC).then_inc(st("oT_mm"), 1)
                    pe.wait_ge(st("oT"), n + 1)
                    product(pe, mm[1][:, 0:D], [(oT[:, c], wo[:, c]) for c in range(IC)]).then_inc(st("wo_mm"), 1)
                    pe.wait_ge(st("x_mid"), n + 1)
                    pe.matmul(mm[0][:, 0:P], R["shift"], x[:, P:D], start=True, stop=True).then_inc(st("shift_mm"), 1)
                    pe.wait_ge(st("n2"), n + 1)
                    transposes(pe, three(mm[1][:, 0:D]), n2, K.ident, DC).then_inc(st("n2T_mm"), 1)
                    pe.wait_ge(st("n2T"), n + 1)
                    for half in (1, 0):
                        for j in range(HC):
                            cols = slice(half * HPAD + j * P, half * HPAD + (j + 1) * P)
                            last = product(pe, big[half][:, j * P:(j + 1) * P], [(w1[:, c, cols], n2T[:, c]) for c in range(DC)])
                        last.then_inc(st("w1_mm"), 1)
                    pe.wait_ge(st("hidT"), n + 1)
                    product(pe, mm[0][:, 0:D], [(hidT[:, c], w2[:, c]) for c in range(HC)]).then_inc(st("w2_mm"), 1)

            @block.scalar
            def _(act):
                norm_scalar(act, st, "ln", lnb)
                for n in range(LAYERS):
                    act.wait_ge(st("sumsq"), n + 1)
                    act.activation(norms[:, 1], norms[:, 0], ACT.Sqrt).then_inc(st("lengths"), 1)
                    softmax_scalar(act, st, f"sdpa{n}", pr[:, :], LOCAL_SCALE)
                    act.wait_ge(st("var"), n + 1)
                    act.activation(ln2b[1][:, 3:4], ln2b[1][:, 2:3], ACT.Sqrt).then_inc(st("std"), 1)
                    act.wait_ge(st("w1_mm"), 2 * n + 1)
                    act.wait_ge(st(f"weights{n}"), 16)
                    for j in range(HC):
                        last = act.activation(gel[:, j], big[1][:, j * P:(j + 1) * P], ACT.Gelu, bias=W["b1"][:, HC + j:HC + j + 1])
                    last.then_inc(st("gelu"), 1)

            @block.vector
            def _(dve):
                link = linked(dve, st("vector_step"))
                norm_vector(dve, link, st, "ln", K.x, x[:, :], lnb)
                dve.wait_ge(st("rotary_in"), 16)
                link(dve.memset(hT[:, 1, 0:1], 0.0))
                for n in range(LAYERS):
                    dve.wait_ge(st("xT_mm"), n + 1)
                    link(dve.tensor_copy(hT[:, 0], mm[0][:, 0:P]))
                    dve.tensor_copy(hT[:, 1, 1:P], mm[0][:, P:2 * P - 1]).then_inc(st("hT"), 1)
                    dve.wait_ge(st(f"weights{n}"), 16)
                    HH = HEAD64 // 2
                    for a, (c, s, w) in enumerate((("cq", "sq", "qs"), ("ck", "sk", "ks"))):
                        link(dve.tensor_tensor(table[:, 2 * a], R[c], W[w], ALU.mult))
                        link(dve.tensor_tensor(table[:, 2 * a + 1, 0:HH], R[s][:, 0:HH], W[w][:, HH:], ALU.mult))
                        link(dve.tensor_tensor(table[:, 2 * a + 1, HH:], R[s][:, HH:], W[w][:, 0:HH], ALU.mult))
                    dve.wait_ge(st("qkv_mm"), 3 * n + 3)
                    flat = lambda t: t[:, :].rearrange("p a h d -> p (a h) d")
                    both = big[0][:, :].rearrange("p (h d) -> p h d", d=HEAD64)
                    link(dve.tensor_copy(flat(qk), both))
                    link(dve.tensor_copy(v[:, :], big[1][:, 0:INNER]))
                    link(dve.tensor_tensor(flat(turned), flat(qk), flat(qk), ALU.mult))
                    dve.tensor_reduce(norms[:, 0], flat(turned), X_AXIS, ALU.add).then_inc(st("sumsq"), 1)
                    dve.wait_ge(st("lengths"), n + 1)
                    link(dve.tensor_scalar(norms[:, 1], norms[:, 1], 1e-12, None, ALU.max))
                    link(dve.reciprocal(norms[:, 2], norms[:, 1]))
                    link(dve.tensor_tensor(flat(qk), flat(qk), spread(norms[:, 2], HEAD64), ALU.mult))
                    for a in range(2):
                        link(dve.tensor_tensor(turned[:, a, :, 0:HH], qk[:, a, :, HH:], repeat(table[:, 2 * a + 1, 0:HH], HEADS8), ALU.mult))
                        link(dve.tensor_tensor(turned[:, a, :, HH:], qk[:, a, :, 0:HH], repeat(table[:, 2 * a + 1, HH:], HEADS8), ALU.mult))
                        link(dve.tensor_tensor(qk[:, a], qk[:, a], repeat(table[:, 2 * a], HEADS8), ALU.mult))
                    dve.tensor_tensor(flat(qk), flat(qk), flat(turned), ALU.add).then_inc(st("rotated"), 1)
                    dve.wait_ge(st("qkT_mm"), n + 1)
                    dve.tensor_copy(qkT[:, :].rearrange("p a c k -> p (a c) k"), three(big[2][:, :])).then_inc(st("qkT"), 1)
                    dve.wait_ge(st("scores_mm"), n + 1)
                    softmax_vector(dve, link, st, f"sdpa{n}", three(big[0][:, :]), pr[:, :], small[:, :, :], 1.0, mask=K.causal)
                    dve.wait_ge(st("prT_mm"), n + 1)
                    dve.tensor_copy(prT[:, :], three(big[1][:, :])).then_inc(st("prT"), 1)
                    dve.wait_ge(st("o_mm"), n + 1)
                    dve.tensor_copy(o[:, :], mm[1][:, :]).then_inc(st("o"), 1)
                    dve.wait_ge(st("oT_mm"), n + 1)
                    dve.tensor_copy(oT[:, :], three(mm[0][:, :])).then_inc(st("oT"), 1)
                    dve.wait_ge(st("wo_mm"), n + 1)
                    dve.tensor_tensor(x[:, :], x[:, :], mm[1][:, 0:D], ALU.add).then_inc(st("x_mid"), 1)
                    dve.wait_ge(st("x_mid"), n + 1)
                    link(dve.tensor_copy(n2[:, 0:P], x[:, 0:P]))
                    dve.wait_ge(st("shift_mm"), n + 1)
                    link(dve.tensor_copy(n2[:, P:D], mm[0][:, 0:P]))
                    link(dve.bn_stats(ln2b[0][:, :], n2[:, :]))
                    link(dve.bn_aggr(ln2b[1][:, 0:2], ln2b[0][:, :]))
                    dve.tensor_scalar(ln2b[1][:, 2:3], ln2b[1][:, 1:2], LN_EPS, None, ALU.add).then_inc(st("var"), 1)
                    dve.wait_ge(st("std"), n + 1)
                    link(dve.reciprocal(ln2b[1][:, 2:3], ln2b[1][:, 3:4]))
                    link(dve.tensor_scalar(n2[:, :], n2[:, :], ln2b[1][:, 0:1], ln2b[1][:, 2:3], ALU.subtract, ALU.mult))
                    link(dve.tensor_tensor(n2[:, :], n2[:, :], W["ln_g"], ALU.mult))
                    dve.tensor_tensor(n2[:, :], n2[:, :], W["ln_b"], ALU.add).then_inc(st("n2"), 1)
                    dve.wait_ge(st("n2T_mm"), n + 1)
                    dve.tensor_copy(n2T[:, :], three(mm[1][:, 0:D])).then_inc(st("n2T"), 1)
                    dve.wait_ge(st("w1_mm"), 2 * n + 2)
                    link(dve.tensor_tensor(hidT[:, :], three(big[0][:, 0:HPAD]), spread(W["b1"][:, 0:HC], P), ALU.add))
                    dve.wait_ge(st("gelu"), n + 1)
                    dve.tensor_tensor(hidT[:, :], hidT[:, :], gel[:, :], ALU.mult).then_inc(st("hidT"), 1)
                    dve.wait_ge(st("w2_mm"), n + 1)
                    link(dve.tensor_tensor(x[:, :], x[:, :], mm[0][:, 0:D], ALU.add))
                    dve.tensor_tensor(x[:, :], x[:, :], W["b2"], ALU.add).then_inc(st("layer"), 1)
                    dve.wait_ge(st("layer"), n + 1)
                link(dve.tensor_tensor(K.x, K.x, x[:, :], ALU.add))



MQA_HEADS = 8
MQA_SPEC = [("wq", DC * MQA_HEADS * P), ("wkv", DC * 2 * P), ("bq", MQA_HEADS), ("bk", 1), ("bv", P), ("peT", P),
            ("wo", MQA_HEADS * D)]


def stage_mqa(nc, K, T):
    with Stage(nc, "mqa") as st:
        wbuf, W = st.pack(nc, MQA_SPEC)
        wq, wkv, wo = chunks(W["wq"], MQA_HEADS * P), chunks(W["wkv"], 2 * P), chunks(W["wo"], D)
        h = st.sb("h", [P, D])
        hT = st.sb("hT", [P, DC, P])
        qT = st.sb("qT", [P, MQA_HEADS, P])
        kT = st.sb("kT", [P, P])
        v = st.sb("v", [P, P])
        pr = st.sb("pr", [P, MQA_HEADS, P])
        prT = st.sb("prT", [P, MQA_HEADS, P])
        oT = st.sb("oT", [P, MQA_HEADS, P])
        small = st.sb("small", [P, 2, MQA_HEADS])
        lnb = norm_buffers(st, "ln")
        q_mm, s_mm, t_mm = (st.psum(n, 2)[:, :].rearrange("p (h k) -> p h k", k=P) for n in ("q_mm", "s_mm", "t_mm"))
        mm = st.psum("mm", 1)
        mm2 = st.psum("mm2", 1)
        with nc.Block() as block:
            @block.sync
            def _(sp):
                sp.dma_start(wbuf[:, :], T["w_mqa"]).then_inc(st("weights"), 16)

            @block.tensor
            def _(pe):
                pe.wait_ge(st("ln_done"), 1)
                transposes(pe, mm[:, 0:D].rearrange("p (c k) -> p c k", k=P), h, K.ident, DC).then_inc(st("hT_mm"), 1)
                pe.wait_ge(st("weights"), 16)
                pe.wait_ge(st("hT"), 1)
                product(pe, mm2[:, 0:P], [(wkv[:, c, 0:P], hT[:, c]) for c in range(DC)])
                product(pe, mm2[:, P:2 * P], [(hT[:, c], wkv[:, c, P:2 * P]) for c in range(DC)])
                for hd in range(MQA_HEADS):
                    last = product(pe, q_mm[:, hd], [(wq[:, c, hd * P:(hd + 1) * P], hT[:, c]) for c in range(DC)])
                last.then_inc(st("qkv_mm"), 1)
                pe.wait_ge(st("qkv"), 1)
                for hd in range(MQA_HEADS):
                    last = pe.matmul(s_mm[:, hd], qT[:, hd], kT[:, :], start=True, stop=True)
                last.then_inc(st("scores_mm"), 1)
                probs_transposed(pe, st, "sdpa", t_mm, pr, K.ident)
                pe.wait_ge(st("prT"), 1)
                for j in range(0, MQA_HEADS, 4):
                    last = pe.matmul(q_mm[:, j:j + 4], v[:, :], prT[:, j:j + 4], start=True, stop=True)
                last.then_inc(st("oT_mm"), 1)
                pe.wait_ge(st("oT"), 1)
                product(pe, mm[:, 0:D], [(oT[:, hd], wo[:, hd]) for hd in range(MQA_HEADS)]).then_inc(st("y_mm"), 1)

            @block.scalar
            def _(act):
                norm_scalar(act, st, "ln", lnb)
                softmax_scalar(act, st, "sdpa", pr[:, :], 1.0)

            @block.vector
            def _(dve):
                link = linked(dve, st("vector_step"))
                norm_vector(dve, link, st, "ln", K.x, h[:, :], lnb)
                dve.wait_ge(st("hT_mm"), 1)
                dve.tensor_copy(hT[:, :], mm[:, 0:D].rearrange("p (c k) -> p c k", k=P)).then_inc(st("hT"), 1)
                dve.wait_ge(st("weights"), 16)
                dve.wait_ge(st("qkv_mm"), 1)
                link(dve.scalar_tensor_tensor(out=kT[:, :], in0=mm2[:, 0:P], scalar=W["bk"], in1=W["peT"], op0=ALU.add, op1=ALU.add))
                link(dve.tensor_tensor(v[:, :], mm2[:, P:2 * P], W["bv"], ALU.add))
                link(dve.tensor_tensor(qT[:, :], q_mm, spread(W["bq"], P), ALU.add))
                dve.tensor_tensor(qT[:, :], qT[:, :], repeat(W["peT"], MQA_HEADS), ALU.add).then_inc(st("qkv"), 1)
                dve.wait_ge(st("scores_mm"), 1)
                softmax_vector(dve, link, st, "sdpa", s_mm, pr[:, :], small[:, :, :], P ** -0.5, mask=K.causal)
                dve.wait_ge(st("sdpa_probsT_mm"), 1)
                dve.tensor_copy(prT[:, :], t_mm).then_inc(st("prT"), 1)
                dve.wait_ge(st("oT_mm"), 1)
                dve.tensor_copy(oT[:, :], q_mm).then_inc(st("oT"), 1)
                residual_vector(dve, st, K.x, mm[:, 0:D], "y_mm")



H_EXPERTS, HSHARED, HROUTED = 8, 512, 256
SC, RC = HSHARED // P, HROUTED // P
PER = P // H_EXPERTS
HASH_SPEC = [("sw1", DC * HSHARED), ("sw3", DC * HSHARED), ("sw2", SC * D), ("sb1", SC), ("sb3", SC), ("sb2", D),
             ("w1", H_EXPERTS * DC * HROUTED), ("w2", H_EXPERTS * RC * D), ("b1", H_EXPERTS * RC), ("b2", H_EXPERTS * DC)]


def stage_hashed(nc, K, T):
    with Stage(nc, "hashed") as st:
        wbuf, W = st.pack(nc, HASH_SPEC)
        sw1, sw3, sw2 = chunks(W["sw1"], HSHARED), chunks(W["sw3"], HSHARED), chunks(W["sw2"], D)
        w1 = W["w1"].rearrange("p (e c n) -> p e c n", e=H_EXPERTS, c=DC)
        w2 = W["w2"].rearrange("p (e c n) -> p e c n", e=H_EXPERTS, c=RC)
        b1, b2 = chunks(W["b1"], RC), chunks(W["b2"], DC)
        h = st.sb("h", [P, D])
        hT = st.sb("hT", [P, DC, P])
        ordered = st.sb("ordered", [P, DC, H_EXPERTS + 1, PER])
        s1 = st.sb("s1", [P, SC, P])
        s3 = st.sb("s3", [P, SC, P])
        hid = st.sb("hid", [P, H_EXPERTS, RC, 2 * PER])
        bias2 = st.sb("bias2", [P, H_EXPERTS, DC])
        routedT = st.sb("routedT", [P, DC, P])
        y = st.sb("y", [P, D])
        lnb = norm_buffers(st, "ln")
        mm, mm_s1, mm_s3 = st.psum("mm", 1), st.psum("mm_s1", 1), st.psum("mm_s3", 1)
        mm_hid = st.psum("mm_hid", 1)[:, :].rearrange("p (e c k) -> p e c k", e=H_EXPERTS, c=RC)
        mm_out = st.psum("mm_out", 1)[:, 0:D].rearrange("p (e c k) -> p e c k", e=H_EXPERTS, c=DC)
        mm_y = st.psum("mm_y", 1)
        three = lambda ap: ap.rearrange("p (c k) -> p c k", k=P)

        def place(e):
            return 3 * e % H_EXPERTS

        with nc.Block() as block:
            @block.sync
            def _(sp):
                sp.dma_start(wbuf[:, :], T["w_hashed"]).then_inc(st("weights"), 16)

            @block.tensor
            def _(pe):
                pe.wait_ge(st("ln_done"), 1)
                transposes(pe, three(mm[:, 0:D]), h, K.ident, DC).then_inc(st("hT_mm"), 1)
                pe.wait_ge(st("weights"), 16)
                pe.wait_ge(st("hT"), 1)
                for out, w, done in ((mm_s1, sw1, "s1_mm"), (mm_s3, sw3, "s3_mm")):
                    for j in range(SC):
                        last = product(pe, out[:, j * P:(j + 1) * P], [(w[:, c, j * P:(j + 1) * P], hT[:, c]) for c in range(DC)])
                    last.then_inc(st(done), 1)
                pe.wait_ge(st("ordered"), 1)
                for e in range(H_EXPERTS):
                    for j in range(RC):
                        last = product(pe, mm_hid[:, e, j], [(w1[:, e, c, j * P:(j + 1) * P],
                                                              ordered[:, c, e:e + 2].rearrange("p a k -> p (a k)")) for c in range(DC)])
                last.then_inc(st("hid_mm"), 1)
                pe.wait_ge(st("gated"), 1)
                product(pe, mm_y[:, 0:D], [(s1[:, c], sw2[:, c]) for c in range(SC)]).then_inc(st("shared_mm"), 1)
                pe.wait_ge(st("hid"), H_EXPERTS * RC)
                for e in range(H_EXPERTS):
                    prev = (e - 1) % H_EXPERTS
                    for c in range(DC):
                        cols = slice(c * P, (c + 1) * P)
                        last = product(pe, mm_out[:, e, c], [(w2[:, e, f, cols], hid[:, e, f, 0:PER]) for f in range(RC)]
                                       + [(w2[:, prev, f, cols], hid[:, prev, f, PER:]) for f in range(RC)])
                last.then_inc(st("routed_mm"), 1)
                pe.wait_ge(st("routed"), 1)
                transposes(pe, three(mm[:, 0:D]), routedT[:, :].rearrange("p c k -> p (c k)"), K.ident, DC).then_inc(st("back_mm"), 1)

            @block.scalar
            def _(act):
                norm_scalar(act, st, "ln", lnb)
                act.wait_ge(st("weights"), 16)
                act.wait_ge(st("s1_in"), 1)
                act.activation(s1[:, :], s1[:, :], ACT.Silu).then_inc(st("silu"), 1)
                act.wait_ge(st("hid_mm"), 1)
                for e in range(H_EXPERTS):
                    for j in range(RC):
                        act.activation(hid[:, e, j], mm_hid[:, e, j], ACT.Gelu, bias=b1[:, e, j:j + 1]).then_inc(st("hid"), 1)

            @block.vector
            def _(dve):
                link = linked(dve, st("vector_step"))
                norm_vector(dve, link, st, "ln", K.x, h[:, :], lnb)
                dve.wait_ge(st("hT_mm"), 1)
                dve.tensor_copy(hT[:, :], three(mm[:, 0:D])).then_inc(st("hT"), 1)
                for e in range(H_EXPERTS + 1):
                    r = place(e % H_EXPERTS)
                    link(dve.tensor_copy(ordered[:, :, e], three(mm[:, 0:D])[:, :, r::H_EXPERTS]))
                dve.wait_ge(st("weights"), 16)
                link(dve.tensor_tensor(bias2[:, 1:], b2[:, 1:], b2[:, 0:H_EXPERTS - 1], ALU.add))
                dve.tensor_tensor(bias2[:, 0], b2[:, 0], b2[:, H_EXPERTS - 1], ALU.add).then_inc(st("ordered"), 1)
                dve.wait_ge(st("s1_mm"), 1)
                dve.tensor_tensor(s1[:, :], three(mm_s1[:, :]), spread(W["sb1"], P), ALU.add).then_inc(st("s1_in"), 1)
                dve.wait_ge(st("s3_mm"), 1)
                link(dve.tensor_tensor(s3[:, :], three(mm_s3[:, :]), spread(W["sb3"], P), ALU.add))
                dve.wait_ge(st("silu"), 1)
                dve.tensor_tensor(s1[:, :], s1[:, :], s3[:, :], ALU.mult).then_inc(st("gated"), 1)
                dve.wait_ge(st("shared_mm"), 1)
                link(dve.tensor_tensor(y[:, :], mm_y[:, 0:D], W["sb2"], ALU.add))
                link(dve.scalar_tensor_tensor(out=K.x, in0=y[:, :], scalar=0.5, in1=K.x, op0=ALU.mult, op1=ALU.add))
                dve.wait_ge(st("ordered"), 1)
                dve.wait_ge(st("routed_mm"), 1)
                for e in range(H_EXPERTS):
                    link(dve.tensor_tensor(routedT[:, :, place(e)::H_EXPERTS], mm_out[:, e], spread(bias2[:, e], PER), ALU.add))
                dve.memset(y[:, 0:1], 0.0).then_inc(st("routed"), 1)
                dve.wait_ge(st("back_mm"), 1)
                dve.scalar_tensor_tensor(out=K.x, in0=mm[:, 0:D], scalar=0.25, in1=K.x, op0=ALU.mult, op1=ALU.add).then_inc(st("residual"), 1)
                dve.wait_ge(st("residual"), 1)


STAGE = {0: stage_slots, 1: stage_pattention, 2: stage_quantised, 3: stage_padded_xattn, 4: stage_folded_attention, 5: stage_experts, 6: stage_cross_heads, 7: stage_delta, 8: stage_local, 9: stage_plain_xattn, 10: stage_mqa, 11: stage_hashed}



def in_chunks(w):
    return w.reshape(-1, P, w.shape[-1]).transpose(1, 0, 2).reshape(P, -1)


def on_all(v):
    return np.broadcast_to(v.reshape(1, -1), (P, v.size))


def columns(v):
    return v.reshape(-1, P).T


def packed(spec, parts):
    for name, n in spec:
        assert parts[name].shape == (P, n), (name, parts[name].shape, n)
    return np.ascontiguousarray(np.concatenate([parts[name] for name, _ in spec], axis=1))


def layouts(a):
    out = {}
    f = np.float32
    out["x"] = np.ascontiguousarray(a["x"].reshape(P, D))
    i, j = np.arange(P)[:, None], np.arange(P)[None, :]
    out["consts"] = np.concatenate([(i == j).astype(f), np.where(j <= i, 0, MASKED).astype(f), (i < j).astype(f)], axis=1)
    ctx = a["ctx_1024"].reshape(GROUPS, TILE, P, D)
    out["ctx_rows"] = np.ascontiguousarray(ctx.transpose(0, 2, 1, 3))
    out["ctxT"] = np.ascontiguousarray(ctx.reshape(GROUPS, GROUP, DC, P).transpose(0, 3, 2, 1))
    g = lambda n: a["L0_xattn_" + n]
    out["w_slots"] = packed(SLOT_SPEC, dict(
        wq=in_chunks(g("Wq").T), wk=in_chunks(g("Wk")), wv=in_chunks(g("Wv").T), wi=in_chunks(g("gru_wi").T),
        wh=in_chunks(g("gru_wh").T), bi=on_all(g("gru_bi")), bh=on_all(g("gru_bh")),
        slot_w=on_all(g("slot_norm_w")), in_w=columns(g("input_norm_w"))))
    g = lambda n: a["L0_attn_" + n]
    out["w_patt"] = packed(PATT, dict(
        [(s + "k", in_chunks(g(s + "K").T)) for s in "kqvpf"] + [(s + "v", in_chunks(g(s + "V"))) for s in "kqvpf"],
        head_mask=(i // HEAD16 == np.arange(8)[None, :]).astype(f)))
    g = lambda n: a["L0_ffn_" + n]
    out["w_quant"] = packed(QUANT_SPEC, dict(up=in_chunks(g("w_up")), gate=in_chunks(g("w_gate")), down=in_chunks(g("w_down"))))
    g = lambda n: a["L1_xattn_" + n]
    out["w_padded"] = packed(PADDED_SPEC, dict(w=in_chunks(g("W").T), b=on_all(g("b")), keypos=on_all(np.arange(GROUP, dtype=f)),
                                               qpos=np.arange(P, dtype=f)[:, None]))
    out["lens"] = np.ascontiguousarray(np.broadcast_to(a["_lenS2"].reshape(1, 1), (P, 1)))
    g = lambda n: a["L1_attn_" + n]
    out["w_fold"] = packed(FOLD_SPEC, dict(wqkv=in_chunks(g("Wqkv").T), bqkv=on_all(g("bqkv")), wo=in_chunks(g("Wo").T),
                                           bo=on_all(g("bo")), head_mask=(i // HEAD16 == np.arange(8)[None, :]).astype(f)))
    out["w_moe"] = packed(MOE_SPEC, dict(wg=in_chunks(a["L1_ffn_Wg"]), places=on_all(np.arange(PLACES, dtype=f))))
    out["moe_w1"], out["moe_w2"] = a["L1_ffn_w1"], a["L1_ffn_w2"]
    g = lambda n: a["L2_xattn_" + n]
    out["w_cross"] = packed(CROSS_SPEC, dict(wq=in_chunks(g("w_q").T), wk=in_chunks(g("w_k").T), wv=in_chunks(g("w_v").T),
                                             wo=in_chunks(g("w_o").T), head_mask=(i // HEAD16 == np.arange(8)[None, :]).astype(f)))
    out["mask"] = np.ascontiguousarray(a["mask_1x1xSxS2_if1"].reshape(P, GROUPS, GROUP).transpose(1, 0, 2))
    g = lambda n: a["L2_attn_" + n]
    taps = lambda w: in_chunks(w.reshape(D, -1))
    w1 = g("mlp_w1")
    joins = [((i >> (n + 1)) == (j >> (n + 1))) & ((i >> n) % 2 == 1) & ((j >> n) % 2 == 0) for n in range(LEVELS)]
    out["w_delta"] = packed(DELTA_SPEC, dict(
        wq=in_chunks(g("Wq")), wk=in_chunks(g("Wk")), wv=in_chunks(g("Wv")), wb=in_chunks(g("Wb")),
        conv=np.concatenate([taps(g("conv_w_" + s)) for s in "qkv"], axis=1), short=taps(g("fir_short_w")), long=taps(g("fir_long_w")),
        w1=in_chunks(w1[:D]), w1s=np.concatenate([w1[D:], np.zeros((P - GATE_IN, D), f)]), b1=columns(g("mlp_b1")),
        w2=in_chunks(g("mlp_w2")), b2=np.tile(on_all(g("mlp_b2")), (1, 4)), temp=on_all(g("logit_temp")), res=on_all(g("conv_res_logit")),
        rms_w=np.tile(on_all(g("rms_w")), (1, 4)), wo=in_chunks(g("Wo")), upper=(i <= j).astype(f),
        join=np.concatenate([m.astype(f) for m in joins], axis=1), joinT=np.concatenate([m.T.astype(f) for m in joins], axis=1)))
    g = lambda n: a["L2_ffn_" + n]
    pad_cols = lambda w: np.concatenate([w, np.zeros((w.shape[0], HPAD - HID), f)], axis=1)
    per_layer = []
    for n in range(LAYERS):
        w1, bias1, w2 = g("w1")[n], g("b1")[n], g("w2")[n]
        w1 = np.concatenate([pad_cols(w1[:, :HID]), pad_cols(w1[:, HID:])], axis=1)
        b1 = np.concatenate([pad_cols(bias1[None, :HID]), pad_cols(bias1[None, HID:])], axis=1)[0]
        per_layer.append(packed(LOCAL_SPEC, dict(
            wqkv=in_chunks(g("wqkv")[n]), wo=in_chunks(g("wo")[n]), w1=in_chunks(w1), w2=in_chunks(pad_cols(w2.T).T), b1=columns(b1),
            ln_g=on_all(g("ln_g")[n]), ln_b=on_all(g("ln_b")[n]), b2=on_all(g("b2")[n]), qs=on_all(g("q_scale")[n]), ks=on_all(g("k_scale")[n]))))
    out["w_local"] = np.stack(per_layer)
    half = np.arange(0, HEAD64, 2, dtype=f)
    t = np.arange(P, dtype=f)
    freqs = np.tile(t[:, None] * (f(1.0) / f(10000.0) ** (half / f(HEAD64)))[None, :], (1, 2))
    growth = np.tile(((half + f(0.4 * HEAD64)) / f(1.4 * HEAD64))[None, :] ** ((t - P // 2) / f(P // 2))[:, None], (1, 2))
    sign = np.where(np.arange(HEAD64) < HEAD64 // 2, -1, 1).astype(f)[None, :]
    out["w_rotary"] = packed(ROTARY_SPEC, dict(cq=np.cos(freqs) * growth, sq=np.sin(freqs) * growth * sign,
                                               ck=np.cos(freqs) / growth, sk=np.sin(freqs) / growth * sign, shift=(i + 1 == j).astype(f)))
    g = lambda n: a["L3_attn_" + n]
    angle = np.arange(P, dtype=f)[:, None] * np.exp(f(-np.log(10000.0)) * np.arange(0, P, 2, dtype=f) / f(P))[None, :]
    pe = np.zeros((P, P), f)
    pe[:, 0::2], pe[:, 1::2] = np.sin(angle), np.cos(angle)
    out["w_mqa"] = packed(MQA_SPEC, dict(wq=in_chunks(g("Wq")), wkv=in_chunks(g("Wkv")), bq=columns(g("bq")), bk=columns(g("bkv")[:P]),
                                         bv=on_all(g("bkv")[P:]), peT=pe.T, wo=in_chunks(g("Wo"))))
    g = lambda n: a["L3_ffn_" + n]
    experts = lambda w: np.concatenate([in_chunks(m) for m in w], axis=1)
    out["w_hashed"] = packed(HASH_SPEC, dict(
        sw1=in_chunks(g("sw1")), sw3=in_chunks(g("sw3")), sw2=in_chunks(g("sw2")), sb1=columns(g("sb1")), sb3=columns(g("sb3")),
        sb2=on_all(g("sb2")), w1=experts(g("w1")), w2=experts(g("w2")), b1=columns(g("b1").reshape(-1)), b2=columns(g("b2").reshape(-1))))
    return out



SCRATCH = {"fold_qkv": (P, 3 * D), "fold_o": (P, D)}

class Kept:
    pass


def perceiver(nc, T, out):
    keep = ExitStack()
    with keep:
        def sb(name, shape, dt=F32):
            return keep.enter_context(nc.sbuf_tensor(name, shape, dt))

        K = Kept()
        out_written = nc.alloc_semaphore(name="out_written")
        K.x = sb("x_kept", [P, D])[:, :]
        consts = sb("consts", [P, 3 * P])
        K.ident, K.causal, K.before = (consts[:, i * P:(i + 1) * P] for i in range(3))
        with Stage(nc, "first") as st:
            with nc.Block() as block:
                @block.sync
                def _(sp):
                    sp.dma_start(K.x, T["x"]).then_inc(st("x_in"), 16)
                    sp.dma_start(consts[:, :], T["consts"]).then_inc(st("consts_in"), 16)
                    sp.wait_ge(st("x_in"), 16)
                    sp.wait_ge(st("consts_in"), 16)
        for span in (range(0, 4), range(4, 9), range(9, 10), range(10, 12)):
            todo = [n for n in span if n in STAGES]
            with ExitStack() as rows:
                if {0, 3, 9} & set(todo):
                    K.ctx = rows.enter_context(nc.sbuf_tensor(f"ctx_rows_{span[0]}", [P, GROUPS * TILE, D + 1], F32))
                if {0, 3} & set(todo):
                    K.rinv = rows.enter_context(nc.sbuf_tensor("ctx_rinv", [P, GROUPS * TILE], F32))
                    stage_context(nc, K, T)
                for n in todo:
                    STAGE[n](nc, K, T)
        with Stage(nc, "last") as st:
            with nc.Block() as block:
                @block.sync
                def _(sp):
                    sp.dma_start(out, K.x).then_inc(out_written, 16)
                    sp.wait_ge(out_written, 16)



def kernel(**inputs):
    import concourse.bacc as bacc
    from concourse.bass_utils import run_bass_kernel_spmd

    arrays = layouts({k: np.asarray(v) for k, v in inputs.items()})
    nc = bacc.Bacc("TRN2", target_bir_lowering=False, num_devices=1)
    T = {}
    for name, a in arrays.items():
        T[name] = nc.dram_tensor(f"in_{name}", a.shape, mybir.dt.from_np(a.dtype), kind="ExternalInput").ap()
    out = nc.dram_tensor("out_0", (P, D), F32, kind="ExternalOutput").ap()
    for name, shape in SCRATCH.items():
        T[name] = nc.dram_tensor(name, shape, F32, kind="Internal").ap()
    perceiver(nc, T, out)
    r = run_bass_kernel_spmd(nc, [{f"in_{k}": v for k, v in arrays.items()}], core_ids=[0])
    return r.results[0]["out_0"].reshape(1, P, D)
```
